# Optimizing a Trainium2 kernel written in Bass

```python
import numpy as np
import jax
import jax.numpy as jnp

def _softmax(x, axis=-1):
    return jax.nn.softmax(x, axis=axis)

def _gelu(x):
    return jax.nn.gelu(x, approximate=True)

def _silu(x):
    return jax.nn.silu(x)

def _sigmoid(x):
    return jax.nn.sigmoid(x)

def _layernorm(x, axis=-1, eps=1e-05):
    m = jnp.mean(x, axis=axis, keepdims=True)
    v = jnp.var(x, axis=axis, keepdims=True)
    return (x - m) / jnp.sqrt(v + eps)

def _scatter_add(tgt, idx, src, axis=0):
    return tgt.at[idx].add(src)

def _segment_sum(src, seg, n):
    return jax.ops.segment_sum(src, seg, n)
kernel_name = 'mk_sandwich_d1_jaxref_r4_893377'

def setup_inputs(seed: int=0):
    np.random.seed(seed)
    _w = jnp.asarray

    def _L0_attn_setup():
        import jax, jax.numpy as jnp
        import numpy as np
        D_MODEL = 256
        N_HEADS = 16
        HEAD_DIM = D_MODEL // N_HEADS
        WINDOW = 128
        LOCAL_BLOCK = 64
        LATENT_TOKENS = 64
        LATENT_D = 64
        LATENT_HEADS = 4
        LATENT_HD = LATENT_D // LATENT_HEADS
        NEG = -1000000000.0

        def _local_attention(q, k, v):
            B, H, S, hd = q.shape
            bs = min(S, max(WINDOW, LOCAL_BLOCK))
            nb = S // bs
            w = WINDOW
            L = bs + w - 1
            k_pad = jnp.pad(k, ((0, 0), (0, 0), (w - 1, 0), (0, 0)))
            v_pad = jnp.pad(v, ((0, 0), (0, 0), (w - 1, 0), (0, 0)))
            starts = jnp.arange(nb) * bs
            idx = starts[:, None] + jnp.arange(L)[None, :]
            kb = k_pad[:, :, idx]
            vb = v_pad[:, :, idx]
            qb = q.reshape(B, H, nb, bs, hd)
            q_pos = starts[:, None] + jnp.arange(bs)[None, :]
            k_gpos = starts[:, None] + jnp.arange(L)[None, :] - (w - 1)
            dist = q_pos[:, :, None] - k_gpos[:, None, :]
            allowed = (dist > 0) & (dist <= w) & (k_gpos[:, None, :] >= 0)
            scale = 1.0 / np.sqrt(hd)
            scores = jnp.einsum('bhnqd,bhnkd->bhnqk', qb, kb) * scale
            scores = jnp.where(allowed, scores, NEG)
            attn = jax.nn.softmax(scores, axis=-1)
            attn = jnp.where(allowed.any(-1)[None, None, :, :, None], attn, 0.0)
            out = jnp.einsum('bhnqk,bhnkd->bhnqd', attn, vb)
            return out.reshape(B, H, S, hd)
        key = jax.random.key(seed)
        ks = jax.random.split(key, 14)
        B, S = (2, 1024)
        s = 0.02
        f32 = jnp.float32
        return {'x': jax.random.normal(ks[0], (B, S, D_MODEL), f32), 'qkv_w': jax.random.normal(ks[1], (D_MODEL, 3 * D_MODEL), f32) * s, 'qkv_b': jnp.zeros((3 * D_MODEL,), f32), 'rq_w': jax.random.normal(ks[2], (D_MODEL, LATENT_D), f32) * s, 'rq_b': jnp.zeros((LATENT_D,), f32), 'rkv_w': jax.random.normal(ks[3], (D_MODEL, 2 * LATENT_D), f32) * s, 'rkv_b': jnp.zeros((2 * LATENT_D,), f32), 'rout_w': jax.random.normal(ks[4], (LATENT_D, D_MODEL), f32) * s, 'rout_b': jnp.zeros((D_MODEL,), f32), 'out_w': jax.random.normal(ks[5], (D_MODEL, D_MODEL), f32) * s, 'out_b': jnp.zeros((D_MODEL,), f32), 'gl_w': jax.random.normal(ks[6], (HEAD_DIM, 1), f32) * s, 'gr_w': jax.random.normal(ks[7], (HEAD_DIM, 1), f32) * s}
    _L0_attn_in = _L0_attn_setup()

    def _L0_ffn_setup():
        import jax, jax.numpy as jnp
        import numpy as np
        B, S, D = (1, 512, 256)
        E, K, F = (8, 2, 352)
        NS = 2
        SCALE = 2.5

        def _swiglu_mlp(x, wg, wu, wd):
            return jax.nn.silu(x @ wg) * (x @ wu) @ wd
        key = jax.random.key(seed)
        ks = jax.random.split(key, 8)
        s = 0.02
        return {'hidden_states': jax.random.normal(ks[0], (B, S, D), jnp.float32), 'gate_w': jax.random.normal(ks[1], (E, D), jnp.float32) * s, 'w_gate': jax.random.normal(ks[2], (E, D, F), jnp.float32) * s, 'w_up': jax.random.normal(ks[3], (E, D, F), jnp.float32) * s, 'w_down': jax.random.normal(ks[4], (E, F, D), jnp.float32) * s, 'sw_gate': jax.random.normal(ks[5], (D, F * NS), jnp.float32) * s, 'sw_up': jax.random.normal(ks[6], (D, F * NS), jnp.float32) * s, 'sw_down': jax.random.normal(ks[7], (F * NS, D), jnp.float32) * s}
    _L0_ffn_in = _L0_ffn_setup()
    _d = {'L0_attn_x': _L0_attn_in['x'], 'L0_attn_qkv_w': _L0_attn_in['qkv_w'], 'L0_attn_qkv_b': _L0_attn_in['qkv_b'], 'L0_attn_rq_w': _L0_attn_in['rq_w'], 'L0_attn_rq_b': _L0_attn_in['rq_b'], 'L0_attn_rkv_w': _L0_attn_in['rkv_w'], 'L0_attn_rkv_b': _L0_attn_in['rkv_b'], 'L0_attn_rout_w': _L0_attn_in['rout_w'], 'L0_attn_rout_b': _L0_attn_in['rout_b'], 'L0_attn_out_w': _L0_attn_in['out_w'], 'L0_attn_out_b': _L0_attn_in['out_b'], 'L0_attn_gl_w': _L0_attn_in['gl_w'], 'L0_attn_gr_w': _L0_attn_in['gr_w'], 'L0_ffn_gate_w': _L0_ffn_in['gate_w'], 'L0_ffn_w_gate': _L0_ffn_in['w_gate'], 'L0_ffn_w_up': _L0_ffn_in['w_up'], 'L0_ffn_w_down': _L0_ffn_in['w_down'], 'L0_ffn_sw_gate': _L0_ffn_in['sw_gate'], 'L0_ffn_sw_up': _L0_ffn_in['sw_up'], 'L0_ffn_sw_down': _L0_ffn_in['sw_down']}
    _x0 = _d['L0_attn_x']
    _d['L0_attn_x'] = jax.random.normal(jax.random.fold_in(jax.random.key(seed), 1), (16, 512, 256), dtype=_x0.dtype)
    del _x0
    return _d

def reference(L0_attn_x, L0_attn_qkv_w, L0_attn_qkv_b, L0_attn_rq_w, L0_attn_rq_b, L0_attn_rkv_w, L0_attn_rkv_b, L0_attn_rout_w, L0_attn_rout_b, L0_attn_out_w, L0_attn_out_b, L0_attn_gl_w, L0_attn_gr_w, L0_ffn_gate_w, L0_ffn_w_gate, L0_ffn_w_up, L0_ffn_w_down, L0_ffn_sw_gate, L0_ffn_sw_up, L0_ffn_sw_down):

    def _L0_attn_ref(x, qkv_w, qkv_b, rq_w, rq_b, rkv_w, rkv_b, rout_w, rout_b, out_w, out_b, gl_w, gr_w):
        import jax, jax.numpy as jnp
        import numpy as np
        D_MODEL = 256
        N_HEADS = 16
        HEAD_DIM = D_MODEL // N_HEADS
        WINDOW = 128
        LOCAL_BLOCK = 64
        LATENT_TOKENS = 64
        LATENT_D = 64
        LATENT_HEADS = 4
        LATENT_HD = LATENT_D // LATENT_HEADS
        NEG = -1000000000.0

        def _local_attention(q, k, v):
            B, H, S, hd = q.shape
            bs = min(S, max(WINDOW, LOCAL_BLOCK))
            nb = S // bs
            w = WINDOW
            L = bs + w - 1
            k_pad = jnp.pad(k, ((0, 0), (0, 0), (w - 1, 0), (0, 0)))
            v_pad = jnp.pad(v, ((0, 0), (0, 0), (w - 1, 0), (0, 0)))
            starts = jnp.arange(nb) * bs
            idx = starts[:, None] + jnp.arange(L)[None, :]
            kb = k_pad[:, :, idx]
            vb = v_pad[:, :, idx]
            qb = q.reshape(B, H, nb, bs, hd)
            q_pos = starts[:, None] + jnp.arange(bs)[None, :]
            k_gpos = starts[:, None] + jnp.arange(L)[None, :] - (w - 1)
            dist = q_pos[:, :, None] - k_gpos[:, None, :]
            allowed = (dist > 0) & (dist <= w) & (k_gpos[:, None, :] >= 0)
            scale = 1.0 / np.sqrt(hd)
            scores = jnp.einsum('bhnqd,bhnkd->bhnqk', qb, kb) * scale
            scores = jnp.where(allowed, scores, NEG)
            attn = jax.nn.softmax(scores, axis=-1)
            attn = jnp.where(allowed.any(-1)[None, None, :, :, None], attn, 0.0)
            out = jnp.einsum('bhnqk,bhnkd->bhnqd', attn, vb)
            return out.reshape(B, H, S, hd)
        B, S, D = x.shape
        qkv = x @ qkv_w + qkv_b
        q, k, v = jnp.split(qkv, 3, axis=-1)

        def heads(t):
            return t.reshape(B, S, N_HEADS, HEAD_DIM).transpose(0, 2, 1, 3)
        local = _local_attention(heads(q), heads(k), heads(v))
        chunk = -(-S // min(LATENT_TOKENS, S))
        nlat = S // chunk
        pooled = x.reshape(B, nlat, chunk, D).mean(axis=2)
        chunk_ids = jnp.arange(S) // chunk
        rq = (x @ rq_w + rq_b).reshape(B, S, LATENT_HEADS, LATENT_HD).transpose(0, 2, 1, 3)
        rkv = pooled @ rkv_w + rkv_b
        rk, rv = jnp.split(rkv, 2, axis=-1)
        rk = rk.reshape(B, nlat, LATENT_HEADS, LATENT_HD).transpose(0, 2, 1, 3)
        rv = rv.reshape(B, nlat, LATENT_HEADS, LATENT_HD).transpose(0, 2, 1, 3)
        lscale = 1.0 / np.sqrt(LATENT_HD)
        lscores = jnp.einsum('bhsd,bhld->bhsl', rq, rk) * lscale
        lat_allowed = jnp.arange(nlat)[None, :] < chunk_ids[:, None]
        lscores = jnp.where(lat_allowed[None, None], lscores, NEG)
        lattn = jax.nn.softmax(lscores, axis=-1)
        lattn = jnp.where(lat_allowed.any(-1)[None, None, :, None], lattn, 0.0)
        lat_out = jnp.einsum('bhsl,bhld->bhsd', lattn, rv)
        lat_out = lat_out.transpose(0, 2, 1, 3).reshape(B, S, LATENT_D)
        remote = lat_out @ rout_w + rout_b
        remote_h = remote.reshape(B, S, N_HEADS, HEAD_DIM).transpose(0, 2, 1, 3)
        gate = jax.nn.sigmoid(local @ gl_w + remote_h @ gr_w)
        mixed = gate * local + (1.0 - gate) * remote_h
        mixed = mixed.transpose(0, 2, 1, 3).reshape(B, S, D)
        return mixed @ out_w + out_b

    def _L0_ffn_ref(hidden_states, gate_w, w_gate, w_up, w_down, sw_gate, sw_up, sw_down):
        import jax, jax.numpy as jnp
        import numpy as np
        B, S, D = (1, 512, 256)
        E, K, F = (8, 2, 352)
        NS = 2
        SCALE = 2.5

        def _swiglu_mlp(x, wg, wu, wd):
            return jax.nn.silu(x @ wg) * (x @ wu) @ wd
        identity = hidden_states
        x = hidden_states.reshape(-1, hidden_states.shape[-1])
        T = x.shape[0]
        logits = x.astype(jnp.float32) @ gate_w.astype(jnp.float32).T
        scores = jax.nn.softmax(logits, axis=-1)
        topk_w, topk_i = jax.lax.top_k(scores, K)
        topk_w = topk_w / (topk_w.sum(-1, keepdims=True) + 1e-20) * SCALE
        combine = jnp.zeros((T, E), jnp.float32).at[jnp.arange(T)[:, None], topk_i].set(topk_w)
        g = jax.nn.silu(jnp.einsum('td,edf->etf', x, w_gate)) * jnp.einsum('td,edf->etf', x, w_up)
        expert_out = jnp.einsum('etf,efd->etd', g, w_down)
        y = jnp.einsum('te,etd->td', combine, expert_out).astype(x.dtype)
        y = y.reshape(identity.shape)
        return y + _swiglu_mlp(identity, sw_gate, sw_up, sw_down)
    x = L0_attn_x
    x = x + _layernorm(_L0_attn_ref(_layernorm(x, axis=-1), L0_attn_qkv_w, L0_attn_qkv_b, L0_attn_rq_w, L0_attn_rq_b, L0_attn_rkv_w, L0_attn_rkv_b, L0_attn_rout_w, L0_attn_rout_b, L0_attn_out_w, L0_attn_out_b, L0_attn_gl_w, L0_attn_gr_w), axis=-1)
    x = x + _layernorm(_L0_ffn_ref(_layernorm(x, axis=-1), L0_ffn_gate_w, L0_ffn_w_gate, L0_ffn_w_up, L0_ffn_w_down, L0_ffn_sw_gate, L0_ffn_sw_up, L0_ffn_sw_down), axis=-1)
    return x

_drawn_inputs = setup_inputs


def setup_inputs(seed=0):
    import zlib

    import numpy as np

    out = dict(_drawn_inputs(seed))
    spreads = {'L0_attn_qkv_b': (0.0, 0.1),
     'L0_attn_rq_b': (0.0, 2.0),
     'L0_attn_rkv_b': (0.0, 0.1),
     'L0_attn_rout_b': (0.0, 0.1),
     'L0_attn_out_b': (0.0, 0.1)}
    factors = {'L0_attn_rq_w': 31.725, 'L0_attn_gl_w': 5.174, 'L0_attn_gr_w': 15.945}
    for name, (base, spread) in spreads.items():
        noise = np.random.default_rng([zlib.crc32(name.encode()), seed]).standard_normal(out[name].shape)
        drawn = base * np.exp(spread * noise) if base else spread * noise
        out[name] = jnp.asarray(drawn.astype(out[name].dtype))
    for name, factor in factors.items():
        out[name] = (out[name] * factor).astype(out[name].dtype)
    return out
```

```python
import concourse.bass as bass
from concourse import mybir
from contextlib import ExitStack


class Steps:

    def __init__(self, sem, per, before=0):
        self.sem, self.per, self.before, self.at, self.done = sem, per, before, 0, None

    def begin(self, seq):
        self.seq, self.at = seq, 0

    def next(self):
        self.at += 1
        return self.sem, self.before + self.seq * self.per + self.at

    def end(self):
        assert self.at == self.per, (self.at, self.per)


class Banks:

    def __init__(self, uses, full, free):
        self.where = {name: (b, k) for b, names in enumerate(uses) for k, name in enumerate(names)}
        self.per = [len(names) for names in uses]
        self.fulls, self.frees = full, free

    def bank(self, name):
        return self.where[name][0]

    def full(self, name):
        return self.fulls[self.bank(name)]

    def free(self, name):
        return self.frees[self.bank(name)]

    def drained(self, seq, name):
        b, k = self.where[name]
        return self.frees[b], seq * self.per[b] + k

    def read(self, seq, name):
        b, k = self.where[name]
        return self.frees[b], seq * self.per[b] + k + 1

    def all_filled(self, seq, name):
        b = self.bank(name)
        return self.fulls[b], seq * self.per[b]

    def filled(self, seq, name):
        b, k = self.where[name]
        return self.fulls[b], seq * self.per[b] + k + 1


def sandwich_kernel(nc, x, qkv_w, qkv_b, rq_w, rq_b, rkv_w, rkv_b, rout_w, rout_b, out_w, out_b, gl_w, gr_w,
                    gate_w, w_gate, w_up, w_down, sw_gate, sw_up, sw_down, out):
    f32, f32r, i32 = mybir.dt.float32, mybir.dt.float32r, mybir.dt.int32
    ALU, ACT, AX = mybir.AluOpType, mybir.ActivationFunctionType, mybir.AxisListType

    P = 128
    SEQS, S, D = x.shape
    T = S // P
    C = D // P
    HEADS, HD = 16, D // 16
    G, HG = 4, 4
    PAD = P // HG
    WIN = 2 * P
    LAT, LH = 64, 4
    LC = S // LAT
    DA = D + HEADS
    E, F = w_gate.shape[0], w_gate.shape[2]
    FS = sw_gate.shape[1]
    SCALE = HD ** -0.5
    EPS, NEG, TINY = 1e-5, -1e30, 1e-30
    RSQRT_SEED = 0x5F3759DF
    SETUP_STEPS, NORM_STEPS, LATENT_STEPS, TAIL_STEPS = 12, 14, 5, 57
    ROUTE_STEPS, END_STEPS, WEIGHT_STEPS, LAST_STEPS = 20, 26, 18, 18

    x1_dram = nc.dram_tensor("x1_scratch", (SEQS, S, D), f32, kind="Internal").ap()
    xn2_dram = nc.dram_tensor("xn2_scratch", (SEQS, S, D), f32, kind="Internal").ap()

    with ExitStack() as ctx:
        def sem(name):
            return ctx.enter_context(nc.semaphore(name))

        psum = [ctx.enter_context(nc.psum_tensor(f"bank{b}", [P, 512], f32)) for b in range(8)]
        ident = ctx.enter_context(nc.sbuf_tensor("ident", [P, P], f32))

        attention = ExitStack()
        with attention:
            def sb(name, shape, dt=f32):
                return attention.enter_context(nc.sbuf_tensor(name, shape, dt))

            wqk_h = sb("wqk_h", [P, 2, C, G * P], f32r)
            wqk_l = sb("wqk_l", [P, 2, C, G * P], f32r)
            wv_h = sb("wv_h", [P, C, DA], f32r)
            wv_l = sb("wv_l", [P, C, DA], f32r)
            wrq_h = sb("wrq_h", [P, C, P], f32r)
            wrq_l = sb("wrq_l", [P, C, P], f32r)
            wrk = sb("wrk", [P, C, P])
            wrv = sb("wrv", [P, C, LAT])
            wout_h = sb("wout_h", [P, C, D], f32r)
            wout_l = sb("wout_l", [P, C, D], f32r)
            wrout = sb("wrout", [P, DA])
            bqk = sb("bqk", [P, 2, G])
            bv = sb("bv", [P, DA])
            brq = sb("brq", [P, 1])
            brk = sb("brk", [P, 1])
            brv = sb("brv", [P, LAT])
            bout = sb("bout", [P, D])
            gl = sb("gl", [P, HD])
            gr = sb("gr", [P, HD])
            ones = sb("ones", [1, S])
            mask_window = sb("mask_window", [P, WIN])
            mask_first = sb("mask_first", [P, P])
            lat_add = sb("lat_add", [P, T, LAT])
            lat_keep = sb("lat_keep", [P, T, LAT])
            rk_mask = sb("rk_mask", [P, LH, LAT])
            rv_mask = sb("rv_mask", [P, 2, LAT])

            x_in = sb("x_in", [P, T, D])
            x_res = sb("x_res", [P, T, D])
            xn = sb("xn", [P, T, D])
            xT_h = sb("xT_h", [P, C, S], f32r)
            xT_l = sb("xT_l", [P, C, S], f32r)
            kT_h = sb("kT_h", [P, 2, S], f32r)
            kT_l = sb("kT_l", [P, 2, S], f32r)
            kD_h = sb("kD_h", [P, G, HG, S], f32r)
            kD_l = sb("kD_l", [P, G, HG, S], f32r)
            qT_h = sb("qT_h", [P, G, S], f32r)
            qT_l = sb("qT_l", [P, G, S], f32r)
            v_sb = sb("v_sb", [P, T, HEADS, PAD])
            row_max = sb("row_max", [P, G, T, HG])
            maxT = sb("maxT", [HG, G, S], f32r)
            prob = sb("prob", [P, 4, 2, WIN])
            pvT = sb("pvT", [P, G, S])
            pool = sb("pool", [P, C, LAT])
            pool2 = sb("pool2", [P, C, 2, LAT])
            rqT = sb("rqT", [P, S])
            rk_t = sb("rk_t", [P, LAT])
            rkD = sb("rkD", [P, LH, LAT])
            rv_t = sb("rv_t", [P, LAT])
            rvD = sb("rvD", [P, 2, LAT])
            lat = sb("lat", [P, T, LH, LAT])
            lat_s = sb("lat_s", [P, 3, T, LH])
            latpT = sb("latpT", [P, 2, S])
            latT = sb("latT", [P, S])
            mixed = sb("mixed", [P, 2, D])
            gate_s = sb("gate_s", [P, 2, 6, HEADS])
            mixT_h = sb("mixT_h", [P, 2, C, P], f32r)
            mixT_l = sb("mixT_l", [P, 2, C, P], f32r)
            att = sb("att", [P, T, D])
            stats = sb("stats", [P, 3, T, 6])
            mv = sb("mv", [P, 3, T, 2])
            rstd = sb("rstd", [P, 3, 3, T])
            wqk_f = pvT[:, :, :].rearrange("p g s -> p (g s)").rearrange("p (j c n) -> p j c n", j=2, c=C)
            x_res_flat = x_res[:, :, :].rearrange("p t d -> p (t d)")
            wv_f = x_res_flat[:, 0:C * DA].rearrange("p (c n) -> p c n", c=C)
            wrq_f = x_res_flat[:, C * DA:C * (DA + P)].rearrange("p (c n) -> p c n", c=C)
            wout_f = att[:, 0:C, :]
            wtmp = x_in[:, 0, :]

            zeroed, consts, weights_in, split = sem("zeroed"), sem("consts"), sem("weights_in"), sem("split")
            x_loaded, xres_loaded, xn_ready = sem("x_loaded"), sem("xres_loaded"), sem("xn_ready")
            xTh_ready, kh_ready, qh_ready = sem("xTh_ready"), sem("kh_ready"), sem("qh_ready")
            k_spread = [sem(f"k_spread{g}") for g in range(G)]
            max_placed = [sem(f"max_placed{g}") for g in range(G)]
            prob_ready, prob_used, pv_read = sem("prob_ready"), sem("prob_used"), sem("pv_read")
            pool_ready, rv_ready = sem("pool_ready"), sem("rv_ready")
            lat_max, lat_exp, lat_ready = sem("lat_max"), sem("lat_exp"), sem("lat_ready")
            z_ready, sig_exp, mixTh_ready = sem("z_ready"), sem("sig_exp"), sem("mixTh_ready")
            x1_ready, xn2_ready, stored = sem("x1_ready"), sem("xn2_ready"), sem("stored")
            step_setup, step_front, step_mid, step_tail = (
                sem("step_setup"), sem("step_front"), sem("step_mid"), sem("step_tail"))

            order = (["xT0", "xT1", "k0", "q0", "k1", "q1", "k2", "q2", "k3", "q3", "v0", "v1", "v2", "v3",
                      "rq", "rk", "rv", "ls0", "ls1", "m0", "lT0", "lT1", "lo", "m1", "m2", "m3"])
            front = Banks([order[0::2], order[1::2]], [sem("front_full0"), sem("front_full1")],
                          [sem("front_free0"), sem("front_free1")])
            FB = [psum[6], psum[7]]
            smax = [f"M{g}{b}{h}" for g in range(G) for b in range(T) for h in range(2)]
            tail_s = ["pv0", "pv1", "mix0", "pv2", "mix1", "pv3", "mix2", "mix3"]
            scores = Banks([(smax + tail_s)[0::2], (smax + tail_s)[1::2]], [sem("score_full0"), sem("score_full1")],
                           [sem("score_free0"), sem("score_free1")])
            SB = [psum[0], psum[1]]
            strans = [f"T{g}{b}{h}" for g in range(G) for b in range(T) for h in range(2)]
            tail_t = ["rem0", "rem1", "rem2", "rem3"]
            keyed = Banks([(strans + tail_t)[0::2], (strans + tail_t)[1::2]], [sem("keyed_full0"), sem("keyed_full1")],
                          [sem("keyed_free0"), sem("keyed_free1")])
            KB = [psum[2], psum[3]]
            PV = [psum[4], psum[5]]
            outs = Banks([["out0", "out2"], ["out1", "out3"]], [sem("out_full0"), sem("out_full1")],
                         [sem("out_free0"), sem("out_free1")])

            loads = []
            for j in range(2):
                for c in range(C):
                    loads.append((wqk_f[:, j, c, :].rearrange("p (n w) -> p n w", w=PAD)[:, :, 0:HD],
                                  qkv_w[c * P:(c + 1) * P, j * D:(j + 1) * D].rearrange("p (n d) -> p n d", d=HD)))
                for h in range(HG):
                    loads.append((bqk[h * PAD:h * PAD + HD, j, :],
                                  qkv_b[j * D:(j + 1) * D].rearrange("(g h d) -> h d g", g=G, d=HD)[h, :, :]))
            for c in range(C):
                rows = slice(c * P, (c + 1) * P)
                loads.append((wv_f[:, c, 0:D], qkv_w[rows, 2 * D:3 * D]))
                loads.append((wout_f[:, c, :], out_w[rows, :]))
                loads.append((wrq_f[:, c, 0:LAT], rq_w[rows, :]))
                loads.append((wrk[:, c, 0:LAT], rkv_w[rows, 0:LAT]))
                loads.append((wrv[:, c, :], rkv_w[rows, LAT:2 * LAT]))
            loads.append((wrout[0:LAT, 0:D], rout_w))
            loads.append((wrout[LAT:LAT + 1, 0:D], rout_b.rearrange("(a n) -> a n", a=1)))
            loads.append((bv[:, 0:D], qkv_b[2 * D:3 * D].partition_broadcast(P)))
            loads.append((bout[:, :], out_b.partition_broadcast(P)))
            loads.append((gl[:, :], gl_w.rearrange("d a -> (d a)").partition_broadcast(P)))
            loads.append((gr[:, :], gr_w.rearrange("d a -> (d a)").partition_broadcast(P)))
            loads.append((brv[:, :], rkv_b[LAT:2 * LAT].partition_broadcast(P)))
            loads.append((brq[0:LAT, :], rq_b.rearrange("(n a) -> n a", a=1)))
            loads.append((brk[0:LAT, :], rkv_b[0:LAT].rearrange("(n a) -> n a", a=1)))
            for h in range(HG):
                loads.append((kD_h[h * PAD + HD:h * PAD + HD + 1, :, h, :].bitcast(f32), ones[:, :].unsqueeze(1).to_broadcast([1, G, S])))

            with nc.Block() as block:

                @block.sync
                def _(sp):
                    sp.wait_ge(zeroed, 1)
                    with nc.allow_non_contiguous_dma(reason="128 biases, once"):
                        for dst, src in loads:
                            sp.dma_start(dst, src).then_inc(weights_in, 16)

                    sp.wait_ge(split, 1)

                    def front_loads(i):
                        sp.wait_ge(xn_ready, i)
                        sp.dma_start(x_in[:, :, :], x[i].rearrange("(t p) d -> p t d", p=P)).then_inc(x_loaded, 16)

                    def spread_k(i):
                        sp.wait_ge(prob_used, 2 * T * G * i)
                        for g in range(G):
                            for ready, src, dst in (((kh_ready, G * i + g + 1), kT_h, kD_h),
                                                    (front.read(i, f"k{g}"), kT_l, kD_l)):
                                sp.wait_ge(*ready)
                                for h in range(HG):
                                    r = slice(h * PAD, h * PAD + HD)
                                    sp.dma_start(dst[r, g, h, :].bitcast(f32), src[r, g % 2, :].bitcast(f32)).then_inc(k_spread[g], 16)

                    def place_max(i):
                        for g in range(G):
                            sp.wait_ge(*front.read(i, f"m{g}"))
                            sp.dma_start(qT_h[HD:P:PAD, g, :].bitcast(f32), maxT[:, g, :].bitcast(f32)).then_inc(max_placed[g], 16)

                    def stores(i):
                        sp.wait_ge(x1_ready, i + 1)
                        sp.dma_start(x1_dram[i].rearrange("(t p) d -> p t d", p=P), x_res[:, :, :]).then_inc(stored, 16)
                        sp.wait_ge(xn2_ready, i + 1)
                        sp.dma_start(xn2_dram[i].rearrange("(t p) d -> p t d", p=P), att[:, :, :]).then_inc(stored, 16)

                    def load_residual(i):
                        sp.wait_ge(stored, 32 * i)
                        sp.dma_start(x_res[:, :, :], x[i].rearrange("(t p) d -> p t d", p=P)).then_inc(xres_loaded, 16)

                    front_loads(0)
                    spread_k(0)
                    with sp.Fori(0, SEQS - 1) as j:
                        load_residual(j)
                        place_max(j)
                        front_loads(j + 1)
                        spread_k(j + 1)
                        stores(j)
                    load_residual(SEQS - 1)
                    place_max(SEQS - 1)
                    stores(SEQS - 1)
                    sp.wait_ge(stored, 32 * SEQS)

                @block.gpsimd
                def _(pool_):
                    e = nc.gpsimd
                    for tile in (pvT, x_res, wrk, bqk, brq, brk, latT, rv_mask, wrout, v_sb):
                        e.memset(tile[:], 0.0)
                    for tile in (kD_h, kD_l):
                        e.memset(tile[:].bitcast(f32), 0.0)
                    e.memset(ones[:, :], 1.0).then_inc(zeroed, 1)
                    pool_.wait_ge(zeroed, 1)
                    parts = [latT[LAT:LAT + 1, :]]
                    for hp in range(2):
                        parts.append(rv_mask[0:LAT, hp, 32 * hp:32 * hp + HD])
                        parts.append(rv_mask[LAT:P, hp, 32 * hp + HD:32 * hp + 2 * HD])
                    for n, part in enumerate(parts):
                        e.memset(part, 1.0).then_inc(zeroed, 1)
                        pool_.wait_ge(zeroed, n + 2)
                    e.memset(v_sb[:, :, :, HD:HD + 1], 1.0)
                    e.memset(ident[:, :], 0.0)
                    e.memset(mask_window[:, :], 0.0)
                    e.memset(mask_first[:, :], 0.0)
                    e.memset(lat_add[:, :, :], 0.0)
                    e.memset(lat_keep[:, :, :], 1.0)
                    e.memset(rk_mask[:, :, :], 1.0).then_inc(consts, 1)
                    pool_.wait_ge(consts, 1)
                    e.affine_select(out=ident[:, :], in_=ident[:, :], compare_op=ALU.not_equal, fill=1.0, base=0,
                                    pattern=[[-1, P]], channel_multiplier=1)
                    e.affine_select(out=mask_window[:, 0:P], in_=mask_window[:, 0:P], compare_op=ALU.is_gt, fill=NEG,
                                    base=0, pattern=[[P + 1, P]], channel_multiplier=-P)
                    e.affine_select(out=mask_window[:, P:WIN], in_=mask_window[:, P:WIN], compare_op=ALU.is_gt, fill=NEG,
                                    base=0, pattern=[[-1, P]], channel_multiplier=1)
                    e.affine_select(out=mask_first[:, :], in_=mask_first[:, :], compare_op=ALU.is_ge, fill=NEG,
                                    base=0, pattern=[[-P - 1, P]], channel_multiplier=P)
                    e.affine_select(out=lat_add[:, :, :], in_=lat_add[:, :, :], compare_op=ALU.is_ge, fill=NEG,
                                    base=-LC, pattern=[[P, T], [-LC, LAT]], channel_multiplier=1)
                    e.affine_select(out=lat_keep[:, :, :], in_=lat_keep[:, :, :], compare_op=ALU.is_ge, fill=0.0,
                                    base=-LC, pattern=[[P, T], [-LC, LAT]], channel_multiplier=1)
                    e.affine_select(out=rk_mask[:, :, :], in_=rk_mask[:, :, :], compare_op=ALU.is_ge, fill=0.0,
                                    base=0, pattern=[[-HD, LH], [0, LAT]], channel_multiplier=1).then_inc(consts, 1)
                    pool_.wait_ge(consts, 2)
                    e.affine_select(out=rk_mask[:, :, :], in_=rk_mask[:, :, :], compare_op=ALU.is_ge, fill=0.0,
                                    base=HD - 1, pattern=[[HD, LH], [0, LAT]], channel_multiplier=-1).then_inc(consts, 1)

                    def wait_alone(s, value):
                        value = value if isinstance(value, int) else pool_.to_reg(value)
                        pool_.wait_ge(consts, 1)
                        pool_.wait_ge(s, value)

                    def select(i):
                        n = 0
                        for g in range(G):
                            for b in range(T):
                                for hp in range(2):
                                    wait_alone(*keyed.read(i, f"T{g}{b}{hp}"))
                                    own = prob[:, n % 4, :, 0:P]
                                    op = e.affine_select(out=own, in_=own, compare_op=ALU.is_gt, fill=0.0, base=0,
                                                         pattern=[[0, 2], [1, P]], channel_multiplier=-1)
                                    if b < T - 1:
                                        after = prob[:, n % 4, :, P:WIN]
                                        op = e.affine_select(out=after, in_=after, compare_op=ALU.is_gt, fill=0.0, base=0,
                                                             pattern=[[0, 2], [-P, P]], channel_multiplier=P + 1)
                                    op.then_inc(prob_ready, 1)
                                    n += 1

                    with pool_.Fori(0, SEQS) as j:
                        select(j)

                @block.scalar
                def _(act):
                    e = nc.scalar

                    def minus_max(i, g):
                        act.wait_ge(*front.filled(i, f"m{g}"))
                        act.wait_ge(max_placed[g], 16 * i)
                        e.activation(maxT[:, g, :], FB[front.bank(f"m{g}")][0:HG, :], ACT.Copy,
                                     scale=-1.0).then_inc(front.free(f"m{g}"), 1)

                    def exps(i, g, b):
                        w = WIN if b < T - 1 else P
                        for hp in range(2):
                            n = (g * T + b) * 2 + hp
                            name = f"T{g}{b}{hp}"
                            act.wait_ge(*keyed.filled(i, name))
                            act.wait_ge(prob_used, 2 * G * T * i + max(n - 3, 0))
                            src = KB[keyed.bank(name)][:, :].rearrange("p (h q) -> p h q", h=2)
                            e.activation(prob[:, n % 4, :, 0:w], src[:, :, 0:w], ACT.Exp,
                                         scale=SCALE).then_inc(keyed.free(name), 1)

                    def keep_pv(i, g):
                        act.wait_ge(prob_used, 2 * T * (G * i + g + 1))
                        if g == 0:
                            act.wait_ge(*scores.all_filled(i, "pv3"))
                        e.activation(pvT[:, g, :], PV[g % 2][:, :], ACT.Copy).then_inc(pv_read, 1)

                    def mid(i):
                        minus_max(i, 0)
                        act.wait_ge(lat_max, i + 1)
                        e.activation(lat[:, :, :, :], lat[:, :, :, :], ACT.Exp, scale=SCALE).then_inc(lat_exp, 1)
                        for g in range(G):
                            for b in range(T):
                                exps(i, g, b)
                                if b == 0 and g >= 1:
                                    keep_pv(i, g - 1)
                                if g == 0 and b == 0:
                                    for hp in range(2):
                                        act.wait_ge(*front.filled(i, f"lT{hp}"))
                                        e.activation(latpT[:, hp, :], FB[front.bank(f"lT{hp}")][:, :],
                                                     ACT.Copy).then_inc(front.free(f"lT{hp}"), 1)
                                if g == 0 and b == 1:
                                    act.wait_ge(*front.filled(i, "lo"))
                                    e.activation(latT[0:LAT, :], FB[front.bank("lo")][0:LAT, :],
                                                 ACT.Copy).then_inc(front.free("lo"), 1)
                                if g < G - 1 and b == 2:
                                    minus_max(i, g + 1)
                        keep_pv(i, G - 1)

                    def seam(prev, nxt):
                        if nxt is not None:
                            for c in range(C):
                                act.wait_ge(*front.filled(nxt, f"xT{c}"))
                                e.activation(xT_h[:, c, :], FB[front.bank(f"xT{c}")][:, :], ACT.Identity).then_inc(xTh_ready, 1)
                        for t in range(T + 1):
                            if prev is not None and t < T:
                                act.wait_ge(z_ready, T * prev + t + 1)
                                e.activation(gate_s[:, t % 2, 3, :], gate_s[:, t % 2, 2, :], ACT.Exp,
                                             scale=-1.0).then_inc(sig_exp, 1)
                            if prev is not None and t >= 1:
                                u = t - 1
                                act.wait_ge(*scores.filled(prev, f"mix{u}"))
                                if u < 2:
                                    act.wait_ge(*outs.all_filled(prev, f"out{u + 2}"))
                                else:
                                    act.wait_ge(*outs.filled(prev, f"out{u - 2}"))
                                e.activation(mixT_h[:, u % 2, :, :].rearrange("p c n -> p (c n)"),
                                             SB[scores.bank(f"mix{u}")][:, 0:D], ACT.Copy).then_inc(mixTh_ready, 1)
                            if nxt is not None and t < T:
                                g = t
                                act.wait_ge(*front.filled(nxt, f"k{g}"))
                                act.wait_ge(k_spread[(g + 2) % G], 16 * 2 * HG * (nxt if g < 2 else nxt + 1))
                                e.activation(kT_h[:, g % 2, :], FB[front.bank(f"k{g}")][:, :], ACT.Identity,
                                             bias=bqk[:, 1, g:g + 1]).then_inc(kh_ready, 1)
                                act.wait_ge(*front.filled(nxt, f"q{g}"))
                                e.activation(qT_h[:, g, :], FB[front.bank(f"q{g}")][:, :], ACT.Identity,
                                             bias=bqk[:, 0, g:g + 1]).then_inc(qh_ready, 1)
                        if nxt is not None:
                            act.wait_ge(*front.filled(nxt, "rq"))
                            e.activation(rqT[:, :], FB[front.bank("rq")][:, :], ACT.Identity,
                                         bias=brq[:, 0:1]).then_inc(front.free("rq"), 1)

                    act.wait_ge(split, 1)
                    seam(None, 0)
                    with act.Fori(0, SEQS - 1) as j:
                        mid(j)
                        seam(j, j + 1)
                    mid(SEQS - 1)
                    seam(SEQS - 1, None)

                @block.vector
                def _(dve):
                    e = nc.vector
                    setup = Steps(step_setup, SETUP_STEPS)
                    norm1, latent, gates = Steps(step_front, NORM_STEPS), Steps(step_mid, LATENT_STEPS), Steps(step_tail, TAIL_STEPS)

                    def wait_alone(s, value):
                        value = value if isinstance(value, int) else dve.to_reg(value)
                        dve.wait_ge(consts, 1)
                        dve.wait_ge(s, value)

                    def link(steps, op, alone=False):
                        s, value = steps.next()
                        op.then_inc(s, 1)
                        (wait_alone if alone else dve.wait_ge)(s, value)

                    def rsqrt(steps, k):
                        y, v, w = rstd[:, k, 0, :], rstd[:, k, 1, :], rstd[:, k, 2, :]
                        link(steps, e.tensor_scalar(v, mv[:, k, :, 1], EPS, None, ALU.add))
                        link(steps, e.tensor_scalar(w.bitcast(i32), v.bitcast(i32), 1, None, ALU.logical_shift_right))
                        link(steps, e.tensor_scalar(y.bitcast(i32), w.bitcast(i32), -1, RSQRT_SEED, ALU.mult, ALU.add))
                        for _ in range(3):
                            link(steps, e.tensor_tensor(w, y, y, ALU.mult))
                            link(steps, e.scalar_tensor_tensor(w, w, -0.5, v, ALU.mult, ALU.mult))
                            link(steps, e.scalar_tensor_tensor(y, w, 1.5, y, ALU.add, ALU.mult))

                    setup.begin(0)
                    dve.wait_ge(weights_in, 16 * len(loads))
                    dve.wait_ge(consts, 3)
                    for c in range(C):
                        link(setup, e.tensor_tensor(wtmp.rearrange("p (h d) -> p h d", d=HD),
                                                    wv_f[:, c, 0:D].rearrange("p (h d) -> p h d", d=HD),
                                                    gl[:, :].unsqueeze(1).to_broadcast([P, HEADS, HD]), ALU.mult))
                        link(setup, e.tensor_reduce(wv_f[:, c, D:DA], wtmp.rearrange("p (h d) -> p h d", d=HD), AX.X, ALU.add))
                    for tile, vec in ((bv, gl), (wrout, gr)):
                        link(setup, e.tensor_tensor(wtmp.rearrange("p (h d) -> p h d", d=HD),
                                                    tile[:, 0:D].rearrange("p (h d) -> p h d", d=HD),
                                                    vec[:, :].unsqueeze(1).to_broadcast([P, HEADS, HD]), ALU.mult))
                        link(setup, e.tensor_reduce(tile[:, D:DA], wtmp.rearrange("p (h d) -> p h d", d=HD), AX.X, ALU.add))
                    for full, hi, lo in ((wqk_f, wqk_h, wqk_l), (wv_f, wv_h, wv_l), (wrq_f, wrq_h, wrq_l), (wout_f, wout_h, wout_l)):
                        link(setup, e.tensor_copy(hi[:], full))
                        op = e.tensor_tensor(lo[:], full, hi[:].bitcast(f32), ALU.subtract)
                    op.then_inc(split, 1)
                    setup.end()

                    def normalize(i):
                        norm1.begin(i)
                        dve.wait_ge(x_loaded, 16 * (i + 1))
                        for t in range(T):
                            op = e.bn_stats(stats[:, 0, t, :], x_in[:, t, :])
                        link(norm1, op, alone=True)
                        for t in range(T):
                            op = e.bn_aggr(mv[:, 0, t, :], stats[:, 0, t, :])
                        link(norm1, op)
                        rsqrt(norm1, 0)
                        dve.wait_ge(*front.all_filled(i, "xT1"))
                        for t in range(T):
                            op = e.tensor_scalar(xn[:, t, :], x_in[:, t, :], mv[:, 0, t, 0:1], rstd[:, 0, 0, t:t + 1],
                                                 ALU.subtract, ALU.mult)
                        op.then_inc(xn_ready, 1)
                        norm1.end()

                    def maxima(i, g):
                        for b in range(T):
                            for hp in range(2):
                                name = f"M{g}{b}{hp}"
                                wait_alone(*scores.filled(i, name))
                                for hh in range(2):
                                    src = SB[scores.bank(name)][:, hh * WIN:(hh + 1) * WIN]
                                    h = 2 * hp + hh
                                    if b == 0:
                                        src, mask = src[:, P:WIN], mask_first[:, :]
                                    else:
                                        mask = mask_window[:, :]
                                    op = e.tensor_tensor_reduce(out=src, in0=src, in1=mask, scale=1.0, scalar=3 * NEG,
                                                                op0=ALU.add, op1=ALU.max, accum_out=row_max[:, g, b, h:h + 1])
                                op.then_inc(scores.free(name), 1)

                    def latents_a(i):
                        latent.begin(i)
                        for n in range(2):
                            dve.wait_ge(*front.filled(i, f"ls{n}"))
                            op = e.tensor_tensor(lat[:, 2 * n:2 * n + 2, :, :],
                                                 FB[front.bank(f"ls{n}")][:, :].rearrange("p (t h l) -> p t h l", t=2, h=LH),
                                                 lat_add[:, 2 * n:2 * n + 2, :].unsqueeze(2).to_broadcast([P, 2, LH, LAT]), ALU.add)
                            op.then_inc(front.free(f"ls{n}"), 1)
                            dve.wait_ge(*front.read(i, f"ls{n}"))
                        flat = lat[:, :, :, :].rearrange("p t h l -> p (t h) l")
                        m = lat_s[:, 0, :, :].rearrange("p t h -> p (t h)")
                        link(latent, e.tensor_reduce(m, flat, AX.X, ALU.max))
                        e.tensor_tensor(flat, flat, m.unsqueeze(2).to_broadcast([P, T * LH, LAT]), ALU.subtract).then_inc(lat_max, 1)

                    def latents_b(i):
                        dve.wait_ge(lat_exp, i + 1)
                        flat = lat[:, :, :, :].rearrange("p t h l -> p (t h) l")
                        s, r = (lat_s[:, k, :, :].rearrange("p t h -> p (t h)") for k in (1, 2))
                        link(latent, e.tensor_tensor(lat[:, :, :, :], lat[:, :, :, :],
                                                     lat_keep[:, :, :].unsqueeze(2).to_broadcast([P, T, LH, LAT]), ALU.mult))
                        link(latent, e.tensor_reduce(s, flat, AX.X, ALU.add))
                        link(latent, e.tensor_scalar(s, s, TINY, None, ALU.max))
                        link(latent, e.reciprocal(r, s))
                        e.tensor_tensor(flat, flat, r.unsqueeze(2).to_broadcast([P, T * LH, LAT]), ALU.mult).then_inc(lat_ready, 1)
                        latent.end()

                    def mid(i):
                        maxima(i, 0)
                        latents_a(i)
                        maxima(i, 1)
                        latents_b(i)
                        maxima(i, 2)
                        maxima(i, 3)

                    def xT_low(i):
                        for c in range(C):
                            src = FB[front.bank(f"xT{c}")]
                            dve.wait_ge(xTh_ready, C * i + c + 1)
                            e.tensor_reduce(pool[:, c, :], src[:, :].rearrange("p (l k) -> p l k", k=LC), AX.X, ALU.add)
                            e.tensor_tensor(xT_l[:, c, :], src[:, :], xT_h[:, c, :].bitcast(f32), ALU.subtract
                                            ).then_inc(front.free(f"xT{c}"), 1)
                            dve.wait_ge(*front.read(i, f"xT{c}"))
                        op = e.tensor_scalar(pool2[:, :, :, :], pool[:, :, :].unsqueeze(2).to_broadcast([P, C, 2, LAT]),
                                             1.0 / LC, None, ALU.mult)
                        op.then_inc(pool_ready, 1)

                    def kq_low(i, g):
                        for name, ready, j, hi, lo in (("k", kh_ready, 1, kT_h[:, g % 2, :], kT_l[:, g % 2, :]),
                                                       ("q", qh_ready, 0, qT_h[:, g, :], qT_l[:, g, :])):
                            dve.wait_ge(ready, G * i + g + 1)
                            e.scalar_tensor_tensor(lo, FB[front.bank(f"{name}{g}")][:, :], bqk[:, j, g:g + 1],
                                                   hi.bitcast(f32), ALU.add, ALU.subtract
                                                   ).then_inc(front.free(f"{name}{g}"), 1)

                    def values(i):
                        for t in range(T):
                            src = FB[front.bank(f"v{t}")]
                            dve.wait_ge(*front.filled(i, f"v{t}"))
                            e.tensor_tensor(v_sb[:, t, :, 0:HD], src[:, 0:D].rearrange("p (h d) -> p h d", d=HD),
                                            bv[:, 0:D].rearrange("p (h d) -> p h d", d=HD), ALU.add)
                            e.tensor_tensor(v_sb[:, t, :, HD + 1], src[:, D:DA], bv[:, D:DA], ALU.add).then_inc(front.free(f"v{t}"), 1)

                    def latent_keys(i):
                        dve.wait_ge(*front.filled(i, "rk"))
                        e.tensor_scalar(rk_t[:, :], FB[front.bank("rk")][:, 0:LAT], brk[:, 0:1], None, ALU.add).then_inc(front.free("rk"), 1)
                        dve.wait_ge(*front.read(i, "rk"))
                        e.tensor_tensor(rkD[:, :, :], rk_mask[:, :, :], rk_t[:, :].unsqueeze(1).to_broadcast([P, LH, LAT]), ALU.mult)
                        dve.wait_ge(*front.filled(i, "rv"))
                        e.tensor_tensor(rv_t[:, :], FB[front.bank("rv")][:, 0:LAT], brv[:, :], ALU.add).then_inc(front.free("rv"), 1)
                        dve.wait_ge(*front.read(i, "rv"))
                        e.tensor_tensor(rvD[:, :, :], rv_mask[:, :, :], rv_t[:, :].unsqueeze(1).to_broadcast([P, 2, LAT]),
                                        ALU.mult).then_inc(rv_ready, 1)

                    def gate_in(i, t):
                        u = t % 2
                        a = SB[scores.bank(f"pv{t}")][:, :].rearrange("p (n w) -> p n w", w=PAD)
                        r = KB[keyed.bank(f"rem{t}")]
                        loc = mixed[:, u, :].rearrange("p (n d) -> p n d", d=HD)
                        dve.wait_ge(*scores.filled(i, f"pv{t}"))
                        link(gates, e.tensor_scalar(gate_s[:, u, 0, :], a[:, :, HD], TINY, None, ALU.max))
                        link(gates, e.reciprocal(gate_s[:, u, 1, :], gate_s[:, u, 0, :]))
                        link(gates, e.tensor_tensor(gate_s[:, u, 0, :], a[:, :, HD + 1], gate_s[:, u, 1, :], ALU.mult))
                        dve.wait_ge(*keyed.filled(i, f"rem{t}"))
                        e.tensor_tensor(gate_s[:, u, 2, :], r[:, D:DA], gate_s[:, u, 0, :], ALU.add).then_inc(z_ready, 1)
                        if t >= 2:
                            dve.wait_ge(*scores.filled(i, f"mix{t - 2}"))
                        e.tensor_tensor(loc, a[:, :, 0:HD], gate_s[:, u, 1, :].unsqueeze(2).to_broadcast([P, HEADS, HD]),
                                        ALU.mult).then_inc(scores.free(f"pv{t}"), 1)
                        dve.wait_ge(*scores.read(i, f"pv{t}"))
                        link(gates, e.tensor_tensor(mixed[:, u, :], mixed[:, u, :], r[:, 0:D], ALU.subtract))

                    def gate_out(i, t):
                        u = t % 2
                        loc = mixed[:, u, :].rearrange("p (n d) -> p n d", d=HD)
                        dve.wait_ge(sig_exp, T * i + t + 1)
                        link(gates, e.tensor_scalar(gate_s[:, u, 4, :], gate_s[:, u, 3, :], 1.0, None, ALU.add))
                        link(gates, e.reciprocal(gate_s[:, u, 5, :], gate_s[:, u, 4, :]))
                        link(gates, e.tensor_tensor(loc, loc, gate_s[:, u, 5, :].unsqueeze(2).to_broadcast([P, HEADS, HD]), ALU.mult))
                        e.tensor_tensor(mixed[:, u, :], mixed[:, u, :], KB[keyed.bank(f"rem{t}")][:, 0:D],
                                        ALU.add).then_inc(keyed.free(f"rem{t}"), 1)

                    def mix_low(i, t):
                        dve.wait_ge(mixTh_ready, T * i + t + 1)
                        e.tensor_tensor(mixT_l[:, t % 2, :, :].rearrange("p c n -> p (c n)"), SB[scores.bank(f"mix{t}")][:, 0:D],
                                        mixT_h[:, t % 2, :, :].rearrange("p c n -> p (c n)").bitcast(f32),
                                        ALU.subtract).then_inc(scores.free(f"mix{t}"), 1)

                    def add_bias(i, t):
                        dve.wait_ge(*outs.filled(i, f"out{t}"))
                        if t == 0:
                            dve.wait_ge(stored, 32 * i)
                        e.tensor_tensor(att[:, t, :], PV[outs.bank(f"out{t}")][:, 0:D], bout[:, :], ALU.add
                                        ).then_inc(outs.free(f"out{t}"), 1)
                        dve.wait_ge(*outs.read(i, f"out{t}"))
                        op = e.bn_stats(stats[:, 1, t, :], att[:, t, :])
                        if t == T - 1:
                            link(gates, op, alone=True)

                    def residual(i):
                        for t in range(T):
                            op = e.bn_aggr(mv[:, 1, t, :], stats[:, 1, t, :])
                        link(gates, op)
                        rsqrt(gates, 1)
                        for t in range(T):
                            op = e.tensor_scalar(att[:, t, :], att[:, t, :], mv[:, 1, t, 0:1], rstd[:, 1, 0, t:t + 1],
                                                 ALU.subtract, ALU.mult)
                        link(gates, op)
                        dve.wait_ge(xres_loaded, 16 * (i + 1))
                        for t in range(T):
                            op = e.tensor_tensor(x_res[:, t, :], x_res[:, t, :], att[:, t, :], ALU.add)
                        op.then_inc(x1_ready, 1)
                        dve.wait_ge(x1_ready, i + 1)
                        for t in range(T):
                            op = e.bn_stats(stats[:, 2, t, :], x_res[:, t, :])
                        link(gates, op, alone=True)
                        for t in range(T):
                            op = e.bn_aggr(mv[:, 2, t, :], stats[:, 2, t, :])
                        link(gates, op)
                        rsqrt(gates, 2)
                        for t in range(T):
                            op = e.tensor_scalar(att[:, t, :], x_res[:, t, :], mv[:, 2, t, 0:1], rstd[:, 2, 0, t:t + 1],
                                                 ALU.subtract, ALU.mult)
                        op.then_inc(xn2_ready, 1)

                    def seam(prev, nxt):
                        if prev is not None:
                            gates.begin(prev)
                        if nxt is not None:
                            normalize(nxt)
                            xT_low(nxt)
                        for t in range(T + 3):
                            if prev is not None:
                                if t < T:
                                    gate_in(prev, t)
                                if 1 <= t <= T:
                                    gate_out(prev, t - 1)
                            if nxt is not None and 1 <= t <= T:
                                kq_low(nxt, t - 1)
                            if prev is not None:
                                if 1 <= t <= T:
                                    mix_low(prev, t - 1)
                                if t >= 3:
                                    add_bias(prev, t - 3)
                        if nxt is not None:
                            values(nxt)
                            latent_keys(nxt)
                        if prev is not None:
                            residual(prev)
                            gates.end()

                    seam(None, 0)
                    with dve.Fori(0, SEQS - 1) as j:
                        mid(j)
                        seam(j, j + 1)
                    mid(SEQS - 1)
                    seam(SEQS - 1, None)

                @block.tensor
                def _(pe):
                    e = nc.tensor

                    def exact(out_, lh, ll, rh, rl, first, last):
                        e.matmul(out_, lh, rh, start=first, stop=False)
                        e.matmul(out_, lh, rl, start=False, stop=False)
                        return e.matmul(out_, ll, rh, start=False, stop=last)

                    def window(i, g, b):
                        lo, w = (P, P) if b == 0 else (0, WIN)
                        for hp in range(2):
                            name = f"M{g}{b}{hp}"
                            pe.wait_ge(*scores.drained(i, name))
                            dst = SB[scores.bank(name)][:, :].rearrange("p (h q) -> p h q", h=2)[:, :, lo:WIN]
                            k0 = max(b - 1, 0) * P
                            e.matmul(dst, qT_h[:, g, b * P:(b + 1) * P], kD_h[:, g, 2 * hp:2 * hp + 2, k0:k0 + w],
                                     start=True, stop=True).then_inc(scores.full(name), 1)

                    def windows(i, g):
                        pe.wait_ge(k_spread[g], 16 * 2 * HG * (i + 1))
                        for b in range(T):
                            window(i, g, b)

                    def turn_max(i, g):
                        name = f"m{g}"
                        for bank in range(2):
                            pe.wait_ge(*scores.read(i, f"M{g}{T - 1}{bank}"))
                        pe.wait_ge(*front.drained(i, name))
                        for b in range(T):
                            op = e.matmul(FB[front.bank(name)][0:HG, b * P:(b + 1) * P], row_max[:, g, b, :], ident[:, :],
                                          start=True, stop=True, is_transpose=True)
                        op.then_inc(front.full(name), 1)

                    def keyed_scores(i, g, b):
                        w = WIN if b < T - 1 else P
                        for hp in range(2):
                            name = f"T{g}{b}{hp}"
                            pe.wait_ge(*keyed.drained(i, name))
                            for hh in range(2):
                                h = 2 * hp + hh
                                k, q = slice(b * P, (b + 1) * P), slice(b * P, b * P + w)
                                op = exact(KB[keyed.bank(name)][:, hh * WIN:hh * WIN + w],
                                           kD_h[:, g, h, k], kD_l[:, g, h, k], qT_h[:, g, q], qT_l[:, g, q], True, True)
                            op.then_inc(keyed.full(name), 1)

                    def weigh_values(i, n):
                        g, b, hp = n // (2 * T), n // 2 % T, n % 2
                        w = WIN if b < T - 1 else P
                        pe.wait_ge(prob_ready, 2 * G * T * i + n + 1)
                        if b == 0 and hp == 0:
                            pe.wait_ge(pv_read, G * i + max(g - 1, 0))
                            if g < 2:
                                pe.wait_ge(*outs.drained(i, f"out{g}"))
                        for hh in range(2):
                            h = 2 * hp + hh
                            op = e.matmul(PV[g % 2][h * PAD:(h + 1) * PAD, b * P:b * P + w], v_sb[:, b, g * HG + h, :],
                                          prob[:, n % 4, hh, 0:w], start=(b == 0), stop=(b == T - 1),
                                          skip_group_check=True)
                        op.then_inc(prob_used, 1)

                    def mid(i):
                        for name in ("v3", "rq"):
                            pe.wait_ge(*front.read(i, name))
                        pe.wait_ge(rv_ready, i + 1)
                        windows(i, 0)
                        for n in range(2):
                            name = f"ls{n}"
                            pe.wait_ge(*front.drained(i, name))
                            for t in (2 * n, 2 * n + 1):
                                op = e.matmul(FB[front.bank(name)][:, (t % 2) * WIN:(t % 2 + 1) * WIN], rqT[:, t * P:(t + 1) * P],
                                              rkD[:, :, :].rearrange("p h l -> p (h l)"), start=True, stop=True)
                            op.then_inc(front.full(name), 1)
                        windows(i, 1)
                        turn_max(i, 0)
                        n = 0
                        for g in range(G):
                            if g + 2 < G:
                                pe.wait_ge(k_spread[g + 2], 16 * 2 * HG * (i + 1))
                            pe.wait_ge(max_placed[g], 16 * (i + 1))
                            for b in range(T):
                                if g + 2 < G:
                                    window(i, g + 2, b)
                                keyed_scores(i, g, b)
                                for _ in range(2):
                                    if n >= 2:
                                        weigh_values(i, n - 2)
                                    n += 1
                                if g == 0 and b == 0:
                                    pe.wait_ge(lat_ready, i + 1)
                                    for hp in range(2):
                                        name = f"lT{hp}"
                                        pe.wait_ge(*front.drained(i, name))
                                        for t in range(T):
                                            op = e.matmul(FB[front.bank(name)][:, t * P:(t + 1) * P],
                                                          lat[:, t, 2 * hp:2 * hp + 2, :].rearrange("p h l -> p (h l)"), ident[:, :],
                                                          start=True, stop=True, is_transpose=True)
                                        op.then_inc(front.full(name), 1)
                                if g == 0 and b == 1:
                                    pe.wait_ge(*front.drained(i, "lo"))
                                    for hp in range(2):
                                        pe.wait_ge(*front.read(i, f"lT{hp}"))
                                        op = e.matmul(FB[front.bank("lo")][0:LAT, :], rvD[:, hp, :], latpT[:, hp, :],
                                                      start=(hp == 0), stop=(hp == 1))
                                    op.then_inc(front.full("lo"), 1)
                                if g < G - 1 and b == 2:
                                    turn_max(i, g + 1)
                        weigh_values(i, n - 2)
                        weigh_values(i, n - 1)

                    def seam(prev, nxt):
                        if nxt is not None:
                            pe.wait_ge(xn_ready, nxt + 1)
                            for c in range(C):
                                name = f"xT{c}"
                                pe.wait_ge(*front.drained(nxt, name))
                                for t in range(T):
                                    op = e.matmul(FB[front.bank(name)][:, t * P:(t + 1) * P], xn[:, t, c * P:(c + 1) * P], ident[:, :],
                                                  start=True, stop=True, is_transpose=True)
                                op.then_inc(front.full(name), 1)
                        for t in range(T + 2):
                            if prev is not None:
                                if t < T:
                                    name = f"pv{t}"
                                    pe.wait_ge(pv_read, G * (prev + 1))
                                    pe.wait_ge(*scores.drained(prev, name))
                                    for g in range(G):
                                        op = e.matmul(SB[scores.bank(name)][:, g * P:(g + 1) * P], pvT[:, g, t * P:(t + 1) * P],
                                                      ident[:, :], start=True, stop=True, is_transpose=True)
                                    op.then_inc(scores.full(name), 1)
                                if t >= 2:
                                    u, name = t - 2, f"out{t - 2}"
                                    pe.wait_ge(*scores.read(prev, f"mix{u}"))
                                    pe.wait_ge(*outs.drained(prev, name))
                                    for c in range(C):
                                        op = exact(PV[outs.bank(name)][:, 0:D], mixT_h[:, u % 2, c, :], mixT_l[:, u % 2, c, :],
                                                   wout_h[:, c, :], wout_l[:, c, :], c == 0, c == C - 1)
                                    op.then_inc(outs.full(name), 1)
                                if t < T:
                                    name = f"rem{t}"
                                    pe.wait_ge(*front.read(prev, "lo"))
                                    pe.wait_ge(*keyed.drained(prev, name))
                                    e.matmul(KB[keyed.bank(name)][:, 0:DA], latT[:, t * P:(t + 1) * P], wrout[:, :],
                                             start=True, stop=True).then_inc(keyed.full(name), 1)
                                if 1 <= t <= T:
                                    u, name = t - 1, f"mix{t - 1}"
                                    pe.wait_ge(*keyed.read(prev, f"rem{u}"))
                                    pe.wait_ge(*scores.drained(prev, name))
                                    for c in range(C):
                                        op = e.matmul(SB[scores.bank(name)][:, c * P:(c + 1) * P], mixed[:, u % 2, c * P:(c + 1) * P],
                                                      ident[:, :], start=True, stop=True, is_transpose=True)
                                    op.then_inc(scores.full(name), 1)
                            if nxt is not None and t < T:
                                for j, kind in ((1, "k"), (0, "q")):
                                    name = f"{kind}{t}"
                                    if name == "k0":
                                        for c in range(C):
                                            pe.wait_ge(*front.read(nxt, f"xT{c}"))
                                    pe.wait_ge(*front.drained(nxt, name))
                                    w = slice(t * P, (t + 1) * P)
                                    for c in range(C):
                                        op = exact(FB[front.bank(name)][:, :], wqk_h[:, j, c, w], wqk_l[:, j, c, w],
                                                   xT_h[:, c, :], xT_l[:, c, :], c == 0, c == C - 1)
                                    op.then_inc(front.full(name), 1)
                        if nxt is not None:
                            for t in range(T):
                                name = f"v{t}"
                                pe.wait_ge(*front.drained(nxt, name))
                                for c in range(C):
                                    op = exact(FB[front.bank(name)][:, 0:DA], xT_h[:, c, t * P:(t + 1) * P], xT_l[:, c, t * P:(t + 1) * P],
                                               wv_h[:, c, :], wv_l[:, c, :], c == 0, c == C - 1)
                                op.then_inc(front.full(name), 1)
                            pe.wait_ge(*front.drained(nxt, "rq"))
                            for c in range(C):
                                op = exact(FB[front.bank("rq")][:, :], wrq_h[:, c, :], wrq_l[:, c, :],
                                           xT_h[:, c, :], xT_l[:, c, :], c == 0, c == C - 1)
                            op.then_inc(front.full("rq"), 1)
                            pe.wait_ge(pool_ready, nxt + 1)
                            pe.wait_ge(*front.drained(nxt, "rk"))
                            for c in range(C):
                                op = e.matmul(FB[front.bank("rk")][:, 0:LAT], wrk[:, c, :], pool2[:, c, 0, :],
                                              start=(c == 0), stop=(c == C - 1))
                            op.then_inc(front.full("rk"), 1)
                            pe.wait_ge(*front.drained(nxt, "rv"))
                            for c in range(C):
                                op = e.matmul(FB[front.bank("rv")][:, 0:LAT], pool2[:, c, :, :].rearrange("p a l -> p (a l)"), wrv[:, c, :],
                                              start=(c == 0), stop=(c == C - 1))
                            op.then_inc(front.full("rv"), 1)

                    pe.wait_ge(split, 1)
                    seam(None, 0)
                    with pe.Fori(0, SEQS - 1) as j:
                        mid(j)
                        seam(j, j + 1)
                    mid(SEQS - 1)
                    seam(SEQS - 1, None)

        ffn = ExitStack()
        with ffn:
            def sb(name, shape, dt=f32):
                return ffn.enter_context(nc.sbuf_tensor(name, shape, dt))

            TILES = SEQS * T
            REGION = SEQS * S + P
            BLOCKS = 2 * TILES + E - 1
            FCS = -(-FS // P)
            FCE = -(-F // P)
            fs = [min(P, FS - n * P) for n in range(FCS)]
            fe = [min(P, F - n * P) for n in range(FCE)]
            TOP_SCALE, TOP_EPS = 2.5, 1e-20

            xg_dram = nc.dram_tensor("xg_scratch", (E * REGION + P, D), f32, kind="Internal").ap()
            yg_dram = nc.dram_tensor("yg_scratch", ((BLOCKS + 1) * P, D), f32, kind="Internal").ap()
            ys_dram = nc.dram_tensor("ys_scratch", (SEQS, S, D), f32, kind="Internal").ap()

            wgu_h = sb("wgu_h", [P, E * C, 2, F], f32r)
            wgu_l = sb("wgu_l", [P, E * C, 2, F], f32r)
            pos_all = sb("pos_all", [P, TILES, 2], i32)
            lg_all = sb("lg_all", [P, TILES, E])
            oh_all = sb("oh_all", [P, 2, TILES, E])
            member = sb("member", [P, E])
            counts = sb("counts", [P, E])
            table = sb("table", [1, 2, BLOCKS + 1], i32)
            shift = sb("shift", [P, E])

            ffn_zeroed, ffn_consts = sem("ffn_zeroed"), sem("ffn_consts")
            consts_ready = sem("consts_ready")
            shared_in, shared_split = sem("shared_in"), sem("shared_split")
            stage_in, stage_split = [sem("stage_in0"), sem("stage_in1")], sem("stage_split")
            counted, table_ready, spare_ready = sem("counted"), sem("table_ready"), sem("spare_ready")
            spare_zeroed, router_done = sem("spare_zeroed"), sem("router_done")
            row_loaded = [sem("row_loaded0"), sem("row_loaded1")]
            scattered = [sem("scattered0"), sem("scattered1")]
            xh2_ready, xh2_low = sem("xh2_ready"), sem("xh2_low")
            pos_ready, member_ready = sem("pos_ready"), sem("member_ready")
            h_ready, hh_ready, hl_ready = sem("h_ready"), sem("hh_ready"), sem("hl_ready")
            router_split, h_used, ys_stored = sem("router_split"), sem("h_used"), sem("ys_stored")
            step_route, step_end = sem("step_route"), sem("step_end")

            small = Banks([["xT0", "lg"], ["xT1", "rk"]], [sem("small_full0"), sem("small_full1")],
                          [sem("small_free0"), sem("small_free1")])
            SM = [psum[6], psum[7]]
            gates2 = Banks([[f"g{n}" for n in range(0, FCS, 2)], [f"g{n}" for n in range(1, FCS, 2)]],
                           [sem("gate_full0"), sem("gate_full1")], [sem("gate_free0"), sem("gate_free1")])
            ys = Banks([["y0"], ["y1"]], [h_used, h_used], [sem("ys_free0"), sem("ys_free1")])
            YB = [psum[4], psum[5]]

            shared = ExitStack()
            with shared:
                def sb(name, shape, dt=f32):
                    return shared.enter_context(nc.sbuf_tensor(name, shape, dt))

                ws_h = sb("ws_h", [P, C, 2, FS], f32r)
                ws_l = sb("ws_l", [P, C, 2, FS], f32r)
                wsd_h = sb("wsd_h", [P, FCS, D], f32r)
                wsd_l = sb("wsd_l", [P, FCS, D], f32r)
                stage = sb("stage", [P, 2, 2 * F])
                wr_f = sb("wr_f", [P, C, E])
                wr_h = sb("wr_h", [P, C, E], f32r)
                wr_l = sb("wr_l", [P, C, E], f32r)
                before = sb("before", [P, P])
                all_ones = sb("all_ones", [P, P])
                base = sb("base", [P, E])
                base_p = sb("base_p", [P, E + 1])
                falling = sb("falling", [P, E])
                zeros = sb("zeros", [P, D])
                spare = sb("spare", [P, E + 1], i32)
                spare_f = sb("spare_f", [P, E + 1])
                rows = sb("rows", [P, 2, T, D])
                rT_h = sb("rT_h", [P, C, S], f32r)
                rT_l = sb("rT_l", [P, C, S], f32r)
                silu = sb("silu", [P, 2, S])
                h_f = sb("h_f", [P, 2, S])
                h_h = sb("h_h", [P, 2, S], f32r)
                h_l = sb("h_l", [P, 2, S], f32r)
                y_sb = sb("y_sb", [P, T, D])
                rt = sb("rt", [P, 8, T, E])
                rt1 = sb("rt1", [P, 6, T])
                pos = sb("pos", [P, 2, T, 2], i32)
                pos_f = sb("pos_f", [P, T, 2])
                grid_i = sb("grid_i", [1, 2, (BLOCKS + 1) * E], i32)
                grid = sb("grid", [1, 4, BLOCKS + 1, E])
                line = sb("line", [1, 6, BLOCKS + 1])
                cum = sb("cum", [P, 5, E])
                cum_i = sb("cum_i", [P, E], i32)
                iota_i = sb("iota_i", [P, 2, E + 1], i32)

                shared_pieces = []
                for c in range(C):
                    for j, w in ((0, sw_gate), (1, sw_up)):
                        shared_pieces.append((w[c * P:(c + 1) * P, :], P, FS, ws_h[:, c, j, :], ws_l[:, c, j, :]))
                for n in range(FCS):
                    shared_pieces.append((sw_down[n * P:n * P + fs[n], :], fs[n], D, wsd_h[0:fs[n], n, :], wsd_l[0:fs[n], n, :]))
                SHARED = len(shared_pieces)
                assert SHARED % 2 == 0 and E * C == SEQS

                with nc.Block() as block:

                    @block.sync
                    def _(sp):
                        sp.wait_ge(stored, 32 * SEQS)
                        with nc.allow_non_contiguous_dma(reason="the router's 2048 weights, once"):
                            for c in range(C):
                                sp.dma_start(wr_f[:, c, :], gate_w[:, c * P:(c + 1) * P].rearrange("e p -> p e")).then_inc(shared_in, 16)

                        def load(j, u):
                            sp.wait_ge(scattered[u], 16 * 2 * T * j)
                            sp.dma_start(rows[:, u, :, :], xn2_dram[bass.ds(2 * j + u, 1)].rearrange("a (t p) d -> p (a t) d", p=P)
                                         ).then_inc(row_loaded[u], 16)

                        def store(i):
                            for name in ("y0", "y1"):
                                sp.wait_ge(*ys.read(i, name))
                            sp.dma_start(ys_dram[bass.ds(i, 1)].rearrange("a (t p) d -> p (a t) d", p=P), y_sb[:, :, :]).then_inc(ys_stored, 16)

                        def expert_chunk(i, u):
                            sp.wait_ge(stage_split, SHARED + i - 1)
                            for k, w in ((0, w_gate), (1, w_up)):
                                rows_of = w.rearrange("e (c p) f -> (e c) p f", p=P)
                                sp.dma_start(stage[:, u, k * F:(k + 1) * F], rows_of[bass.ds(i, 1)].rearrange("a p f -> p (a f)")
                                             ).then_inc(stage_in[u], 16)

                        load(0, 0)
                        for n, (src, p, w, _, _) in enumerate(shared_pieces):
                            if n >= 2:
                                sp.wait_ge(stage_split, n - 1)
                            sp.dma_start(stage[0:p, n % 2, 0:w], src).then_inc(stage_in[n % 2], 16)
                        load(0, 1)
                        with sp.Fori(0, SEQS // 2 - 1) as j:
                            expert_chunk(2 * j, 0)
                            store(2 * j)
                            load(j + 1, 0)
                            expert_chunk(2 * j + 1, 1)
                            store(2 * j + 1)
                            load(j + 1, 1)
                        for u in range(2):
                            expert_chunk(SEQS - 2 + u, u)
                            store(SEQS - 2 + u)

                    @block.gpsimd
                    def _(gp):
                        e = nc.gpsimd
                        gp.wait_ge(stored, 32 * SEQS)
                        e.memset(zeros[:, :], 0.0)
                        e.memset(member[:, :], 0.0)
                        e.memset(all_ones[:, :], 1.0)
                        e.memset(before[:, :], 1.0).then_inc(ffn_zeroed, 1)
                        gp.wait_ge(ffn_zeroed, 1)
                        e.affine_select(out=before[:, :], in_=before[:, :], compare_op=ALU.is_gt, fill=0.0, base=0,
                                        pattern=[[1, P]], channel_multiplier=-1)
                        e.iota(iota_i[:, 0, :], pattern=[[REGION, E + 1]], base=0, channel_multiplier=1)
                        e.iota(iota_i[:, 1, 0:E], pattern=[[-1, E]], base=E, channel_multiplier=0)
                        e.iota(grid_i[:, 0, :], pattern=[[1, BLOCKS + 1], [0, E]], base=0, channel_multiplier=0)
                        e.iota(grid_i[:, 1, :], pattern=[[0, BLOCKS + 1], [1, E]], base=0, channel_multiplier=0).then_inc(ffn_consts, 1)

                        def scatter(i, u):
                            value = gp.to_reg(i + 1)
                            gp.wait_ge(ffn_consts, 1)
                            gp.wait_ge(pos_ready, value)
                            for t in range(T):
                                for k in range(2):
                                    e.indirect_dma_start(out=xg_dram, out_offset=bass.IndirectOffsetOnAxis(ap=pos[:, u, t, k:k + 1], axis=0),
                                                         in_=rows[:, u, t, :], in_offset=None).then_inc(scattered[u], 16)

                        def split_chunk(j, u):
                            i = 2 * j + u
                            full = stage[:, u, :]
                            hi, lo = (w[:, bass.ds(i, 1), :, :].rearrange("p a k f -> p (a k f)") for w in (wgu_h, wgu_l))
                            gp.wait_ge(stage_in[u], 16 * (SHARED // 2 + 2 * (j + 1)))
                            e.tensor_copy(hi, full).then_inc(shared_split, 1)
                            gp.wait_ge(shared_split, SHARED + i + 1)
                            e.tensor_tensor(lo, full, hi.bitcast(f32), ALU.subtract).then_inc(stage_split, 1)

                        for n, (_, p, w, hi, lo) in enumerate(shared_pieces):
                            gp.wait_ge(stage_in[n % 2], 16 * (n // 2 + 1))
                            e.tensor_copy(hi, stage[0:p, n % 2, 0:w]).then_inc(shared_split, 1)
                            gp.wait_ge(shared_split, n + 1)
                            e.tensor_tensor(lo, stage[0:p, n % 2, 0:w], hi.bitcast(f32), ALU.subtract).then_inc(stage_split, 1)
                        with gp.Fori(0, SEQS // 2) as j:
                            for u in range(2):
                                split_chunk(j, u)
                                scatter(2 * j + u, u)
                        gp.wait_ge(spare_ready, 1)
                        for u in range(2):
                            gp.wait_ge(scattered[u], 16 * T * SEQS)
                        for x_ in range(E + 1):
                            e.indirect_dma_start(out=xg_dram, out_offset=bass.IndirectOffsetOnAxis(ap=spare[:, x_:x_ + 1], axis=0),
                                                 in_=zeros[:, :], in_offset=None).then_inc(spare_zeroed, 16)
                        gp.wait_ge(spare_zeroed, 16 * (E + 1))

                    @block.scalar
                    def _(act):
                        e = nc.scalar
                        act.wait_ge(stored, 32 * SEQS)

                        def hidden_high(i, n):
                            p = fs[n]
                            act.wait_ge(h_ready, FCS * i + n + 1)
                            act.wait_ge(h_used, FCS * i + max(n - 1, 0))
                            e.activation(h_h[0:p, n % 2, :], h_f[0:p, n % 2, :], ACT.Copy).then_inc(hh_ready, 1)

                        with act.Fori(0, SEQS) as i:
                            for c in range(C):
                                name = f"xT{c}"
                                act.wait_ge(*small.filled(i, name))
                                e.activation(rT_h[:, c, :], SM[small.bank(name)][:, :], ACT.Copy).then_inc(xh2_ready, 1)
                            for n in range(FCS):
                                name, p = f"g{n}", fs[n]
                                act.wait_ge(*gates2.filled(i, name))
                                act.wait_ge(h_ready, FCS * i + max(n - 1, 0))
                                e.activation(silu[0:p, n % 2, :], psum[n % 2][0:p, :], ACT.Silu
                                             ).then_inc(gates2.free(name), 1)
                                if n >= 1:
                                    hidden_high(i, n - 1)
                            hidden_high(i, FCS - 1)
                            act.wait_ge(ys_stored, 16 * i)
                            for n in range(2):
                                name = f"y{n}"
                                act.wait_ge(h_used, FCS * (i + 1))
                                e.activation(y_sb[:, 2 * n:2 * n + 2, :].rearrange("p t d -> p (t d)"), YB[n][:, :],
                                             ACT.Copy).then_inc(ys.free(name), 1)

                    @block.vector
                    def _(dve):
                        e = nc.vector
                        route, ending = Steps(step_route, ROUTE_STEPS), Steps(step_end, END_STEPS)

                        def wait_alone(s, value):
                            value = value if isinstance(value, int) else dve.to_reg(value)
                            dve.wait_ge(ffn_consts, 1)
                            dve.wait_ge(s, value)

                        def link(steps, op, alone=False):
                            s, value = steps.next()
                            op.then_inc(s, 1)
                            (wait_alone if alone else dve.wait_ge)(s, value)

                        def over_e(ap):
                            return ap.unsqueeze(2).to_broadcast([P, T, E])

                        def over_t(ap):
                            return ap.unsqueeze(1).to_broadcast([P, T, E])

                        dve.wait_ge(stored, 32 * SEQS)
                        ending.begin(0)
                        dve.wait_ge(ffn_consts, 1)
                        e.tensor_copy(base_p[:, :], iota_i[:, 0, :])
                        e.tensor_copy(falling[:, :], iota_i[:, 1, 0:E])
                        e.tensor_copy(grid[:, 0, :, :].rearrange("a b x -> a (b x)"), grid_i[:, 0, :])
                        link(ending, e.tensor_copy(grid[:, 1, :, :].rearrange("a b x -> a (b x)"), grid_i[:, 1, :]))
                        for x_ in range(E):
                            op = e.memset(base[:, x_:x_ + 1], float(x_ * REGION))
                        link(ending, op)
                        dve.wait_ge(shared_in, 16 * C)
                        link(ending, e.tensor_copy(wr_h[:, :, :], wr_f[:, :, :]))
                        e.tensor_tensor(wr_l[:, :, :], wr_f[:, :, :], wr_h[:, :, :].bitcast(f32), ALU.subtract).then_inc(router_split, 1)

                        def choose(i):
                            route.begin(i)
                            m1, k1, m2, k2 = (rt1[:, k, :] for k in range(4))
                            L, eq, key, oh1, rest, oh2, both, cpre = (rt[:, k, :, :] for k in range(8))
                            dve.wait_ge(*small.filled(i, "lg"))
                            e.tensor_copy(L, SM[small.bank("lg")][:, 0:T * E].rearrange("p (t x) -> p t x", t=T)).then_inc(small.free("lg"), 1)
                            dve.wait_ge(*small.read(i, "lg"))
                            for scores_, m, k, oh in ((L, m1, k1, oh1), (rest, m2, k2, oh2)):
                                link(route, e.tensor_reduce(m, scores_, AX.X, ALU.max))
                                link(route, e.tensor_tensor(eq, scores_, over_e(m), ALU.is_equal))
                                link(route, e.tensor_tensor(key, eq, over_t(falling[:, :]), ALU.mult))
                                link(route, e.tensor_reduce(k, key, AX.X, ALU.max))
                                link(route, e.tensor_tensor(oh, key, over_e(k), ALU.is_equal))
                                if oh is oh1:
                                    link(route, e.scalar_tensor_tensor(rest, oh1, NEG, L, ALU.mult, ALU.add))
                            e.tensor_tensor(lg_all[:, bass.ds(T * i, T), :], L, over_e(m1), ALU.subtract)
                            e.tensor_copy(oh_all[:, 0, bass.ds(T * i, T), :], oh1)
                            e.tensor_copy(oh_all[:, 1, bass.ds(T * i, T), :], oh2)
                            link(route, e.tensor_tensor(both, oh1, oh2, ALU.add))
                            link(route, e.tensor_copy(cpre[:, 0, :], member[:, :]))
                            for t in range(1, T):
                                link(route, e.tensor_tensor(cpre[:, t, :], cpre[:, t - 1, :], both[:, t - 1, :], ALU.add))
                            e.tensor_tensor(member[:, :], cpre[:, T - 1, :], both[:, T - 1, :], ALU.add).then_inc(member_ready, 1)

                        def place(i, j, u):
                            L, eq, key, oh1, rest, oh2, both, cpre = (rt[:, k, :, :] for k in range(8))
                            dve.wait_ge(*small.filled(i, "rk"))
                            e.tensor_tensor(eq, SM[small.bank("rk")][:, 0:T * E].rearrange("p (t x) -> p t x", t=T),
                                            over_t(base[:, :]), ALU.add).then_inc(small.free("rk"), 1)
                            dve.wait_ge(*small.read(i, "rk"))
                            for k, oh in ((0, oh1), (1, oh2)):
                                link(route, e.tensor_tensor(key, oh, eq, ALU.mult))
                                link(route, e.tensor_reduce(pos_f[:, :, k], key, AX.X, ALU.add))
                            dve.wait_ge(scattered[u], 16 * 2 * T * j)
                            e.tensor_copy(pos_all[:, bass.ds(T * i, T), :], pos_f[:, :, :])
                            e.tensor_copy(pos[:, u, :, :], pos_f[:, :, :]).then_inc(pos_ready, 1)
                            route.end()

                        def hidden(i, n):
                            p = fs[n]
                            dve.wait_ge(*gates2.read(i, f"g{n}"))
                            dve.wait_ge(hh_ready, FCS * i + max(n - 1, 0))
                            e.tensor_tensor(h_f[0:p, n % 2, :], silu[0:p, n % 2, :], psum[2 + n % 2][0:p, :], ALU.mult).then_inc(h_ready, 1)
                            dve.wait_ge(hh_ready, FCS * i + n + 1)
                            e.tensor_tensor(h_l[0:p, n % 2, :], h_f[0:p, n % 2, :], h_h[0:p, n % 2, :].bitcast(f32),
                                            ALU.subtract).then_inc(hl_ready, 1)

                        with dve.Fori(0, SEQS // 2) as j:
                            for u in range(2):
                                i = 2 * j + u
                                for c in range(C):
                                    name = f"xT{c}"
                                    dve.wait_ge(xh2_ready, C * i + c + 1)
                                    e.tensor_tensor(rT_l[:, c, :], SM[small.bank(name)][:, :], rT_h[:, c, :].bitcast(f32),
                                                    ALU.subtract).then_inc(small.free(name), 1)
                                choose(i)
                                hidden(i, 0)
                                hidden(i, 1)
                                place(i, j, u)
                                for n in range(2, FCS):
                                    hidden(i, n)

                        dve.wait_ge(counted, 1)
                        NB = BLOCKS + 1
                        link(ending, e.tensor_copy(counts[:, :], SM[0][:, 0:E]))
                        link(ending, e.tensor_tensor(base_p[:, 0:E], base_p[:, 0:E], counts[:, :], ALU.add))
                        e.tensor_copy(spare[:, :], base_p[:, :]).then_inc(spare_ready, 1)
                        nb, ca, cb, excl = (cum[:, k, :] for k in range(4))
                        link(ending, e.tensor_scalar(cum_i[:, :], counts[:, :], float(P - 1), None, ALU.add))
                        link(ending, e.tensor_scalar(cum_i[:, :], cum_i[:, :], P.bit_length() - 1, None, ALU.logical_shift_right))
                        link(ending, e.tensor_copy(nb, cum_i[:, :]))
                        src, dst = nb, ca
                        for d in (1, 2, 4):
                            link(ending, e.tensor_copy(dst[:, 0:d], src[:, 0:d]))
                            link(ending, e.tensor_tensor(dst[:, d:E], src[:, d:E], src[:, 0:E - d], ALU.add))
                            src, dst = dst, (cb if dst is ca else ca)
                        incl = src
                        link(ending, e.tensor_tensor(excl, incl, nb, ALU.subtract))
                        link(ending, e.scalar_tensor_tensor(excl, excl, -float(P), base[:, :], ALU.mult, ALU.add))
                        e.tensor_scalar(shift[:, :], excl, -1.0, None, ALU.mult)

                        def per_block(ap):
                            return ap[0:1, :].unsqueeze(1).to_broadcast([1, NB, E])

                        blk, ex, work, row = (grid[:, k, :, :] for k in range(4))
                        eb, ok, rb = (line[:, k, :] for k in range(3))
                        link(ending, e.tensor_tensor(work, blk, per_block(incl), ALU.is_ge))
                        link(ending, e.tensor_reduce(eb, work, AX.X, ALU.add))
                        link(ending, e.tensor_scalar(row, blk, float(P), None, ALU.mult))
                        link(ending, e.tensor_tensor(row, row, per_block(excl), ALU.add))
                        link(ending, e.tensor_tensor(work, ex, eb.unsqueeze(2).to_broadcast([1, NB, E]), ALU.is_equal))
                        link(ending, e.tensor_tensor(work, work, row, ALU.mult))
                        link(ending, e.tensor_reduce(rb, work, AX.X, ALU.add))
                        link(ending, e.tensor_scalar(ok, eb, float(E), None, ALU.is_ge))
                        link(ending, e.scalar_tensor_tensor(rb, ok, float(E * REGION), rb, ALU.mult, ALU.add))
                        link(ending, e.scalar_tensor_tensor(eb, ok, -float(E), eb, ALU.mult, ALU.add))
                        e.tensor_copy(table[:, 0, :], rb)
                        e.tensor_copy(table[:, 1, :], eb).then_inc(table_ready, 1)
                        ending.end()

                    @block.tensor
                    def _(pe):
                        e = nc.tensor

                        def exact(out_, lh, ll, rh, rl, first, last):
                            e.matmul(out_, lh, rh, start=first, stop=False, skip_group_check=True)
                            e.matmul(out_, lh, rl, start=False, stop=False, skip_group_check=True)
                            return e.matmul(out_, ll, rh, start=False, stop=last, skip_group_check=True)

                        def gate_up(i, n):
                            name, p = f"g{n}", fs[n]
                            w = slice(n * P, n * P + p)
                            pe.wait_ge(*gates2.drained(i, name))
                            pe.wait_ge(h_ready, FCS * i + max(n - 1, 0))
                            for k in range(2):
                                for c in range(C):
                                    op = exact(psum[2 * k + n % 2][0:p, :], ws_h[:, c, k, w], ws_l[:, c, k, w],
                                               rT_h[:, c, :], rT_l[:, c, :], c == 0, c == C - 1)
                            op.then_inc(gates2.full(name), 1)

                        def down(i, n):
                            p = fs[n]
                            pe.wait_ge(hl_ready, FCS * i + n + 1)
                            if n == 0:
                                for name in ("y0", "y1"):
                                    pe.wait_ge(*ys.drained(i, name))
                            for t in range(T):
                                half = slice((t % 2) * D, (t % 2 + 1) * D)
                                op = exact(YB[t // 2][:, half], h_h[0:p, n % 2, t * P:(t + 1) * P], h_l[0:p, n % 2, t * P:(t + 1) * P],
                                           wsd_h[0:p, n, :], wsd_l[0:p, n, :], n == 0 and t % 2 == 0, n == FCS - 1)
                            op.then_inc(h_used, 1)

                        pe.wait_ge(stored, 32 * SEQS)
                        pe.wait_ge(router_split, 1)
                        pe.wait_ge(stage_split, SHARED)
                        with pe.Fori(0, SEQS // 2) as j:
                            for u in range(2):
                                i = 2 * j + u
                                pe.wait_ge(row_loaded[u], 16 * (j + 1))
                                for c in range(C):
                                    name = f"xT{c}"
                                    pe.wait_ge(*small.drained(i, name))
                                    for t in range(T):
                                        op = e.matmul(SM[small.bank(name)][:, t * P:(t + 1) * P], rows[:, u, t, c * P:(c + 1) * P], ident[:, :],
                                                      start=True, stop=True, is_transpose=True)
                                    op.then_inc(small.full(name), 1)
                                for c in range(C):
                                    pe.wait_ge(*small.read(i, f"xT{c}"))
                                pe.wait_ge(*small.drained(i, "lg"))
                                for t in range(T):
                                    for c in range(C):
                                        op = exact(SM[small.bank("lg")][:, t * E:(t + 1) * E], rT_h[:, c, t * P:(t + 1) * P],
                                                   rT_l[:, c, t * P:(t + 1) * P], wr_h[:, c, :], wr_l[:, c, :], c == 0, c == C - 1)
                                op.then_inc(small.full("lg"), 1)
                                gate_up(i, 0)
                                gate_up(i, 1)
                                pe.wait_ge(member_ready, i + 1)
                                pe.wait_ge(*small.drained(i, "rk"))
                                out_ = SM[small.bank("rk")][:, 0:T * E]
                                e.matmul(out_, before[:, :], rt[:, 6, :, :].rearrange("p t x -> p (t x)"), start=True, stop=False)
                                e.matmul(out_, all_ones[:, :], rt[:, 7, :, :].rearrange("p t x -> p (t x)"), start=False, stop=True
                                         ).then_inc(small.full("rk"), 1)
                                for n in range(FCS):
                                    if n + 2 < FCS:
                                        gate_up(i, n + 2)
                                    down(i, n)
                        pe.wait_ge(*small.read(SEQS - 1, "lg"))
                        e.matmul(SM[0][:, 0:E], all_ones[:, :], member[:, :], start=True, stop=True).then_inc(counted, 1)

            NBLK = BLOCKS + 1
            assert NBLK % 2 == 0
            down_in, down_high, down_low = sem("down_in"), sem("down_high"), sem("down_low")
            blk_loaded = [sem(f"blk_loaded{n}") for n in range(4)]
            blk_stored = [sem("blk_stored0"), sem("blk_stored1")]
            bx_full, bx_high, bx_low = sem("bx_full"), sem("bx_high"), sem("bx_low")
            bg_full, bg_silu, bh_ready = sem("bg_full"), sem("bg_silu"), sem("bh_ready")
            bt_full, bt_high, bt_low = sem("bt_full"), sem("bt_high"), sem("bt_low")
            by_full, by_read = sem("by_full"), sem("by_read")
            experts = ExitStack()
            with experts:
                def sb(name, shape, dt=f32):
                    return experts.enter_context(nc.sbuf_tensor(name, shape, dt))

                wd_f = sb("wd_f", [P, FCE, E, D])
                wd_h = sb("wd_h", [P, FCE, E, D], f32r)
                wd_l = sb("wd_l", [P, FCE, E, D], f32r)
                bx = sb("bx", [P, 4, D])
                bxT_h = sb("bxT_h", [P, 2, C, P], f32r)
                bxT_l = sb("bxT_l", [P, 2, C, P], f32r)
                b_silu = sb("b_silu", [P, 2, F])
                b_h = sb("b_h", [P, 2, F])
                bhT_h = sb("bhT_h", [P, 2, FCE, P], f32r)
                bhT_l = sb("bhT_l", [P, 2, FCE, P], f32r)
                b_y = sb("b_y", [P, 2, D])
                FULL = F // P
                REST = F - FULL * P

                def second_part_over(eng):
                    eng.wait_ge(ys_stored, 16 * SEQS)
                    eng.wait_ge(spare_zeroed, 16 * (E + 1))
                    eng.wait_ge(table_ready, 1)

                with nc.Block() as block:

                    @block.sync
                    def _(sp):
                        second_part_over(sp)

                        def load(b, n):
                            row = sp.value_load(table[0:1, 0, bass.ds(b, 1)], min_val=0, max_val=E * REGION)
                            sp.dma_start(bx[:, n, :], xg_dram[bass.ds(row, P), :]).then_inc(blk_loaded[n], 16)

                        def store(b, n):
                            sp.wait_ge(by_read, b + 1)
                            sp.dma_start(yg_dram[bass.ds(b * P, P), :], b_y[:, n, :]).then_inc(blk_stored[n], 16)

                        for b in range(2):
                            load(b, b)
                        for n in range(FCE):
                            sp.dma_start(wd_f[0:fe[n], n, :, :], w_down[:, n * P:n * P + fe[n], :].rearrange("e p d -> p e d")
                                         ).then_inc(down_in, 16)
                        for b in range(2, 4):
                            load(b, b)
                        with sp.Fori(0, NBLK // 4 - 1) as j:
                            for n in range(4):
                                store(4 * j + n, n % 2)
                                sp.wait_ge(bx_full, 4 * j + n + 1)
                                load(4 * j + n + 4, n)
                        for b in range(NBLK - 4, NBLK):
                            store(b, b % 2)
                        for n in range(2):
                            sp.wait_ge(blk_stored[n], 16 * (NBLK // 2))

                    @block.scalar
                    def _(act):
                        e = nc.scalar
                        second_part_over(act)

                        def rows_high(b, u):
                            act.wait_ge(bx_full, b + 1)
                            e.activation(bxT_h[:, u, :, :].rearrange("p c n -> p (c n)"), psum[6 + u][:, 0:D], ACT.Copy).then_inc(bx_high, 1)

                        def gate(b, u):
                            act.wait_ge(bg_full, b + 1)
                            e.activation(b_silu[:, u, :], psum[u][:, 0:F], ACT.Silu).then_inc(bg_silu, 1)

                        def hidden_high(b, u):
                            act.wait_ge(bt_full, b + 1)
                            e.activation(bhT_h[:, u, 0:FULL, :].rearrange("p n k -> p (n k)"), psum[4][:, 0:FULL * P], ACT.Copy)
                            e.activation(bhT_h[0:REST, u, FULL, :], psum[4][0:REST, FULL * P:(FULL + 1) * P], ACT.Copy).then_inc(bt_high, 1)

                        def result(b, u, j):
                            act.wait_ge(by_full, b + 1)
                            act.wait_ge(blk_stored[u], 16 * j)
                            e.activation(b_y[:, u, :], psum[5][:, 0:D], ACT.Copy).then_inc(by_read, 1)

                        rows_high(0, 0)
                        rows_high(1, 1)
                        act.wait_ge(down_in, 16 * FCE)
                        for n in range(FCE):
                            e.activation(wd_h[0:fe[n], n, :, :], wd_f[0:fe[n], n, :, :], ACT.Copy).then_inc(down_high, 1)
                        gate(0, 0)
                        with act.Fori(0, NBLK // 2 - 1) as j:
                            for u in range(2):
                                b = 2 * j + u + 1
                                hidden_high(b - 1, u)
                                gate(b, 1 - u)
                                rows_high(b + 1, u)
                                result(b - 1, u, j)
                        hidden_high(NBLK - 2, 0)
                        gate(NBLK - 1, 1)
                        result(NBLK - 2, 0, NBLK // 2 - 1)
                        hidden_high(NBLK - 1, 1)
                        result(NBLK - 1, 1, NBLK // 2 - 1)

                    @block.vector
                    def _(dve):
                        e = nc.vector
                        second_part_over(dve)

                        def rows_low(b, u):
                            dve.wait_ge(bx_high, b + 1)
                            e.tensor_tensor(bxT_l[:, u, :, :].rearrange("p c n -> p (c n)"), psum[6 + u][:, 0:D],
                                            bxT_h[:, u, :, :].rearrange("p c n -> p (c n)").bitcast(f32), ALU.subtract).then_inc(bx_low, 1)

                        def hidden(b, u):
                            dve.wait_ge(bg_silu, b + 1)
                            e.tensor_tensor(b_h[:, u, :], b_silu[:, u, :], psum[2 + u][:, 0:F], ALU.mult).then_inc(bh_ready, 1)

                        def hidden_low(b, u):
                            dve.wait_ge(bt_high, b + 1)
                            e.tensor_tensor(bhT_l[:, u, 0:FULL, :].rearrange("p n k -> p (n k)"), psum[4][:, 0:FULL * P],
                                            bhT_h[:, u, 0:FULL, :].rearrange("p n k -> p (n k)").bitcast(f32), ALU.subtract)
                            e.tensor_tensor(bhT_l[0:REST, u, FULL, :], psum[4][0:REST, FULL * P:(FULL + 1) * P],
                                            bhT_h[0:REST, u, FULL, :].bitcast(f32), ALU.subtract).then_inc(bt_low, 1)

                        rows_low(0, 0)
                        rows_low(1, 1)
                        for n in range(FCE):
                            dve.wait_ge(down_high, n + 1)
                            e.tensor_tensor(wd_l[0:fe[n], n, :, :], wd_f[0:fe[n], n, :, :], wd_h[0:fe[n], n, :, :].bitcast(f32),
                                            ALU.subtract).then_inc(down_low, 1)
                        hidden(0, 0)
                        with dve.Fori(0, NBLK // 2 - 1) as j:
                            for u in range(2):
                                b = 2 * j + u + 1
                                hidden_low(b - 1, u)
                                hidden(b, 1 - u)
                                rows_low(b + 1, u)
                        hidden_low(NBLK - 2, 0)
                        hidden(NBLK - 1, 1)
                        hidden_low(NBLK - 1, 1)

                    @block.tensor
                    def _(pe):
                        e = nc.tensor
                        second_part_over(pe)

                        def expert_of(b):
                            return pe.value_load(table[0:1, 1, bass.ds(b, 1)], min_val=0, max_val=E - 1)

                        def turn_rows(b, u, n, j):
                            pe.wait_ge(blk_loaded[n], 16 * (j + 1))
                            pe.wait_ge(bx_low, max(b - 1, 0) if isinstance(b, int) else b - 1)
                            for c in range(C):
                                op = e.matmul(psum[6 + u][:, c * P:(c + 1) * P], bx[:, n, c * P:(c + 1) * P], ident[:, :],
                                              start=True, stop=True, is_transpose=True)
                            op.then_inc(bx_full, 1)

                        def gate_up(b, u):
                            x_ = expert_of(b)
                            pe.wait_ge(bx_low, b + 1)
                            pe.wait_ge(bh_ready, max(b - 1, 0) if isinstance(b, int) else b - 1)
                            for c in range(C):
                                for k in range(2):
                                    wh, wl = (w[:, bass.ds(x_ * C + c, 1), k, :].rearrange("p a f -> p (a f)") for w in (wgu_h, wgu_l))
                                    out_, xh, xl = psum[2 * k + u][:, 0:F], bxT_h[:, u, c, :], bxT_l[:, u, c, :]
                                    e.matmul(out_, xh, wh, start=(c == 0), stop=False)
                                    e.matmul(out_, xh, wl, start=False, stop=False)
                                    op = e.matmul(out_, xl, wh, start=False, stop=(c == C - 1))
                            op.then_inc(bg_full, 1)

                        def turn_hidden(b, u):
                            pe.wait_ge(bh_ready, b + 1)
                            pe.wait_ge(bt_low, b)
                            for n in range(FCE):
                                op = e.matmul(psum[4][0:fe[n], n * P:(n + 1) * P], b_h[:, u, n * P:n * P + fe[n]], ident[:, :],
                                              start=True, stop=True, is_transpose=True)
                            op.then_inc(bt_full, 1)

                        def down(b, u):
                            x_ = expert_of(b)
                            pe.wait_ge(bt_low, b + 1)
                            pe.wait_ge(by_read, b)
                            for n in range(FCE):
                                wh, wl = (w[0:fe[n], n, bass.ds(x_, 1), :].rearrange("p a d -> p (a d)") for w in (wd_h, wd_l))
                                out_, hh, hl = psum[5][:, 0:D], bhT_h[0:fe[n], u, n, :], bhT_l[0:fe[n], u, n, :]
                                e.matmul(out_, hh, wh, start=(n == 0), stop=False)
                                e.matmul(out_, hh, wl, start=False, stop=False)
                                op = e.matmul(out_, hl, wh, start=False, stop=(n == FCE - 1))
                            op.then_inc(by_full, 1)

                        turn_rows(0, 0, 0, 0)
                        turn_rows(1, 1, 1, 0)
                        gate_up(0, 0)
                        pe.wait_ge(down_low, FCE)
                        with pe.Fori(0, NBLK // 4 - 1) as j:
                            for m in range(4):
                                b = 4 * j + m + 1
                                turn_hidden(b - 1, m % 2)
                                gate_up(b, (m + 1) % 2)
                                turn_rows(b + 1, m % 2, (m + 2) % 4, j + (m + 2) // 4)
                                down(b - 1, m % 2)
                        for b in range(NBLK - 3, NBLK):
                            turn_hidden(b - 1, (b - 1) % 2)
                            gate_up(b, b % 2)
                            if b + 1 < NBLK:
                                turn_rows(b + 1, (b + 1) % 2, (b + 1) % 4, (b + 1) // 4)
                            down(b - 1, (b - 1) % 2)
                        turn_hidden(NBLK - 1, 1)
                        down(NBLK - 1, 1)

            fin_loaded = [sem("fin_loaded0"), sem("fin_loaded1")]
            gathered = [sem("gathered0"), sem("gathered1")]
            index_ready, weights_ready, exp_ready, logits_ready = (
                sem("index_ready"), sem("weights_ready"), sem("exp_ready"), sem("logits_ready"))
            out_ready, out_stored, step_weight, step_last = (
                sem("out_ready"), [sem("out_stored0"), sem("out_stored1")], sem("step_weight"), sem("step_last"))
            last = ExitStack()
            with last:
                def sb(name, shape, dt=f32):
                    return last.enter_context(nc.sbuf_tensor(name, shape, dt))

                f_x1 = sb("f_x1", [P, 2, T, D])
                f_ys = sb("f_ys", [P, 2, T, D])
                f_y = sb("f_y", [P, 2, 2, T, D])
                f_out = sb("f_out", [P, 2, T, D])
                index = sb("index", [P, 2, T, 2], i32)
                index_all = sb("index_all", [P, TILES, 2], i32)
                moved = sb("moved", [P, TILES])
                weight = sb("weight", [P, 2, TILES])
                w_now = sb("w_now", [P, 2, T])
                probs = sb("probs", [P, TILES, E])
                picked = sb("picked", [P, TILES, E])
                z_sum = sb("z_sum", [P, 4, TILES])
                f_stats = sb("f_stats", [P, T, 6])
                f_mv = sb("f_mv", [P, T, 2])
                f_rstd = sb("f_rstd", [P, 3, T])

                def third_part_over(eng):
                    for n in range(2):
                        eng.wait_ge(blk_stored[n], 16 * (NBLK // 2))

                with nc.Block() as block:

                    @block.sync
                    def _(sp):
                        third_part_over(sp)

                        def load(j, u):
                            i = 2 * j + u
                            for src, dst in ((x1_dram, f_x1), (ys_dram, f_ys)):
                                sp.dma_start(dst[:, u, :, :], src[bass.ds(i, 1)].rearrange("a (t p) d -> p (a t) d", p=P)).then_inc(fin_loaded[u], 16)

                        def store(j, u):
                            i = 2 * j + u
                            sp.wait_ge(out_ready, i + 1)
                            sp.dma_start(out[bass.ds(i, 1)].rearrange("a (t p) d -> p (a t) d", p=P), f_out[:, u, :, :]).then_inc(out_stored[u], 16)

                        load(0, 0)
                        load(0, 1)
                        with sp.Fori(0, SEQS // 2 - 1) as j:
                            for u in range(2):
                                store(j, u)
                                load(j + 1, u)
                        for u in range(2):
                            store(SEQS // 2 - 1, u)
                        for u in range(2):
                            sp.wait_ge(out_stored[u], 16 * (SEQS // 2))

                    @block.gpsimd
                    def _(gp):
                        e = nc.gpsimd
                        third_part_over(gp)
                        with gp.Fori(0, SEQS // 2) as j:
                            for u in range(2):
                                value = gp.to_reg(2 * j + u + 1)
                                gp.wait_ge(blk_stored[0], 16)
                                gp.wait_ge(index_ready, value)
                                for t in range(T):
                                    for k in range(2):
                                        e.indirect_dma_start(out=f_y[:, u, k, t, :], out_offset=None, in_=yg_dram,
                                                             in_offset=bass.IndirectOffsetOnAxis(ap=index[:, u, t, k:k + 1], axis=0)
                                                             ).then_inc(gathered[u], 16)

                    @block.scalar
                    def _(act):
                        third_part_over(act)
                        nc.scalar.activation(probs[:, :, :], lg_all[:, :, :], ACT.Exp).then_inc(exp_ready, 1)

                    @block.vector
                    def _(dve):
                        e = nc.vector
                        prepare, steps = Steps(step_weight, WEIGHT_STEPS), Steps(step_last, LAST_STEPS)

                        def wait_alone(s, value):
                            value = value if isinstance(value, int) else dve.to_reg(value)
                            dve.wait_ge(ys_stored, 16)
                            dve.wait_ge(s, value)

                        def link(steps, op, alone=False):
                            s, value = steps.next()
                            op.then_inc(s, 1)
                            (wait_alone if alone else dve.wait_ge)(s, value)

                        def indices(i, j, u):
                            if not (isinstance(j, int) and j == 0):
                                dve.wait_ge(gathered[u], 16 * 2 * T * j)
                            e.tensor_copy(index[:, u, :, :], index_all[:, bass.ds(T * i, T), :]).then_inc(index_ready, 1)

                        third_part_over(dve)
                        prepare.begin(0)
                        for k in range(2):
                            link(prepare, e.tensor_tensor(picked[:, :, :], oh_all[:, k, :, :],
                                                          shift[:, :].unsqueeze(1).to_broadcast([P, TILES, E]), ALU.mult))
                            link(prepare, e.tensor_reduce(moved[:, :], picked[:, :, :], AX.X, ALU.add))
                            link(prepare, e.tensor_tensor(index_all[:, :, k], pos_all[:, :, k], moved[:, :], ALU.add))
                        indices(0, 0, 0)
                        indices(1, 0, 1)
                        dve.wait_ge(exp_ready, 1)
                        z, p1, p2, s_ = (z_sum[:, k, :] for k in range(4))
                        link(prepare, e.tensor_reduce(z, probs[:, :, :], AX.X, ALU.add))
                        link(prepare, e.reciprocal(s_, z))
                        for k, p_ in ((0, p1), (1, p2)):
                            link(prepare, e.tensor_tensor(picked[:, :, :], probs[:, :, :], oh_all[:, k, :, :], ALU.mult))
                            link(prepare, e.tensor_reduce(p_, picked[:, :, :], AX.X, ALU.add))
                            link(prepare, e.tensor_tensor(p_, p_, s_, ALU.mult))
                        link(prepare, e.scalar_tensor_tensor(z, p1, TOP_EPS, p2, ALU.add, ALU.add))
                        link(prepare, e.reciprocal(s_, z))
                        for k, p_ in ((0, p1), (1, p2)):
                            link(prepare, e.scalar_tensor_tensor(weight[:, k, :], p_, TOP_SCALE, s_, ALU.mult, ALU.mult))
                        prepare.end()

                        def sequence(i, j, u):
                            steps.begin(i)
                            dve.wait_ge(fin_loaded[u], 32 * (j + 1))
                            link(steps, e.tensor_copy(w_now[:, :, :], weight[:, :, bass.ds(T * i, T)]))
                            dve.wait_ge(gathered[u], 16 * 2 * T * (j + 1))
                            acc = f_ys[:, u, :, :]
                            for k in range(2):
                                for t in range(T):
                                    op = e.scalar_tensor_tensor(acc[:, t, :], f_y[:, u, k, t, :], w_now[:, k, t:t + 1], acc[:, t, :],
                                                                ALU.mult, ALU.add)
                                link(steps, op)
                            for t in range(T):
                                op = e.bn_stats(f_stats[:, t, :], acc[:, t, :])
                            link(steps, op, alone=True)
                            for t in range(T):
                                op = e.bn_aggr(f_mv[:, t, :], f_stats[:, t, :])
                            link(steps, op)
                            y, v, w = (f_rstd[:, k, :] for k in range(3))
                            link(steps, e.tensor_scalar(v, f_mv[:, :, 1], EPS, None, ALU.add))
                            link(steps, e.tensor_scalar(w.bitcast(i32), v.bitcast(i32), 1, None, ALU.logical_shift_right))
                            link(steps, e.tensor_scalar(y.bitcast(i32), w.bitcast(i32), -1, RSQRT_SEED, ALU.mult, ALU.add))
                            for _ in range(3):
                                link(steps, e.tensor_tensor(w, y, y, ALU.mult))
                                link(steps, e.scalar_tensor_tensor(w, w, -0.5, v, ALU.mult, ALU.mult))
                                link(steps, e.scalar_tensor_tensor(y, w, 1.5, y, ALU.add, ALU.mult))
                            for t in range(T):
                                op = e.tensor_scalar(acc[:, t, :], acc[:, t, :], f_mv[:, t, 0:1], y[:, t:t + 1], ALU.subtract, ALU.mult)
                            link(steps, op)
                            dve.wait_ge(out_stored[u], 16 * j)
                            for t in range(T):
                                op = e.tensor_tensor(f_out[:, u, t, :], acc[:, t, :], f_x1[:, u, t, :], ALU.add)
                            op.then_inc(out_ready, 1)
                            steps.end()

                        with dve.Fori(0, SEQS // 2 - 1) as j:
                            for u in range(2):
                                sequence(2 * j + u, j, u)
                                indices(2 * j + u + 2, j + 1, u)
                        for u in range(2):
                            sequence(SEQS - 2 + u, SEQS // 2 - 1, u)


_INS = ["L0_attn_x", "L0_attn_qkv_w", "L0_attn_qkv_b", "L0_attn_rq_w", "L0_attn_rq_b", "L0_attn_rkv_w", "L0_attn_rkv_b",
        "L0_attn_rout_w", "L0_attn_rout_b", "L0_attn_out_w", "L0_attn_out_b", "L0_attn_gl_w", "L0_attn_gr_w",
        "L0_ffn_gate_w", "L0_ffn_w_gate", "L0_ffn_w_up", "L0_ffn_w_down", "L0_ffn_sw_gate", "L0_ffn_sw_up", "L0_ffn_sw_down"]
_OUTS = [((16, 512, 256), "float32")]


def kernel(**inputs):
    import numpy as _np
    import concourse.bacc as _bacc
    from concourse import mybir as _mybir
    from concourse.bass_utils import run_bass_kernel_spmd as _run

    nc = _bacc.Bacc("TRN2", target_bir_lowering=False, num_devices=1)
    arrays, args = {}, []
    for name in _INS:
        a = _np.ascontiguousarray(inputs[name])
        arrays[f"in_{name}_dram"] = a
        args.append(nc.dram_tensor(f"in_{name}_dram", a.shape, _mybir.dt.from_np(a.dtype), kind="ExternalInput").ap())
    for i, (shape, dtype) in enumerate(_OUTS):
        dt = _mybir.dt.from_np(_np.dtype(dtype))
        args.append(nc.dram_tensor(f"out_{i}_dram", shape, dt, kind="ExternalOutput").ap())
    sandwich_kernel(nc, *args)
    r = _run(nc, [arrays], core_ids=[0])
    return r.results[0]["out_0_dram"]
```

```python
import concourse.bass as bass
from concourse import mybir
from contextlib import ExitStack


class Steps:

    def __init__(self, sem, per, before=0):
        self.sem, self.per, self.before, self.at, self.done = sem, per, before, 0, None

    def begin(self, seq):
        self.seq, self.at = seq, 0

    def next(self):
        self.at += 1
        return self.sem, self.before + self.seq * self.per + self.at

    def end(self):
        assert self.at == self.per, (self.at, self.per)


class Banks:

    def __init__(self, uses, full, free):
        self.where = {name: (b, k) for b, names in enumerate(uses) for k, name in enumerate(names)}
        self.per = [len(names) for names in uses]
        self.fulls, self.frees = full, free

    def bank(self, name):
        return self.where[name][0]

    def full(self, name):
        return self.fulls[self.bank(name)]

    def free(self, name):
        return self.frees[self.bank(name)]

    def drained(self, seq, name):
        b, k = self.where[name]
        return self.frees[b], seq * self.per[b] + k

    def read(self, seq, name):
        b, k = self.where[name]
        return self.frees[b], seq * self.per[b] + k + 1

    def all_filled(self, seq, name):
        b = self.bank(name)
        return self.fulls[b], seq * self.per[b]

    def filled(self, seq, name):
        b, k = self.where[name]
        return self.fulls[b], seq * self.per[b] + k + 1


def sandwich_kernel(nc, x, qkv_w, qkv_b, rq_w, rq_b, rkv_w, rkv_b, rout_w, rout_b, out_w, out_b, gl_w, gr_w,
                    gate_w, w_gate, w_up, w_down, sw_gate, sw_up, sw_down, out):
    f32, f32r, i32 = mybir.dt.float32, mybir.dt.float32r, mybir.dt.int32
    ALU, ACT, AX = mybir.AluOpType, mybir.ActivationFunctionType, mybir.AxisListType

    P = 128
    SEQS, S, D = x.shape
    T = S // P
    C = D // P
    HEADS, HD = 16, D // 16
    G, HG = 4, 4
    PAD = P // HG
    WIN = 2 * P
    LAT, LH = 64, 4
    LC = S // LAT
    DA = D + HEADS
    E, F = w_gate.shape[0], w_gate.shape[2]
    FS = sw_gate.shape[1]
    SCALE = HD ** -0.5
    AHEAD = 5
    EPS, NEG, TINY = 1e-5, -1e30, 1e-30
    RSQRT_SEED = 0x5F3759DF
    SETUP_STEPS, NORM_STEPS, LATENT_STEPS, TAIL_STEPS, RESIDUAL_STEPS = 12, 14, 5, 25, 28
    ROUTE_STEPS, END_STEPS, WEIGHT_STEPS, LAST_STEPS = 20, 26, 18, 19

    x1_dram = nc.dram_tensor("x1_scratch", (SEQS, S, D), f32, kind="Internal").ap()
    xn2_dram = nc.dram_tensor("xn2_scratch", (SEQS, S, D), f32, kind="Internal").ap()

    with ExitStack() as ctx:
        def sem(name):
            return ctx.enter_context(nc.semaphore(name))

        psum = [ctx.enter_context(nc.psum_tensor(f"bank{b}", [P, 512], f32)) for b in range(8)]
        ident = ctx.enter_context(nc.sbuf_tensor("ident", [P, P], f32))

        attention = ExitStack()
        with attention:
            def sb(name, shape, dt=f32):
                return attention.enter_context(nc.sbuf_tensor(name, shape, dt))

            wqk_h = sb("wqk_h", [P, 2, C, G * P], f32r)
            wqk_l = sb("wqk_l", [P, 2, C, G * P], f32r)
            wv_h = sb("wv_h", [P, C, DA], f32r)
            wv_l = sb("wv_l", [P, C, DA], f32r)
            wrq_h = sb("wrq_h", [P, C, P], f32r)
            wrq_l = sb("wrq_l", [P, C, P], f32r)
            wrk = sb("wrk", [P, C, P])
            wrv = sb("wrv", [P, C, LAT])
            wout_h = sb("wout_h", [P, C, D], f32r)
            wout_l = sb("wout_l", [P, C, D], f32r)
            wrout = sb("wrout", [P, DA])
            bqk = sb("bqk", [P, 2, G])
            bv = sb("bv", [P, DA])
            brq = sb("brq", [P, 1])
            brk = sb("brk", [P, 1])
            brv = sb("brv", [P, LAT])
            bout = sb("bout", [P, D])
            gl = sb("gl", [P, HD])
            gr = sb("gr", [P, HD])
            ones = sb("ones", [1, S])
            mask_window = sb("mask_window", [P, WIN])
            mask_first = sb("mask_first", [P, P])
            lat_add = sb("lat_add", [P, T, LAT])
            rk_mask = sb("rk_mask", [P, LH, LAT])
            rv_mask = sb("rv_mask", [P, 2, LAT])

            x_in = sb("x_in", [P, T, D])
            x_res = sb("x_res", [P, T, D])
            xn = sb("xn", [P, T, D])
            xT_h = sb("xT_h", [P, C, S], f32r)
            xT_l = sb("xT_l", [P, C, S], f32r)
            kT_h = sb("kT_h", [P, 2, S], f32r)
            kT_l = sb("kT_l", [P, 2, S], f32r)
            kD_h = sb("kD_h", [P, G, HG, S], f32r)
            kD_l = sb("kD_l", [P, G, HG, S], f32r)
            qT_h = sb("qT_h", [P, G, S], f32r)
            qT_l = sb("qT_l", [P, G, S], f32r)
            v_sb = sb("v_sb", [P, T, HEADS, PAD])
            row_max = sb("row_max", [P, G, T, HG])
            maxT = sb("maxT", [HG, G, S], f32r)
            prob = sb("prob", [P, 4, 2, WIN])
            pvT = sb("pvT", [P, G, S])
            pool = sb("pool", [P, C, LAT])
            pool2 = sb("pool2", [P, C, 2, LAT])
            rqT = sb("rqT", [P, S])
            rk_t = sb("rk_t", [P, LAT])
            rkD = sb("rkD", [P, LH, LAT])
            rv_t = sb("rv_t", [P, LAT])
            rvD = sb("rvD", [P, 2, LAT])
            lat = sb("lat", [P, T, LH, LAT])
            lat_s = sb("lat_s", [P, 3, T, LH])
            latpT = sb("latpT", [P, 2, S])
            latT = sb("latT", [P, S])
            mixed = sb("mixed", [P, 2, D])
            gate_s = sb("gate_s", [P, 2, 6, HEADS])
            mixT_h = sb("mixT_h", [P, 2, C, P], f32r)
            mixT_l = sb("mixT_l", [P, 2, C, P], f32r)
            att = sb("att", [P, T, D])
            stats = sb("stats", [P, 3, T, 6])
            mv = sb("mv", [P, 3, T, 2])
            rstd = sb("rstd", [P, 3, 3, T])
            wqk_f = pvT[:, :, :].rearrange("p g s -> p (g s)").rearrange("p (j c n) -> p j c n", j=2, c=C)
            x_res_flat = x_res[:, :, :].rearrange("p t d -> p (t d)")
            wv_f = x_res_flat[:, 0:C * DA].rearrange("p (c n) -> p c n", c=C)
            wrq_f = x_res_flat[:, C * DA:C * (DA + P)].rearrange("p (c n) -> p c n", c=C)
            wout_f = att[:, 0:C, :]
            wtmp = x_in[:, 0, :]

            keys_zeroed = sem("keys_zeroed")
            zeroed, consts, weights_in, split = sem("zeroed"), sem("consts"), sem("weights_in"), sem("split")
            x_loaded, xres_loaded, xn_ready = sem("x_loaded"), sem("xres_loaded"), sem("xn_ready")
            xTh_ready, kh_ready, qh_ready = sem("xTh_ready"), sem("kh_ready"), sem("qh_ready")
            k_spread = [sem(f"k_spread{g}") for g in range(G)]
            max_placed = [sem(f"max_placed{g}") for g in range(G)]
            prob_ready, prob_used, pv_read = sem("prob_ready"), sem("prob_used"), sem("pv_read")
            pool_ready, rv_ready = sem("pool_ready"), sem("rv_ready")
            lat_max, lat_exp, lat_ready = sem("lat_max"), sem("lat_exp"), sem("lat_ready")
            exp_written = sem("exp_written")
            z_ready, sig_exp, mixTh_ready = sem("z_ready"), sem("sig_exp"), sem("mixTh_ready")
            x1_ready, xn2_ready, stored = sem("x1_ready"), sem("xn2_ready"), sem("stored")
            step_setup, step_front, step_mid, step_tail, step_residual = (
                sem("step_setup"), sem("step_front"), sem("step_mid"), sem("step_tail"), sem("step_residual"))

            order = (["xT0", "xT1", "k0", "q0", "k1", "q1", "k2", "q2", "k3", "q3", "v0", "v1", "v2", "v3",
                      "rq", "rk", "rv", "m0", "ls0", "ls1", "m1", "m2", "m3", "lT0", "lT1", "lo"])
            front = Banks([order[0::2], order[1::2]], [sem("front_full0"), sem("front_full1")],
                          [sem("front_free0"), sem("front_free1")])
            FB = [psum[6], psum[7]]
            smax = [f"M{g}{b}{h}" for g in range(G) for b in range(T) for h in range(2)]
            tail_s = ["pv0", "pv1", "mix0", "pv2", "mix1", "pv3", "mix2", "mix3"]
            scores = Banks([(smax + tail_s)[0::2], (smax + tail_s)[1::2]], [sem("score_full0"), sem("score_full1")],
                           [sem("score_free0"), sem("score_free1")])
            SB = [psum[0], psum[1]]
            strans = [f"T{g}{b}{h}" for g in range(G) for b in range(T) for h in range(2)]
            tail_t = ["rem0", "rem1", "rem2", "rem3"]
            keyed = Banks([(strans + tail_t)[0::2], (strans + tail_t)[1::2]], [sem("keyed_full0"), sem("keyed_full1")],
                          [sem("keyed_free0"), sem("keyed_free1")])
            KB = [psum[2], psum[3]]
            PV = [psum[4], psum[5]]
            outs = Banks([["out0", "out2"], ["out1", "out3"]], [sem("out_full0"), sem("out_full1")],
                         [sem("out_free0"), sem("out_free1")])

            loads = []
            for j in range(2):
                for c in range(C):
                    loads.append((wqk_f[:, j, c, :].rearrange("p (n w) -> p n w", w=PAD)[:, :, 0:HD],
                                  qkv_w[c * P:(c + 1) * P, j * D:(j + 1) * D].rearrange("p (n d) -> p n d", d=HD)))
                for h in range(HG):
                    loads.append((bqk[h * PAD:h * PAD + HD, j, :],
                                  qkv_b[j * D:(j + 1) * D].rearrange("(g h d) -> h d g", g=G, d=HD)[h, :, :]))
            for c in range(C):
                rows = slice(c * P, (c + 1) * P)
                loads.append((wv_f[:, c, 0:D], qkv_w[rows, 2 * D:3 * D]))
                loads.append((wout_f[:, c, :], out_w[rows, :]))
                loads.append((wrq_f[:, c, 0:LAT], rq_w[rows, :]))
                loads.append((wrk[:, c, 0:LAT], rkv_w[rows, 0:LAT]))
                loads.append((wrv[:, c, :], rkv_w[rows, LAT:2 * LAT]))
            loads.append((wrout[0:LAT, 0:D], rout_w))
            loads.append((wrout[LAT:LAT + 1, 0:D], rout_b.rearrange("(a n) -> a n", a=1)))
            loads.append((bv[:, 0:D], qkv_b[2 * D:3 * D].partition_broadcast(P)))
            loads.append((bout[:, :], out_b.partition_broadcast(P)))
            loads.append((gl[:, :], gl_w.rearrange("d a -> (d a)").partition_broadcast(P)))
            loads.append((gr[:, :], gr_w.rearrange("d a -> (d a)").partition_broadcast(P)))
            loads.append((brv[:, :], rkv_b[LAT:2 * LAT].partition_broadcast(P)))
            loads.append((brq[0:LAT, :], rq_b.rearrange("(n a) -> n a", a=1)))
            loads.append((brk[0:LAT, :], rkv_b[0:LAT].rearrange("(n a) -> n a", a=1)))
            for h in range(HG):
                loads.append((kD_h[h * PAD + HD:h * PAD + HD + 1, :, h, :].bitcast(f32), ones[:, :].unsqueeze(1).to_broadcast([1, G, S])))

            with nc.Block() as block:

                @block.sync
                def _(sp):
                    sp.wait_ge(zeroed, 1)
                    with nc.allow_non_contiguous_dma(reason="128 biases, once"):
                        for n, (dst, src) in enumerate(loads):
                            if n == len(loads) - HG:
                                sp.wait_ge(keys_zeroed, 2)
                            sp.dma_start(dst, src).then_inc(weights_in, 16)

                    sp.wait_ge(split, 1)

                    def front_loads(i):
                        sp.wait_ge(xn_ready, i)
                        sp.dma_start(x_in[:, :, :], x[i].rearrange("(t p) d -> p t d", p=P)).then_inc(x_loaded, 16)

                    def spread_k(i):
                        sp.wait_ge(prob_used, 2 * T * G * i)
                        for g in range(G):
                            for ready, src, dst in (((kh_ready, G * i + g + 1), kT_h, kD_h),
                                                    (front.read(i, f"k{g}"), kT_l, kD_l)):
                                sp.wait_ge(*ready)
                                for h in range(HG):
                                    r = slice(h * PAD, h * PAD + HD)
                                    sp.dma_start(dst[r, g, h, :].bitcast(f32), src[r, g % 2, :].bitcast(f32)).then_inc(k_spread[g], 16)

                    def place_max(i):
                        for g in range(G):
                            sp.wait_ge(*front.read(i, f"m{g}"))
                            sp.dma_start(qT_h[HD:P:PAD, g, :].bitcast(f32), maxT[:, g, :].bitcast(f32)).then_inc(max_placed[g], 16)

                    def stores(i):
                        sp.wait_ge(x1_ready, i + 1)
                        sp.dma_start(x1_dram[i].rearrange("(t p) d -> p t d", p=P), x_res[:, :, :]).then_inc(stored, 16)
                        sp.wait_ge(xn2_ready, i + 1)
                        sp.dma_start(xn2_dram[i].rearrange("(t p) d -> p t d", p=P), att[:, :, :]).then_inc(stored, 16)

                    def load_residual(i):
                        sp.wait_ge(stored, 32 * i)
                        sp.dma_start(x_res[:, :, :], x[i].rearrange("(t p) d -> p t d", p=P)).then_inc(xres_loaded, 16)

                    front_loads(0)
                    spread_k(0)
                    load_residual(0)
                    front_loads(1)
                    place_max(0)
                    spread_k(1)
                    with sp.Fori(0, SEQS - 2) as j:
                        front_loads(j + 2)
                        place_max(j + 1)
                        stores(j)
                        load_residual(j + 1)
                        spread_k(j + 2)
                    place_max(SEQS - 1)
                    stores(SEQS - 2)
                    load_residual(SEQS - 1)
                    stores(SEQS - 1)
                    sp.wait_ge(stored, 32 * SEQS)

                @block.gpsimd
                def _(pool_):
                    e = nc.gpsimd
                    for tile in (pvT, x_res, wrk, bqk, brq, brk, latT, rv_mask, wrout, v_sb):
                        e.memset(tile[:], 0.0)
                    e.memset(ones[:, :], 1.0).then_inc(zeroed, 1)
                    pool_.wait_ge(zeroed, 1)
                    parts = [latT[LAT:LAT + 1, :]]
                    for hp in range(2):
                        parts.append(rv_mask[0:LAT, hp, 32 * hp:32 * hp + HD])
                        parts.append(rv_mask[LAT:P, hp, 32 * hp + HD:32 * hp + 2 * HD])
                    for n, part in enumerate(parts):
                        e.memset(part, 1.0).then_inc(zeroed, 1)
                        pool_.wait_ge(zeroed, n + 2)
                    e.memset(v_sb[:, :, :, HD:HD + 1], 1.0)
                    e.memset(ident[:, :], 0.0)
                    e.memset(mask_window[:, :], 0.0)
                    e.memset(mask_first[:, :], 0.0)
                    e.memset(lat_add[:, :, :], 0.0)
                    e.memset(rk_mask[:, :, :], 1.0).then_inc(consts, 1)
                    pool_.wait_ge(consts, 1)
                    e.affine_select(out=ident[:, :], in_=ident[:, :], compare_op=ALU.not_equal, fill=1.0, base=0,
                                    pattern=[[-1, P]], channel_multiplier=1)
                    e.affine_select(out=mask_window[:, 0:P], in_=mask_window[:, 0:P], compare_op=ALU.is_gt, fill=NEG,
                                    base=0, pattern=[[P + 1, P]], channel_multiplier=-P)
                    e.affine_select(out=mask_window[:, P:WIN], in_=mask_window[:, P:WIN], compare_op=ALU.is_gt, fill=NEG,
                                    base=0, pattern=[[-1, P]], channel_multiplier=1)
                    e.affine_select(out=mask_first[:, :], in_=mask_first[:, :], compare_op=ALU.is_ge, fill=NEG,
                                    base=0, pattern=[[-P - 1, P]], channel_multiplier=P)
                    e.affine_select(out=lat_add[:, :, :], in_=lat_add[:, :, :], compare_op=ALU.is_ge, fill=NEG,
                                    base=-LC, pattern=[[P, T], [-LC, LAT]], channel_multiplier=1)
                    e.affine_select(out=rk_mask[:, :, :], in_=rk_mask[:, :, :], compare_op=ALU.is_ge, fill=0.0,
                                    base=0, pattern=[[-HD, LH], [0, LAT]], channel_multiplier=1).then_inc(consts, 1)
                    pool_.wait_ge(consts, 2)
                    e.affine_select(out=rk_mask[:, :, :], in_=rk_mask[:, :, :], compare_op=ALU.is_ge, fill=0.0,
                                    base=HD - 1, pattern=[[HD, LH], [0, LAT]], channel_multiplier=-1).then_inc(consts, 1)

                    def wait_alone(s, value):
                        value = value if isinstance(value, int) else pool_.to_reg(value)
                        pool_.wait_ge(consts, 1)
                        pool_.wait_ge(s, value)

                    def select(i):
                        n = 0
                        for g in range(G):
                            for b in range(T):
                                for hp in range(2):
                                    wait_alone(*keyed.read(i, f"T{g}{b}{hp}"))
                                    own = prob[:, n % 4, :, 0:P]
                                    op = e.affine_select(out=own, in_=own, compare_op=ALU.is_gt, fill=0.0, base=0,
                                                         pattern=[[0, 2], [1, P]], channel_multiplier=-1)
                                    if b < T - 1:
                                        after = prob[:, n % 4, :, P:WIN]
                                        op = e.affine_select(out=after, in_=after, compare_op=ALU.is_gt, fill=0.0, base=0,
                                                             pattern=[[0, 2], [-P, P]], channel_multiplier=P + 1)
                                    op.then_inc(prob_ready, 1)
                                    n += 1

                    with pool_.Fori(0, SEQS) as j:
                        select(j)

                @block.scalar
                def _(act):
                    e = nc.scalar

                    def minus_max(i, g):
                        act.wait_ge(*front.filled(i, f"m{g}"))
                        act.wait_ge(max_placed[g], 16 * i)
                        e.activation(maxT[:, g, :], FB[front.bank(f"m{g}")][0:HG, :], ACT.Copy,
                                     scale=-1.0).then_inc(front.free(f"m{g}"), 1)

                    def turned_x(i):
                        for c in range(C):
                            act.wait_ge(*front.filled(i, f"xT{c}"))
                            e.activation(xT_h[:, c, :], FB[front.bank(f"xT{c}")][:, :], ACT.Identity).then_inc(xTh_ready, 1)

                    def exps(i, g, b):
                        w = WIN if b < T - 1 else P
                        for hp in range(2):
                            n = (g * T + b) * 2 + hp
                            name = f"T{g}{b}{hp}"
                            act.wait_ge(*keyed.filled(i, name))
                            act.wait_ge(prob_used, 2 * G * T * i + max(n - 3, 0))
                            src = KB[keyed.bank(name)][:, :].rearrange("p (h q) -> p h q", h=2)
                            e.activation(prob[:, n % 4, :, 0:w], src[:, :, 0:w], ACT.Exp,
                                         scale=SCALE).then_inc(keyed.free(name), 1)

                    def keep_pv(i, g):
                        act.wait_ge(prob_used, 2 * T * (G * i + g + 1))
                        if g == 0:
                            act.wait_ge(*scores.all_filled(i, "pv3"))
                        e.activation(pvT[:, g, :], PV[g % 2][:, :], ACT.Copy).then_inc(pv_read, 1)

                    def mid(i, nxt):
                        act.wait_ge(*front.filled(i, "rq"))
                        e.activation(rqT[:, :], FB[front.bank("rq")][:, :], ACT.Identity,
                                     bias=brq[:, 0:1]).then_inc(front.free("rq"), 1)
                        minus_max(i, 0)
                        for g in range(G):
                            for b in range(T):
                                exps(i, g, b)
                                if b == 0 and g >= 1:
                                    keep_pv(i, g - 1)
                                if g < G - 1 and b == 2:
                                    minus_max(i, g + 1)
                                if g == 0 and b == T - 1:
                                    act.wait_ge(lat_max, i + 1)
                                    e.activation(lat[:, :, :, :], lat[:, :, :, :], ACT.Exp, scale=SCALE).then_inc(lat_exp, 1)
                                if g == G - 1 and b == 0:
                                    for hp in range(2):
                                        act.wait_ge(*front.filled(i, f"lT{hp}"))
                                        e.activation(latpT[:, hp, :], FB[front.bank(f"lT{hp}")][:, :],
                                                     ACT.Copy).then_inc(front.free(f"lT{hp}"), 1)
                                if g == G - 1 and b == 2:
                                    act.wait_ge(*front.filled(i, "lo"))
                                    e.activation(latT[0:LAT, :], FB[front.bank("lo")][0:LAT, :],
                                                 ACT.Copy).then_inc(front.free("lo"), 1)
                        if nxt is not None:
                            turned_x(nxt)
                        keep_pv(i, G - 1)

                    def seam(prev, nxt):
                        for t in range(T + 1):
                            if nxt is not None and t < T:
                                g = t
                                act.wait_ge(*front.filled(nxt, f"k{g}"))
                                act.wait_ge(k_spread[(g + 2) % G], 16 * 2 * HG * (nxt if g < 2 else nxt + 1))
                                e.activation(kT_h[:, g % 2, :], FB[front.bank(f"k{g}")][:, :], ACT.Identity,
                                             bias=bqk[:, 1, g:g + 1]).then_inc(kh_ready, 1)
                                act.wait_ge(*front.filled(nxt, f"q{g}"))
                                e.activation(qT_h[:, g, :], FB[front.bank(f"q{g}")][:, :], ACT.Identity,
                                             bias=bqk[:, 0, g:g + 1]).then_inc(qh_ready, 1)
                            if prev is not None and t < T:
                                act.wait_ge(z_ready, T * prev + t + 1)
                                e.activation(gate_s[:, t % 2, 3, :], gate_s[:, t % 2, 2, :], ACT.Exp,
                                             scale=-1.0).then_inc(exp_written, 1)
                                act.wait_ge(exp_written, T * prev + t + 1)
                                e.activation(gate_s[:, t % 2, 4, :], gate_s[:, t % 2, 3, :], ACT.Copy, bias=1.0).then_inc(sig_exp, 1)
                            if prev is not None and t >= 1:
                                u = t - 1
                                act.wait_ge(*scores.filled(prev, f"mix{u}"))
                                if u < 2:
                                    act.wait_ge(*outs.all_filled(prev, f"out{u + 2}"))
                                else:
                                    act.wait_ge(*outs.filled(prev, f"out{u - 2}"))
                                e.activation(mixT_h[:, u % 2, :, :].rearrange("p c n -> p (c n)"),
                                             SB[scores.bank(f"mix{u}")][:, 0:D], ACT.Copy).then_inc(mixTh_ready, 1)

                    act.wait_ge(split, 1)
                    turned_x(0)
                    seam(None, 0)
                    mid(0, 1)
                    seam(0, 1)
                    with act.Fori(0, SEQS - 2) as j:
                        mid(j + 1, j + 2)
                        seam(j + 1, j + 2)
                    mid(SEQS - 1, None)
                    seam(SEQS - 1, None)

                @block.vector
                def _(dve):
                    e = nc.vector
                    setup = Steps(step_setup, SETUP_STEPS)
                    norm1, latent, gates = Steps(step_front, NORM_STEPS), Steps(step_mid, LATENT_STEPS), Steps(step_tail, TAIL_STEPS)
                    last = Steps(step_residual, RESIDUAL_STEPS)

                    def wait_alone(s, value):
                        value = value if isinstance(value, int) else dve.to_reg(value)
                        dve.wait_ge(consts, 1)
                        dve.wait_ge(s, value)

                    def link(steps, op, alone=False):
                        s, value = steps.next()
                        op.then_inc(s, 1)
                        (wait_alone if alone else dve.wait_ge)(s, value)

                    def rsqrt(steps, k):
                        y, v, w = rstd[:, k, 0, :], rstd[:, k, 1, :], rstd[:, k, 2, :]
                        link(steps, e.tensor_scalar(v, mv[:, k, :, 1], EPS, None, ALU.add))
                        link(steps, e.tensor_scalar(w.bitcast(i32), v.bitcast(i32), 1, None, ALU.logical_shift_right))
                        link(steps, e.tensor_scalar(y.bitcast(i32), w.bitcast(i32), -1, RSQRT_SEED, ALU.mult, ALU.add))
                        for _ in range(3):
                            link(steps, e.tensor_tensor(w, y, y, ALU.mult))
                            link(steps, e.scalar_tensor_tensor(w, w, -0.5, v, ALU.mult, ALU.mult))
                            link(steps, e.scalar_tensor_tensor(y, w, 1.5, y, ALU.add, ALU.mult))

                    for tile in (kD_h, kD_l):
                        e.memset(tile[:].bitcast(f32), 0.0).then_inc(keys_zeroed, 1)
                    setup.begin(0)
                    dve.wait_ge(weights_in, 16 * len(loads))
                    dve.wait_ge(consts, 3)
                    for c in range(C):
                        link(setup, e.tensor_tensor(wtmp.rearrange("p (h d) -> p h d", d=HD),
                                                    wv_f[:, c, 0:D].rearrange("p (h d) -> p h d", d=HD),
                                                    gl[:, :].unsqueeze(1).to_broadcast([P, HEADS, HD]), ALU.mult))
                        link(setup, e.tensor_reduce(wv_f[:, c, D:DA], wtmp.rearrange("p (h d) -> p h d", d=HD), AX.X, ALU.add))
                    for tile, vec in ((bv, gl), (wrout, gr)):
                        link(setup, e.tensor_tensor(wtmp.rearrange("p (h d) -> p h d", d=HD),
                                                    tile[:, 0:D].rearrange("p (h d) -> p h d", d=HD),
                                                    vec[:, :].unsqueeze(1).to_broadcast([P, HEADS, HD]), ALU.mult))
                        link(setup, e.tensor_reduce(tile[:, D:DA], wtmp.rearrange("p (h d) -> p h d", d=HD), AX.X, ALU.add))
                    for full, hi, lo in ((wqk_f, wqk_h, wqk_l), (wv_f, wv_h, wv_l), (wrq_f, wrq_h, wrq_l), (wout_f, wout_h, wout_l)):
                        link(setup, e.tensor_copy(hi[:], full))
                        op = e.tensor_tensor(lo[:], full, hi[:].bitcast(f32), ALU.subtract)
                    op.then_inc(split, 1)
                    setup.end()

                    def normalize(i):
                        norm_stats(i)
                        norm_scale(i)
                        norm_apply(i)

                    def norm_stats(i):
                        norm1.begin(i)
                        dve.wait_ge(x_loaded, 16 * (i + 1))
                        for t in range(T):
                            op = e.bn_stats(stats[:, 0, t, :], x_in[:, t, :])
                        link(norm1, op, alone=True)

                    def norm_scale(i):
                        for t in range(T):
                            op = e.bn_aggr(mv[:, 0, t, :], stats[:, 0, t, :])
                        link(norm1, op)
                        rsqrt(norm1, 0)

                    def norm_apply(i):
                        if not isinstance(i, int) or i > 0:
                            dve.wait_ge(*front.filled(i - 1, "xT1"))
                        for t in range(T):
                            op = e.tensor_scalar(xn[:, t, :], x_in[:, t, :], mv[:, 0, t, 0:1], rstd[:, 0, 0, t:t + 1],
                                                 ALU.subtract, ALU.mult)
                        op.then_inc(xn_ready, 1)
                        norm1.end()

                    def maxima(i, g):
                        for b in range(T):
                            maxima_of(i, g, b)

                    def maxima_of(i, g, b):
                        for hp in range(2):
                            name = f"M{g}{b}{hp}"
                            wait_alone(*scores.filled(i, name))
                            for hh in range(2):
                                src = SB[scores.bank(name)][:, hh * WIN:(hh + 1) * WIN]
                                h = 2 * hp + hh
                                if b == 0:
                                    src, mask = src[:, P:WIN], mask_first[:, :]
                                else:
                                    mask = mask_window[:, :]
                                op = e.tensor_tensor_reduce(out=src, in0=src, in1=mask, scale=1.0, scalar=3 * NEG,
                                                            op0=ALU.add, op1=ALU.max, accum_out=row_max[:, g, b, h:h + 1])
                            op.then_inc(scores.free(name), 1)

                    def latents_a(i):
                        latent.begin(i)
                        for n in range(2):
                            dve.wait_ge(*front.filled(i, f"ls{n}"))
                            op = e.tensor_tensor(lat[:, 2 * n:2 * n + 2, :, :],
                                                 FB[front.bank(f"ls{n}")][:, :].rearrange("p (t h l) -> p t h l", t=2, h=LH),
                                                 lat_add[:, 2 * n:2 * n + 2, :].unsqueeze(2).to_broadcast([P, 2, LH, LAT]), ALU.add)
                            op.then_inc(front.free(f"ls{n}"), 1)
                            dve.wait_ge(*front.read(i, f"ls{n}"))
                        flat = lat[:, :, :, :].rearrange("p t h l -> p (t h) l")
                        m = lat_s[:, 0, :, :].rearrange("p t h -> p (t h)")
                        link(latent, e.tensor_reduce(m, flat, AX.X, ALU.max))
                        link(latent, e.tensor_scalar(m, m, NEG / 2, None, ALU.max))
                        e.tensor_tensor(flat, flat, m.unsqueeze(2).to_broadcast([P, T * LH, LAT]), ALU.subtract).then_inc(lat_max, 1)

                    def latents_b(i):
                        dve.wait_ge(lat_exp, i + 1)
                        flat = lat[:, :, :, :].rearrange("p t h l -> p (t h) l")
                        s, r = (lat_s[:, k, :, :].rearrange("p t h -> p (t h)") for k in (1, 2))
                        link(latent, e.tensor_reduce(s, flat, AX.X, ALU.add))
                        link(latent, e.tensor_scalar(s, s, TINY, None, ALU.max))
                        link(latent, e.reciprocal(r, s))
                        e.tensor_tensor(flat, flat, r.unsqueeze(2).to_broadcast([P, T * LH, LAT]), ALU.mult).then_inc(lat_ready, 1)
                        latent.end()

                    def mid(i, prev, nxt):
                        maxima(i, 0)
                        latent_keys(i)
                        maxima_of(i, 1, 0)
                        latents_a(i)
                        maxima_of(i, 1, 1)
                        maxima_of(i, 1, 2)
                        maxima_of(i, 1, 3)
                        if prev is not None:
                            residual_scale(prev)
                        maxima_of(i, 2, 0)
                        maxima_of(i, 2, 1)
                        if prev is not None:
                            residual_apply(prev)
                        maxima_of(i, 2, 2)
                        maxima_of(i, 2, 3)
                        if nxt is not None:
                            norm_stats(nxt)
                        maxima_of(i, 3, 0)
                        if prev is not None:
                            residual_add(prev)
                        maxima_of(i, 3, 1)
                        maxima_of(i, 3, 2)
                        if prev is not None:
                            residual_stats(prev)
                        maxima_of(i, 3, 3)
                        latents_b(i)
                        if nxt is not None:
                            norm_scale(nxt)
                        if nxt is not None:
                            norm_apply(nxt)
                        if prev is not None:
                            residual_norm(prev)
                        if nxt is not None:
                            xT_low(nxt)

                    def xT_low(i):
                        for c in range(C):
                            src = FB[front.bank(f"xT{c}")]
                            dve.wait_ge(xTh_ready, C * i + c + 1)
                            e.tensor_reduce(pool[:, c, :], src[:, :].rearrange("p (l k) -> p l k", k=LC), AX.X, ALU.add)
                            e.tensor_tensor(xT_l[:, c, :], src[:, :], xT_h[:, c, :].bitcast(f32), ALU.subtract
                                            ).then_inc(front.free(f"xT{c}"), 1)
                            dve.wait_ge(*front.read(i, f"xT{c}"))
                        op = e.tensor_scalar(pool2[:, :, :, :], pool[:, :, :].unsqueeze(2).to_broadcast([P, C, 2, LAT]),
                                             1.0 / LC, None, ALU.mult)
                        op.then_inc(pool_ready, 1)

                    def kq_low(i, g):
                        for name, ready, j, hi, lo in (("k", kh_ready, 1, kT_h[:, g % 2, :], kT_l[:, g % 2, :]),
                                                       ("q", qh_ready, 0, qT_h[:, g, :], qT_l[:, g, :])):
                            dve.wait_ge(ready, G * i + g + 1)
                            e.scalar_tensor_tensor(lo, FB[front.bank(f"{name}{g}")][:, :], bqk[:, j, g:g + 1],
                                                   hi.bitcast(f32), ALU.add, ALU.subtract
                                                   ).then_inc(front.free(f"{name}{g}"), 1)

                    def values(i, t):
                        src = FB[front.bank(f"v{t}")]
                        dve.wait_ge(*front.filled(i, f"v{t}"))
                        e.tensor_tensor(v_sb[:, t, :, 0:HD], src[:, 0:D].rearrange("p (h d) -> p h d", d=HD),
                                        bv[:, 0:D].rearrange("p (h d) -> p h d", d=HD), ALU.add)
                        e.tensor_tensor(v_sb[:, t, :, HD + 1], src[:, D:DA], bv[:, D:DA], ALU.add).then_inc(front.free(f"v{t}"), 1)

                    def latent_keys(i):
                        dve.wait_ge(*front.filled(i, "rk"))
                        e.tensor_scalar(rk_t[:, :], FB[front.bank("rk")][:, 0:LAT], brk[:, 0:1], None, ALU.add).then_inc(front.free("rk"), 1)
                        dve.wait_ge(*front.read(i, "rk"))
                        e.tensor_tensor(rkD[:, :, :], rk_mask[:, :, :], rk_t[:, :].unsqueeze(1).to_broadcast([P, LH, LAT]), ALU.mult)
                        dve.wait_ge(*front.filled(i, "rv"))
                        e.tensor_tensor(rv_t[:, :], FB[front.bank("rv")][:, 0:LAT], brv[:, :], ALU.add).then_inc(front.free("rv"), 1)
                        dve.wait_ge(*front.read(i, "rv"))
                        e.tensor_tensor(rvD[:, :, :], rv_mask[:, :, :], rv_t[:, :].unsqueeze(1).to_broadcast([P, 2, LAT]),
                                        ALU.mult).then_inc(rv_ready, 1)

                    def gate_in(i, t):
                        u = t % 2
                        a = SB[scores.bank(f"pv{t}")][:, :].rearrange("p (n w) -> p n w", w=PAD)
                        r = KB[keyed.bank(f"rem{t}")]
                        loc = mixed[:, u, :].rearrange("p (n d) -> p n d", d=HD)
                        dve.wait_ge(*scores.filled(i, f"pv{t}"))
                        link(gates, e.tensor_scalar(gate_s[:, u, 0, :], a[:, :, HD], TINY, None, ALU.max))
                        link(gates, e.reciprocal(gate_s[:, u, 1, :], gate_s[:, u, 0, :]))
                        link(gates, e.tensor_tensor(gate_s[:, u, 0, :], a[:, :, HD + 1], gate_s[:, u, 1, :], ALU.mult))
                        dve.wait_ge(*keyed.filled(i, f"rem{t}"))
                        e.tensor_tensor(gate_s[:, u, 2, :], r[:, D:DA], gate_s[:, u, 0, :], ALU.add).then_inc(z_ready, 1)
                        if t >= 2:
                            dve.wait_ge(*scores.filled(i, f"mix{t - 2}"))
                        e.tensor_tensor(loc, a[:, :, 0:HD], gate_s[:, u, 1, :].unsqueeze(2).to_broadcast([P, HEADS, HD]),
                                        ALU.mult).then_inc(scores.free(f"pv{t}"), 1)
                        dve.wait_ge(*scores.read(i, f"pv{t}"))
                        link(gates, e.tensor_tensor(mixed[:, u, :], mixed[:, u, :], r[:, 0:D], ALU.subtract))

                    def gate_out(i, t):
                        u = t % 2
                        loc = mixed[:, u, :].rearrange("p (n d) -> p n d", d=HD)
                        dve.wait_ge(sig_exp, T * i + t + 1)
                        link(gates, e.reciprocal(gate_s[:, u, 5, :], gate_s[:, u, 4, :]))
                        link(gates, e.tensor_tensor(loc, loc, gate_s[:, u, 5, :].unsqueeze(2).to_broadcast([P, HEADS, HD]), ALU.mult))
                        e.tensor_tensor(mixed[:, u, :], mixed[:, u, :], KB[keyed.bank(f"rem{t}")][:, 0:D],
                                        ALU.add).then_inc(keyed.free(f"rem{t}"), 1)

                    def mix_low(i, t):
                        dve.wait_ge(mixTh_ready, T * i + t + 1)
                        e.tensor_tensor(mixT_l[:, t % 2, :, :].rearrange("p c n -> p (c n)"), SB[scores.bank(f"mix{t}")][:, 0:D],
                                        mixT_h[:, t % 2, :, :].rearrange("p c n -> p (c n)").bitcast(f32),
                                        ALU.subtract).then_inc(scores.free(f"mix{t}"), 1)

                    def add_bias(i, t):
                        dve.wait_ge(*outs.filled(i, f"out{t}"))
                        if t == 0:
                            dve.wait_ge(stored, 32 * i)
                        e.tensor_tensor(att[:, t, :], PV[outs.bank(f"out{t}")][:, 0:D], bout[:, :], ALU.add
                                        ).then_inc(outs.free(f"out{t}"), 1)
                        dve.wait_ge(*outs.read(i, f"out{t}"))
                        op = e.bn_stats(stats[:, 1, t, :], att[:, t, :])
                        if t == T - 1:
                            link(gates, op, alone=True)

                    def residual_scale(i):
                        last.begin(i)
                        for t in range(T):
                            op = e.bn_aggr(mv[:, 1, t, :], stats[:, 1, t, :])
                        link(last, op)
                        rsqrt(last, 1)

                    def residual_apply(i):
                        for t in range(T):
                            op = e.tensor_scalar(att[:, t, :], att[:, t, :], mv[:, 1, t, 0:1], rstd[:, 1, 0, t:t + 1],
                                                 ALU.subtract, ALU.mult)
                        link(last, op)

                    def residual_add(i):
                        dve.wait_ge(xres_loaded, 16 * (i + 1))
                        for t in range(T):
                            op = e.tensor_tensor(x_res[:, t, :], x_res[:, t, :], att[:, t, :], ALU.add)
                        op.then_inc(x1_ready, 1)
                        dve.wait_ge(x1_ready, i + 1)

                    def residual_stats(i):
                        for t in range(T):
                            op = e.bn_stats(stats[:, 2, t, :], x_res[:, t, :])
                        link(last, op, alone=True)

                    def residual_norm(i):
                        for t in range(T):
                            op = e.bn_aggr(mv[:, 2, t, :], stats[:, 2, t, :])
                        link(last, op)
                        rsqrt(last, 2)
                        for t in range(T):
                            op = e.tensor_scalar(att[:, t, :], x_res[:, t, :], mv[:, 2, t, 0:1], rstd[:, 2, 0, t:t + 1],
                                                 ALU.subtract, ALU.mult)
                        op.then_inc(xn2_ready, 1)
                        last.end()

                    def seam(prev, nxt):
                        if prev is not None:
                            gates.begin(prev)
                        for t in range(T + 3):
                            if nxt is not None and 1 <= t <= T:
                                kq_low(nxt, t - 1)
                            if prev is not None and 2 <= t <= T + 1:
                                mix_low(prev, t - 2)
                            if prev is not None:
                                if t < T:
                                    gate_in(prev, t)
                                if 1 <= t <= T:
                                    gate_out(prev, t - 1)
                                if t >= 3:
                                    add_bias(prev, t - 3)
                            if nxt is not None and T <= t < T + 2:
                                values(nxt, 2 * (t - T))
                                values(nxt, 2 * (t - T) + 1)
                        if prev is not None:
                            gates.end()

                    normalize(0)
                    xT_low(0)
                    seam(None, 0)
                    mid(0, None, 1)
                    seam(0, 1)
                    with dve.Fori(0, SEQS - 2) as j:
                        mid(j + 1, j, j + 2)
                        seam(j + 1, j + 2)
                    mid(SEQS - 1, SEQS - 2, None)
                    seam(SEQS - 1, None)
                    residual_scale(SEQS - 1)
                    residual_apply(SEQS - 1)
                    residual_add(SEQS - 1)
                    residual_stats(SEQS - 1)
                    residual_norm(SEQS - 1)

                @block.tensor
                def _(pe):
                    e = nc.tensor

                    def exact(out_, lh, ll, rh, rl, first, last):
                        e.matmul(out_, lh, rh, start=first, stop=False)
                        e.matmul(out_, lh, rl, start=False, stop=False)
                        return e.matmul(out_, ll, rh, start=False, stop=last)

                    def window(i, g, b):
                        lo, w = (P, P) if b == 0 else (0, WIN)
                        for hp in range(2):
                            name = f"M{g}{b}{hp}"
                            pe.wait_ge(*scores.drained(i, name))
                            dst = SB[scores.bank(name)][:, :].rearrange("p (h q) -> p h q", h=2)[:, :, lo:WIN]
                            k0 = max(b - 1, 0) * P
                            e.matmul(dst, qT_h[:, g, b * P:(b + 1) * P], kD_h[:, g, 2 * hp:2 * hp + 2, k0:k0 + w],
                                     start=True, stop=True).then_inc(scores.full(name), 1)

                    def windows(i, g):
                        pe.wait_ge(k_spread[g], 16 * 2 * HG * (i + 1))
                        for b in range(T):
                            window(i, g, b)

                    def turn_max(i, g):
                        name = f"m{g}"
                        for bank in range(2):
                            pe.wait_ge(*scores.read(i, f"M{g}{T - 1}{bank}"))
                        pe.wait_ge(*front.drained(i, name))
                        for b in range(T):
                            op = e.matmul(FB[front.bank(name)][0:HG, b * P:(b + 1) * P], row_max[:, g, b, :], ident[:, :],
                                          start=True, stop=True, is_transpose=True)
                        op.then_inc(front.full(name), 1)

                    def keyed_scores(i, g, b):
                        w = WIN if b < T - 1 else P
                        for hp in range(2):
                            name = f"T{g}{b}{hp}"
                            pe.wait_ge(*keyed.drained(i, name))
                            for hh in range(2):
                                h = 2 * hp + hh
                                k, q = slice(b * P, (b + 1) * P), slice(b * P, b * P + w)
                                op = exact(KB[keyed.bank(name)][:, hh * WIN:hh * WIN + w],
                                           kD_h[:, g, h, k], kD_l[:, g, h, k], qT_h[:, g, q], qT_l[:, g, q], True, True)
                            op.then_inc(keyed.full(name), 1)

                    def weigh_values(i, n):
                        g, b, hp = n // (2 * T), n // 2 % T, n % 2
                        w = WIN if b < T - 1 else P
                        pe.wait_ge(prob_ready, 2 * G * T * i + n + 1)
                        if b == 0 and hp == 0:
                            pe.wait_ge(pv_read, G * i + max(g - 1, 0))
                            if g < 2:
                                pe.wait_ge(*outs.drained(i, f"out{g}"))
                        for hh in range(2):
                            h = 2 * hp + hh
                            op = e.matmul(PV[g % 2][h * PAD:(h + 1) * PAD, b * P:b * P + w], v_sb[:, b, g * HG + h, :],
                                          prob[:, n % 4, hh, 0:w], start=(b == 0), stop=(b == T - 1),
                                          skip_group_check=True)
                        op.then_inc(prob_used, 1)

                    def turn_x(i):
                        pe.wait_ge(xn_ready, i + 1)
                        for c in range(C):
                            name = f"xT{c}"
                            pe.wait_ge(*front.drained(i, name))
                            for t in range(T):
                                op = e.matmul(FB[front.bank(name)][:, t * P:(t + 1) * P], xn[:, t, c * P:(c + 1) * P], ident[:, :],
                                              start=True, stop=True, is_transpose=True)
                            op.then_inc(front.full(name), 1)

                    def mid(i, nxt):
                        windows(i, 0)
                        pe.wait_ge(*front.drained(i, "rq"))
                        for c in range(C):
                            op = exact(FB[front.bank("rq")][:, :], wrq_h[:, c, :], wrq_l[:, c, :],
                                       xT_h[:, c, :], xT_l[:, c, :], c == 0, c == C - 1)
                        op.then_inc(front.full("rq"), 1)
                        pe.wait_ge(pool_ready, i + 1)
                        pe.wait_ge(*front.drained(i, "rk"))
                        for c in range(C):
                            op = e.matmul(FB[front.bank("rk")][:, 0:LAT], wrk[:, c, :], pool2[:, c, 0, :],
                                          start=(c == 0), stop=(c == C - 1))
                        op.then_inc(front.full("rk"), 1)
                        pe.wait_ge(*front.drained(i, "rv"))
                        for c in range(C):
                            op = e.matmul(FB[front.bank("rv")][:, 0:LAT], pool2[:, c, :, :].rearrange("p a l -> p (a l)"), wrv[:, c, :],
                                          start=(c == 0), stop=(c == C - 1))
                        op.then_inc(front.full("rv"), 1)
                        turn_max(i, 0)
                        pe.wait_ge(k_spread[1], 16 * 2 * HG * (i + 1))
                        for n in range(T, AHEAD):
                            window(i, n // T, n % T)
                        for name in ("v3", "rq"):
                            pe.wait_ge(*front.read(i, name))
                        pe.wait_ge(rv_ready, i + 1)
                        for n in range(2):
                            name = f"ls{n}"
                            pe.wait_ge(*front.drained(i, name))
                            for t in (2 * n, 2 * n + 1):
                                op = e.matmul(FB[front.bank(name)][:, (t % 2) * WIN:(t % 2 + 1) * WIN], rqT[:, t * P:(t + 1) * P],
                                              rkD[:, :, :].rearrange("p h l -> p (h l)"), start=True, stop=True)
                            op.then_inc(front.full(name), 1)
                        n = 0
                        for g in range(G):
                            pe.wait_ge(max_placed[g], 16 * (i + 1))
                            for b in range(T):
                                ahead = g * T + b + AHEAD
                                if ahead < G * T:
                                    if ahead % T == 0:
                                        pe.wait_ge(k_spread[ahead // T], 16 * 2 * HG * (i + 1))
                                    window(i, ahead // T, ahead % T)
                                keyed_scores(i, g, b)
                                if g == G - 1 and b == T - 1 and nxt is not None:
                                    turn_x(nxt)
                                for _ in range(2):
                                    if n >= 2:
                                        weigh_values(i, n - 2)
                                    n += 1
                                if g == G - 1 and b == 0:
                                    pe.wait_ge(lat_ready, i + 1)
                                    for hp in range(2):
                                        name = f"lT{hp}"
                                        pe.wait_ge(*front.drained(i, name))
                                        for t in range(T):
                                            op = e.matmul(FB[front.bank(name)][:, t * P:(t + 1) * P],
                                                          lat[:, t, 2 * hp:2 * hp + 2, :].rearrange("p h l -> p (h l)"), ident[:, :],
                                                          start=True, stop=True, is_transpose=True)
                                        op.then_inc(front.full(name), 1)
                                if g == G - 1 and b == 2:
                                    pe.wait_ge(*front.drained(i, "lo"))
                                    for hp in range(2):
                                        pe.wait_ge(*front.read(i, f"lT{hp}"))
                                        op = e.matmul(FB[front.bank("lo")][0:LAT, :], rvD[:, hp, :], latpT[:, hp, :],
                                                      start=(hp == 0), stop=(hp == 1))
                                    op.then_inc(front.full("lo"), 1)
                                if g < G - 1 and b == 2:
                                    turn_max(i, g + 1)
                        weigh_values(i, n - 2)
                        weigh_values(i, n - 1)

                    def seam(prev, nxt):
                        for t in range(T + 2):
                            if prev is not None and t < T:
                                name = f"pv{t}"
                                pe.wait_ge(pv_read, G * (prev + 1))
                                pe.wait_ge(*scores.drained(prev, name))
                                for g in range(G):
                                    op = e.matmul(SB[scores.bank(name)][:, g * P:(g + 1) * P], pvT[:, g, t * P:(t + 1) * P],
                                                  ident[:, :], start=True, stop=True, is_transpose=True)
                                op.then_inc(scores.full(name), 1)
                                name = f"rem{t}"
                                pe.wait_ge(*front.read(prev, "lo"))
                                pe.wait_ge(*keyed.drained(prev, name))
                                e.matmul(KB[keyed.bank(name)][:, 0:DA], latT[:, t * P:(t + 1) * P], wrout[:, :],
                                         start=True, stop=True).then_inc(keyed.full(name), 1)
                            if nxt is not None and t < T:
                                for j, kind in ((1, "k"), (0, "q")):
                                    name = f"{kind}{t}"
                                    if name == "k0":
                                        for c in range(C):
                                            pe.wait_ge(*front.read(nxt, f"xT{c}"))
                                    pe.wait_ge(*front.drained(nxt, name))
                                    w = slice(t * P, (t + 1) * P)
                                    for c in range(C):
                                        op = exact(FB[front.bank(name)][:, :], wqk_h[:, j, c, w], wqk_l[:, j, c, w],
                                                   xT_h[:, c, :], xT_l[:, c, :], c == 0, c == C - 1)
                                    op.then_inc(front.full(name), 1)
                            if nxt is not None and t >= T:
                                for n in (2 * (t - T), 2 * (t - T) + 1):
                                    name = f"v{n}"
                                    pe.wait_ge(*front.drained(nxt, name))
                                    for c in range(C):
                                        op = exact(FB[front.bank(name)][:, 0:DA], xT_h[:, c, n * P:(n + 1) * P],
                                                   xT_l[:, c, n * P:(n + 1) * P], wv_h[:, c, :], wv_l[:, c, :], c == 0, c == C - 1)
                                    op.then_inc(front.full(name), 1)
                            if prev is not None and 1 <= t <= T:
                                u, name = t - 1, f"mix{t - 1}"
                                pe.wait_ge(*keyed.read(prev, f"rem{u}"))
                                pe.wait_ge(*scores.drained(prev, name))
                                for c in range(C):
                                    op = e.matmul(SB[scores.bank(name)][:, c * P:(c + 1) * P], mixed[:, u % 2, c * P:(c + 1) * P],
                                                  ident[:, :], start=True, stop=True, is_transpose=True)
                                op.then_inc(scores.full(name), 1)
                            if prev is not None and t >= 2:
                                u, name = t - 2, f"out{t - 2}"
                                pe.wait_ge(*scores.read(prev, f"mix{u}"))
                                pe.wait_ge(*outs.drained(prev, name))
                                for c in range(C):
                                    op = exact(PV[outs.bank(name)][:, 0:D], mixT_h[:, u % 2, c, :], mixT_l[:, u % 2, c, :],
                                               wout_h[:, c, :], wout_l[:, c, :], c == 0, c == C - 1)
                                op.then_inc(outs.full(name), 1)

                    pe.wait_ge(split, 1)
                    turn_x(0)
                    seam(None, 0)
                    mid(0, 1)
                    seam(0, 1)
                    with pe.Fori(0, SEQS - 2) as j:
                        mid(j + 1, j + 2)
                        seam(j + 1, j + 2)
                    mid(SEQS - 1, None)
                    seam(SEQS - 1, None)

        ffn = ExitStack()
        with ffn:
            def sb(name, shape, dt=f32):
                return ffn.enter_context(nc.sbuf_tensor(name, shape, dt))

            TILES = SEQS * T
            REGION = SEQS * S + P
            BLOCKS = 2 * TILES + E - 1
            FCS = -(-FS // P)
            FCE = -(-F // P)
            fs = [min(P, FS - n * P) for n in range(FCS)]
            fe = [min(P, F - n * P) for n in range(FCE)]
            TOP_SCALE, TOP_EPS = 2.5, 1e-20

            xg_dram = nc.dram_tensor("xg_scratch", (E * REGION + P, D), f32, kind="Internal").ap()
            yg_dram = nc.dram_tensor("yg_scratch", ((BLOCKS + 1) * P, D), f32, kind="Internal").ap()
            ys_dram = nc.dram_tensor("ys_scratch", (SEQS, S, D), f32, kind="Internal").ap()

            wgu_h = sb("wgu_h", [P, E * C, 2, F], f32r)
            wgu_l = sb("wgu_l", [P, E * C, 2, F], f32r)
            pos_all = sb("pos_all", [P, TILES, 2], i32)
            lg_all = sb("lg_all", [P, TILES, E])
            oh_all = sb("oh_all", [P, 2, TILES, E])
            member = sb("member", [P, E])
            counts = sb("counts", [P, E])
            raw = sb("raw", [P, FCE * E * D])
            table = sb("table", [1, 2, BLOCKS + 1], i32)
            shift = sb("shift", [P, E])

            ffn_zeroed, ffn_consts = sem("ffn_zeroed"), sem("ffn_consts")
            down_in = sem("down_in")
            shared_in, shared_high, shared_split = sem("shared_in"), sem("shared_high"), sem("shared_split")
            chunk_high = sem("chunk_high")
            piece_in = [sem(f"piece_in{n}") for n in range(2 * C + FCS)]
            stage_in, stage_split = [sem("stage_in0"), sem("stage_in1")], sem("stage_split")
            counted, table_ready, spare_ready = sem("counted"), sem("table_ready"), sem("spare_ready")
            spare_zeroed, router_zeroed = sem("spare_zeroed"), sem("router_zeroed")
            row_loaded = [sem("row_loaded0"), sem("row_loaded1")]
            scattered = [sem("scattered0"), sem("scattered1")]
            xh2_ready = sem("xh2_ready")
            pos_ready, member_ready = sem("pos_ready"), sem("member_ready")
            h_ready, hh_ready, hl_ready = sem("h_ready"), sem("hh_ready"), sem("hl_ready")
            router_split, h_used, ys_stored = sem("router_split"), sem("h_used"), sem("ys_stored")
            step_route, step_end = sem("step_route"), sem("step_end")

            small = Banks([["xT0", "lgT", "rk"], ["xT1", "lg"]], [sem("small_full0"), sem("small_full1")],
                          [sem("small_free0"), sem("small_free1")])
            SM = [psum[6], psum[7]]
            gates2 = Banks([[f"g{n}" for n in range(0, FCS, 2)], [f"g{n}" for n in range(1, FCS, 2)]],
                           [sem("gate_full0"), sem("gate_full1")], [sem("gate_free0"), sem("gate_free1")])
            ys = Banks([["y0"], ["y1"]], [h_used, h_used], [sem("ys_free0"), sem("ys_free1")])
            YB = [psum[4], psum[5]]

            shared = ExitStack()
            with shared:
                def sb(name, shape, dt=f32):
                    return shared.enter_context(nc.sbuf_tensor(name, shape, dt))

                ws_h = sb("ws_h", [P, C, 2, FS], f32r)
                ws_l = sb("ws_l", [P, C, 2, FS], f32r)
                wsd_h = sb("wsd_h", [P, FCS, D], f32r)
                wsd_l = sb("wsd_l", [P, FCS, D], f32r)
                ws_f = raw[:, 0:C * 2 * FS].rearrange("p (c k f) -> p c k f", c=C, k=2)
                wd_f = raw[:, :].rearrange("p (n x d) -> p n x d", n=FCE, x=E)
                wsd_f = raw[:, C * 2 * FS:C * 2 * FS + FCS * D].rearrange("p (n d) -> p n d", d=D)
                moving = sb("moving", [P, 4 * S + 4 * F])
                silu = moving[:, 0:2 * S].rearrange("p (u s) -> p u s", u=2)
                h_f = moving[:, 2 * S:4 * S].rearrange("p (u s) -> p u s", u=2)
                stage = moving[:, 4 * S:4 * S + 4 * F].rearrange("p (u f) -> p u f", u=2)
                wr_f = sb("wr_f", [P, C, P])
                wr_h = sb("wr_h", [P, C, P], f32r)
                wr_l = sb("wr_l", [P, C, P], f32r)
                before = sb("before", [P, P])
                all_ones = sb("all_ones", [P, P])
                base = sb("base", [P, E])
                base_p = sb("base_p", [P, E + 1])
                falling = sb("falling", [P, E])
                zeros = sb("zeros", [P, D])
                spare = sb("spare", [P, E + 1], i32)
                spare_f = sb("spare_f", [P, E + 1])
                rows = sb("rows", [P, 2, T, D])
                rT_h = sb("rT_h", [P, C, S], f32r)
                rT_l = sb("rT_l", [P, C, S], f32r)
                lgT = sb("lgT", [P, S])
                h_h = sb("h_h", [P, 2, S], f32r)
                h_l = sb("h_l", [P, 2, S], f32r)
                y_sb = sb("y_sb", [P, T, D])
                rt = sb("rt", [P, 8, T, E])
                rt1 = sb("rt1", [P, 6, T])
                pos = sb("pos", [P, 2, T, 2], i32)
                pos_f = sb("pos_f", [P, T, 2])
                grid_i = sb("grid_i", [1, BLOCKS + 1 + E], i32)
                numbers = sb("numbers", [1, BLOCKS + 1 + E])
                line = sb("line", [1, 3, BLOCKS + 1])
                cum = sb("cum", [P, 5, E])
                cum_i = sb("cum_i", [P, E], i32)
                iota_i = sb("iota_i", [P, 2, E + 1], i32)

                shared_pieces = []
                for c in range(C):
                    for j, w in ((0, sw_gate), (1, sw_up)):
                        shared_pieces.append((w[c * P:(c + 1) * P, :], ws_f[:, c, j, :], ws_h[:, c, j, :], ws_l[:, c, j, :]))
                for n in range(FCS):
                    shared_pieces.append((sw_down[n * P:n * P + fs[n], :], wsd_f[0:fs[n], n, :],
                                          wsd_h[0:fs[n], n, :], wsd_l[0:fs[n], n, :]))
                SHARED = len(shared_pieces)
                assert E * C == SEQS

                with nc.Block() as block:

                    @block.sync
                    def _(sp):
                        sp.wait_ge(stored, 32 * SEQS)
                        sp.wait_ge(router_zeroed, 1)
                        with nc.allow_non_contiguous_dma(reason="the router's 2048 weights, once"):
                            for c in range(C):
                                sp.dma_start(wr_f[:, c, 0:E], gate_w[:, c * P:(c + 1) * P].rearrange("e p -> p e")).then_inc(shared_in, 16)

                        def load(j, u):
                            sp.wait_ge(scattered[u], 16 * 2 * T * j)
                            sp.dma_start(rows[:, u, :, :], xn2_dram[bass.ds(2 * j + u, 1)].rearrange("a (t p) d -> p (a t) d", p=P)
                                         ).then_inc(row_loaded[u], 16)

                        def store(i):
                            for name in ("y0", "y1"):
                                sp.wait_ge(*ys.read(i, name))
                            sp.dma_start(ys_dram[bass.ds(i, 1)].rearrange("a (t p) d -> p (a t) d", p=P), y_sb[:, :, :]).then_inc(ys_stored, 16)

                        def expert_chunk(i, u):
                            if not isinstance(i, int) or i >= 2:
                                sp.wait_ge(stage_split, i - 1)
                            for k, w in ((0, w_gate), (1, w_up)):
                                rows_of = w.rearrange("e (c p) f -> (e c) p f", p=P)
                                sp.dma_start(stage[:, u, k * F:(k + 1) * F], rows_of[bass.ds(i, 1)].rearrange("a p f -> p (a f)")
                                             ).then_inc(stage_in[u], 16)

                        load(0, 0)
                        for n, (src, full, _, _) in enumerate(shared_pieces):
                            sp.dma_start(full, src).then_inc(piece_in[n], 16)
                        load(0, 1)
                        for u in range(2):
                            expert_chunk(u, u)
                        sp.wait_ge(shared_split, SHARED)
                        for n in range(FCE):
                            sp.dma_start(wd_f[0:fe[n], n, :, :], w_down[:, n * P:n * P + fe[n], :].rearrange("e p d -> p e d")
                                         ).then_inc(down_in, 16)
                        with sp.Fori(0, SEQS // 2 - 1) as j:
                            for u in range(2):
                                store(2 * j + u)
                                load(j + 1, u)
                                expert_chunk(2 * j + u + 2, u)
                        for u in range(2):
                            store(SEQS - 2 + u)

                    @block.gpsimd
                    def _(gp):
                        e = nc.gpsimd
                        gp.wait_ge(stored, 32 * SEQS)
                        e.memset(wr_f[:, :, :], 0.0).then_inc(router_zeroed, 1)
                        e.memset(zeros[:, :], 0.0)
                        e.memset(member[:, :], 0.0)
                        e.memset(all_ones[:, :], 1.0)
                        e.memset(before[:, :], 1.0).then_inc(ffn_zeroed, 1)
                        gp.wait_ge(ffn_zeroed, 1)
                        e.affine_select(out=before[:, :], in_=before[:, :], compare_op=ALU.is_gt, fill=0.0, base=0,
                                        pattern=[[1, P]], channel_multiplier=-1)
                        e.iota(iota_i[:, 0, :], pattern=[[REGION, E + 1]], base=0, channel_multiplier=1)
                        e.iota(iota_i[:, 1, 0:E], pattern=[[-1, E]], base=E, channel_multiplier=0)
                        e.iota(grid_i[:, 0:BLOCKS + 1], pattern=[[1, BLOCKS + 1]], base=0, channel_multiplier=0)
                        e.iota(grid_i[:, BLOCKS + 1:], pattern=[[1, E]], base=0, channel_multiplier=0).then_inc(ffn_consts, 1)

                        def scatter(i, u):
                            value = gp.to_reg(i + 1)
                            gp.wait_ge(ffn_consts, 1)
                            gp.wait_ge(pos_ready, value)
                            for t in range(T):
                                for k in range(2):
                                    e.indirect_dma_start(out=xg_dram, out_offset=bass.IndirectOffsetOnAxis(ap=pos[:, u, t, k:k + 1], axis=0),
                                                         in_=rows[:, u, t, :], in_offset=None).then_inc(scattered[u], 16)

                        def split_chunk(j, u):
                            i = 2 * j + u
                            full = stage[:, u, :]
                            hi, lo = (w[:, bass.ds(i, 1), :, :].rearrange("p a k f -> p (a k f)") for w in (wgu_h, wgu_l))
                            gp.wait_ge(stage_in[u], 32 * (j + 1))
                            e.tensor_copy(hi, full).then_inc(chunk_high, 1)
                            gp.wait_ge(chunk_high, i + 1)
                            e.tensor_tensor(lo, full, hi.bitcast(f32), ALU.subtract).then_inc(stage_split, 1)

                        with gp.Fori(0, SEQS // 2) as j:
                            for u in range(2):
                                split_chunk(j, u)
                                scatter(2 * j + u, u)
                        gp.wait_ge(spare_ready, 1)
                        for u in range(2):
                            gp.wait_ge(scattered[u], 16 * T * SEQS)
                        for x_ in range(E + 1):
                            e.indirect_dma_start(out=xg_dram, out_offset=bass.IndirectOffsetOnAxis(ap=spare[:, x_:x_ + 1], axis=0),
                                                 in_=zeros[:, :], in_offset=None).then_inc(spare_zeroed, 16)
                        gp.wait_ge(spare_zeroed, 16 * (E + 1))

                    @block.scalar
                    def _(act):
                        e = nc.scalar
                        act.wait_ge(stored, 32 * SEQS)

                        def hidden_high(i, n):
                            p = fs[n]
                            act.wait_ge(h_ready, FCS * i + n + 1)
                            act.wait_ge(h_used, FCS * i + max(n - 1, 0))
                            e.activation(h_h[0:p, n % 2, :], h_f[0:p, n % 2, :], ACT.Copy).then_inc(hh_ready, 1)

                        def rows_high(i):
                            for c in range(C):
                                name = f"xT{c}"
                                act.wait_ge(*small.filled(i, name))
                                e.activation(rT_h[:, c, :], SM[small.bank(name)][:, :], ACT.Copy).then_inc(xh2_ready, 1)

                        def logits_copy(i):
                            act.wait_ge(*small.filled(i, "lgT"))
                            if not isinstance(i, int) or i > 0:
                                act.wait_ge(*small.filled(i - 1, "lg"))
                            e.activation(lgT[:, :], SM[small.bank("lgT")][:, :], ACT.Copy).then_inc(small.free("lgT"), 1)

                        def sequence(i, more):
                            for n in range(FCS):
                                name, p = f"g{n}", fs[n]
                                act.wait_ge(*gates2.filled(i, name))
                                act.wait_ge(h_ready, FCS * i + max(n - 1, 0))
                                e.activation(silu[0:p, n % 2, :], psum[n % 2][0:p, :], ACT.Silu
                                             ).then_inc(gates2.free(name), 1)
                                if n >= 1:
                                    hidden_high(i, n - 1)
                            hidden_high(i, FCS - 1)
                            if more:
                                rows_high(i + 1)
                            act.wait_ge(ys_stored, 16 * i)
                            for n in range(2):
                                name = f"y{n}"
                                act.wait_ge(h_used, FCS * (i + 1))
                                e.activation(y_sb[:, 2 * n:2 * n + 2, :].rearrange("p t d -> p (t d)"), YB[n][:, :],
                                             ACT.Copy).then_inc(ys.free(name), 1)
                            if more:
                                logits_copy(i + 1)

                        for n, (_, full, hi, _) in enumerate(shared_pieces):
                            act.wait_ge(piece_in[n], 16)
                            e.activation(hi, full, ACT.Copy).then_inc(shared_high, 1)
                        rows_high(0)
                        logits_copy(0)
                        with act.Fori(0, SEQS - 1) as i:
                            sequence(i, True)
                        sequence(SEQS - 1, False)

                    @block.vector
                    def _(dve):
                        e = nc.vector
                        route, ending = Steps(step_route, ROUTE_STEPS), Steps(step_end, END_STEPS)

                        def wait_alone(s, value):
                            value = value if isinstance(value, int) else dve.to_reg(value)
                            dve.wait_ge(ffn_consts, 1)
                            dve.wait_ge(s, value)

                        def link(steps, op, alone=False):
                            s, value = steps.next()
                            op.then_inc(s, 1)
                            (wait_alone if alone else dve.wait_ge)(s, value)

                        def over_e(ap):
                            return ap.unsqueeze(2).to_broadcast([P, T, E])

                        def over_t(ap):
                            return ap.unsqueeze(1).to_broadcast([P, T, E])

                        dve.wait_ge(stored, 32 * SEQS)
                        ending.begin(0)
                        dve.wait_ge(ffn_consts, 1)
                        e.tensor_copy(base_p[:, :], iota_i[:, 0, :])
                        e.tensor_copy(falling[:, :], iota_i[:, 1, 0:E])
                        link(ending, e.tensor_copy(numbers[:, :], grid_i[:, :]))
                        for x_ in range(E):
                            op = e.memset(base[:, x_:x_ + 1], float(x_ * REGION))
                        link(ending, op)
                        dve.wait_ge(shared_in, 16 * C)
                        link(ending, e.tensor_copy(wr_h[:, :, :], wr_f[:, :, :]))
                        e.tensor_tensor(wr_l[:, :, :], wr_f[:, :, :], wr_h[:, :, :].bitcast(f32), ALU.subtract).then_inc(router_split, 1)

                        m1, k1, m2, k2 = (rt1[:, k, :] for k in range(4))
                        L, eq, key, oh1, rest, oh2, both, cpre = (rt[:, k, :, :] for k in range(8))

                        def largest(scores_, m, k, oh):
                            link(route, e.tensor_reduce(m, scores_, AX.X, ALU.max))
                            link(route, e.tensor_tensor(eq, scores_, over_e(m), ALU.is_equal))
                            link(route, e.tensor_tensor(key, eq, over_t(falling[:, :]), ALU.mult))
                            link(route, e.tensor_reduce(k, key, AX.X, ALU.max))
                            link(route, e.tensor_tensor(oh, key, over_e(k), ALU.is_equal))

                        def choose_first(i):
                            route.begin(i)
                            dve.wait_ge(*small.filled(i, "lg"))
                            e.tensor_copy(L, SM[small.bank("lg")][:, :].rearrange("p (t x) -> p t x", t=T)[:, :, 0:E]).then_inc(small.free("lg"), 1)
                            dve.wait_ge(*small.read(i, "lg"))
                            largest(L, m1, k1, oh1)
                            link(route, e.scalar_tensor_tensor(rest, oh1, NEG, L, ALU.mult, ALU.add))

                        def choose_second(i):
                            largest(rest, m2, k2, oh2)
                            e.tensor_tensor(lg_all[:, bass.ds(T * i, T), :], L, over_e(m1), ALU.subtract)
                            e.tensor_copy(oh_all[:, 0, bass.ds(T * i, T), :], oh1)
                            e.tensor_copy(oh_all[:, 1, bass.ds(T * i, T), :], oh2)
                            link(route, e.tensor_tensor(both, oh1, oh2, ALU.add))
                            link(route, e.tensor_copy(cpre[:, 0, :], member[:, :]))
                            for t in range(1, T):
                                link(route, e.tensor_tensor(cpre[:, t, :], cpre[:, t - 1, :], both[:, t - 1, :], ALU.add))
                            e.tensor_tensor(member[:, :], cpre[:, T - 1, :], both[:, T - 1, :], ALU.add).then_inc(member_ready, 1)

                        def place(i, j, u):
                            dve.wait_ge(*small.filled(i, "rk"))
                            e.tensor_tensor(eq, SM[small.bank("rk")][:, 0:T * E].rearrange("p (t x) -> p t x", t=T),
                                            over_t(base[:, :]), ALU.add).then_inc(small.free("rk"), 1)
                            dve.wait_ge(*small.read(i, "rk"))
                            for k, oh in ((0, oh1), (1, oh2)):
                                link(route, e.tensor_tensor(key, oh, eq, ALU.mult))
                                link(route, e.tensor_reduce(pos_f[:, :, k], key, AX.X, ALU.add))
                            dve.wait_ge(scattered[u], 16 * 2 * T * j)
                            e.tensor_copy(pos_all[:, bass.ds(T * i, T), :], pos_f[:, :, :])
                            e.tensor_copy(pos[:, u, :, :], pos_f[:, :, :]).then_inc(pos_ready, 1)
                            route.end()

                        def hidden(i, n):
                            p = fs[n]
                            dve.wait_ge(*gates2.read(i, f"g{n}"))
                            dve.wait_ge(hh_ready, FCS * i + max(n - 1, 0))
                            e.tensor_tensor(h_f[0:p, n % 2, :], silu[0:p, n % 2, :], psum[2 + n % 2][0:p, :], ALU.mult).then_inc(h_ready, 1)
                            dve.wait_ge(hh_ready, FCS * i + n + 1)
                            e.tensor_tensor(h_l[0:p, n % 2, :], h_f[0:p, n % 2, :], h_h[0:p, n % 2, :].bitcast(f32),
                                            ALU.subtract).then_inc(hl_ready, 1)

                        def rows_low(i):
                            for c in range(C):
                                name = f"xT{c}"
                                dve.wait_ge(xh2_ready, C * i + c + 1)
                                e.tensor_tensor(rT_l[:, c, :], SM[small.bank(name)][:, :], rT_h[:, c, :].bitcast(f32),
                                                ALU.subtract).then_inc(small.free(name), 1)

                        def sequence(i, j, u, more):
                            hidden(i, 0)
                            choose_first(i)
                            hidden(i, 1)
                            choose_second(i)
                            hidden(i, 2)
                            hidden(i, 3)
                            place(i, j, u)
                            for n in range(4, FCS):
                                hidden(i, n)
                            if more:
                                rows_low(i + 1)

                        for n, (_, full, hi, lo) in enumerate(shared_pieces):
                            dve.wait_ge(shared_high, n + 1)
                            e.tensor_tensor(lo, full, hi.bitcast(f32), ALU.subtract).then_inc(shared_split, 1)
                        rows_low(0)
                        with dve.Fori(0, SEQS // 2 - 1) as j:
                            for u in range(2):
                                sequence(2 * j + u, j, u, True)
                        for u in range(2):
                            sequence(SEQS - 2 + u, SEQS // 2 - 1, u, u == 0)

                        dve.wait_ge(counted, 1)
                        NB = BLOCKS + 1
                        link(ending, e.tensor_copy(counts[:, :], SM[0][:, 0:E]))
                        link(ending, e.tensor_tensor(base_p[:, 0:E], base_p[:, 0:E], counts[:, :], ALU.add))
                        e.tensor_copy(spare[:, :], base_p[:, :]).then_inc(spare_ready, 1)
                        nb, ca, cb, excl = (cum[:, k, :] for k in range(4))
                        link(ending, e.tensor_scalar(cum_i[:, :], counts[:, :], float(P - 1), None, ALU.add))
                        link(ending, e.tensor_scalar(cum_i[:, :], cum_i[:, :], P.bit_length() - 1, None, ALU.logical_shift_right))
                        link(ending, e.tensor_copy(nb, cum_i[:, :]))
                        src, dst = nb, ca
                        for d in (1, 2, 4):
                            link(ending, e.tensor_copy(dst[:, 0:d], src[:, 0:d]))
                            link(ending, e.tensor_tensor(dst[:, d:E], src[:, d:E], src[:, 0:E - d], ALU.add))
                            src, dst = dst, (cb if dst is ca else ca)
                        incl = src
                        link(ending, e.tensor_tensor(excl, incl, nb, ALU.subtract))
                        link(ending, e.scalar_tensor_tensor(excl, excl, -float(P), base[:, :], ALU.mult, ALU.add))
                        e.tensor_scalar(shift[:, :], excl, -1.0, None, ALU.mult)

                        def per_block(ap):
                            return ap[0:1, :].unsqueeze(1).to_broadcast([1, NB, E])

                        dve.wait_ge(stage_split, SEQS)
                        work, row = (moving[0:1, k * NB * E:(k + 1) * NB * E].rearrange("a (b x) -> a b x", x=E) for k in range(2))
                        blk = numbers[:, 0:NB].unsqueeze(2).to_broadcast([1, NB, E])
                        ex = per_block(numbers[:, NB:NB + E])
                        eb, ok, rb = (line[:, k, :] for k in range(3))
                        link(ending, e.tensor_tensor(work, blk, per_block(incl), ALU.is_ge))
                        link(ending, e.tensor_reduce(eb, work, AX.X, ALU.add))
                        link(ending, e.tensor_scalar(row, blk, float(P), None, ALU.mult))
                        link(ending, e.tensor_tensor(row, row, per_block(excl), ALU.add))
                        link(ending, e.tensor_tensor(work, ex, eb.unsqueeze(2).to_broadcast([1, NB, E]), ALU.is_equal))
                        link(ending, e.tensor_tensor(work, work, row, ALU.mult))
                        link(ending, e.tensor_reduce(rb, work, AX.X, ALU.add))
                        link(ending, e.tensor_scalar(ok, eb, float(E), None, ALU.is_ge))
                        link(ending, e.scalar_tensor_tensor(rb, ok, float(E * REGION), rb, ALU.mult, ALU.add))
                        link(ending, e.scalar_tensor_tensor(eb, ok, -float(E), eb, ALU.mult, ALU.add))
                        e.tensor_copy(table[:, 0, :], rb)
                        e.tensor_copy(table[:, 1, :], eb).then_inc(table_ready, 1)
                        ending.end()

                    @block.tensor
                    def _(pe):
                        e = nc.tensor

                        def exact(out_, lh, ll, rh, rl, first, last):
                            e.matmul(out_, lh, rh, start=first, stop=False, skip_group_check=True)
                            e.matmul(out_, lh, rl, start=False, stop=False, skip_group_check=True)
                            return e.matmul(out_, ll, rh, start=False, stop=last, skip_group_check=True)

                        def gate_up(i, n):
                            name, p = f"g{n}", fs[n]
                            w = slice(n * P, n * P + p)
                            pe.wait_ge(*gates2.drained(i, name))
                            pe.wait_ge(h_ready, FCS * i + max(n - 1, 0))
                            for k in range(2):
                                for c in range(C):
                                    op = exact(psum[2 * k + n % 2][0:p, :], ws_h[:, c, k, w], ws_l[:, c, k, w],
                                               rT_h[:, c, :], rT_l[:, c, :], c == 0, c == C - 1)
                            op.then_inc(gates2.full(name), 1)

                        def down(i, n):
                            p = fs[n]
                            pe.wait_ge(hl_ready, FCS * i + n + 1)
                            if n == 0:
                                for name in ("y0", "y1"):
                                    pe.wait_ge(*ys.drained(i, name))
                            for t in range(T):
                                half = slice((t % 2) * D, (t % 2 + 1) * D)
                                op = exact(YB[t // 2][:, half], h_h[0:p, n % 2, t * P:(t + 1) * P], h_l[0:p, n % 2, t * P:(t + 1) * P],
                                           wsd_h[0:p, n, :], wsd_l[0:p, n, :], n == 0 and t % 2 == 0, n == FCS - 1)
                            op.then_inc(h_used, 1)

                        pe.wait_ge(stored, 32 * SEQS)
                        pe.wait_ge(router_split, 1)
                        pe.wait_ge(shared_split, SHARED)

                        def turn_rows(i, j, u):
                            pe.wait_ge(row_loaded[u], 16 * (j + 1))
                            for c in range(C):
                                name = f"xT{c}"
                                pe.wait_ge(*small.drained(i, name))
                                for t in range(T):
                                    op = e.matmul(SM[small.bank(name)][:, t * P:(t + 1) * P], rows[:, u, t, c * P:(c + 1) * P], ident[:, :],
                                                  start=True, stop=True, is_transpose=True)
                                op.then_inc(small.full(name), 1)

                        def logits(i):
                            for c in range(C):
                                pe.wait_ge(*small.read(i, f"xT{c}"))
                            for c in range(C):
                                op = exact(SM[small.bank("lgT")][:, :], wr_h[:, c, :], wr_l[:, c, :], rT_h[:, c, :], rT_l[:, c, :],
                                           c == 0, c == C - 1)
                            op.then_inc(small.full("lgT"), 1)

                        def turn_logits(i):
                            pe.wait_ge(*small.read(i, "lgT"))
                            pe.wait_ge(*small.drained(i, "lg"))
                            for t in range(T):
                                op = e.matmul(SM[small.bank("lg")][:, t * P:(t + 1) * P], lgT[:, t * P:(t + 1) * P], ident[:, :],
                                              start=True, stop=True, is_transpose=True)
                            op.then_inc(small.full("lg"), 1)

                        def ranks(i):
                            pe.wait_ge(member_ready, i + 1)
                            pe.wait_ge(*small.drained(i, "rk"))
                            out_ = SM[small.bank("rk")][:, 0:T * E]
                            e.matmul(out_, before[:, :], rt[:, 6, :, :].rearrange("p t x -> p (t x)"), start=True, stop=False)
                            e.matmul(out_, all_ones[:, :], rt[:, 7, :, :].rearrange("p t x -> p (t x)"), start=False, stop=True
                                     ).then_inc(small.full("rk"), 1)

                        def sequence(i, j, u, more):
                            gate_up(i, 0)
                            turn_logits(i)
                            gate_up(i, 1)
                            for n in range(FCS):
                                if n + 2 < FCS:
                                    gate_up(i, n + 2)
                                if n == 2:
                                    ranks(i)
                                if n == FCS - 3 and more:
                                    turn_rows(i + 1, j + u, 1 - u)
                                down(i, n)
                            if more:
                                logits(i + 1)

                        turn_rows(0, 0, 0)
                        logits(0)
                        with pe.Fori(0, SEQS // 2 - 1) as j:
                            for u in range(2):
                                sequence(2 * j + u, j, u, True)
                        for u in range(2):
                            sequence(SEQS - 2 + u, SEQS // 2 - 1, u, u == 0)
                        pe.wait_ge(*small.read(SEQS - 1, "rk"))
                        e.matmul(SM[0][:, 0:E], all_ones[:, :], member[:, :], start=True, stop=True).then_inc(counted, 1)

            NBLK = BLOCKS + 1
            assert NBLK % 2 == 0
            down_high, down_low = sem("down_high"), sem("down_low")
            blk_loaded = [sem(f"blk_loaded{n}") for n in range(4)]
            blk_stored = [sem("blk_stored0"), sem("blk_stored1")]
            bx_full, bx_high, bx_low = sem("bx_full"), sem("bx_high"), sem("bx_low")
            bg_full, bg_silu, bh_ready = sem("bg_full"), sem("bg_silu"), sem("bh_ready")
            bt_full, bt_high, bt_low = sem("bt_full"), sem("bt_high"), sem("bt_low")
            by_full, by_read = sem("by_full"), sem("by_read")
            experts = ExitStack()
            with experts:
                def sb(name, shape, dt=f32):
                    return experts.enter_context(nc.sbuf_tensor(name, shape, dt))

                wd_h = sb("wd_h", [P, FCE, E, D], f32r)
                wd_l = sb("wd_l", [P, FCE, E, D], f32r)
                bx = sb("bx", [P, 4, D])
                bxT_h = sb("bxT_h", [P, 2, C, P], f32r)
                bxT_l = sb("bxT_l", [P, 2, C, P], f32r)
                b_silu = sb("b_silu", [P, 2, F])
                b_h = sb("b_h", [P, 2, F])
                bhT_h = sb("bhT_h", [P, 2, FCE, P], f32r)
                bhT_l = sb("bhT_l", [P, 2, FCE, P], f32r)
                b_y = sb("b_y", [P, 2, D])
                FULL = F // P
                REST = F - FULL * P

                def second_part_over(eng):
                    eng.wait_ge(ys_stored, 16 * SEQS)
                    eng.wait_ge(spare_zeroed, 16 * (E + 1))
                    eng.wait_ge(table_ready, 1)

                with nc.Block() as block:

                    @block.sync
                    def _(sp):
                        second_part_over(sp)

                        def load(b, n):
                            row = sp.value_load(table[0:1, 0, bass.ds(b, 1)], min_val=0, max_val=E * REGION)
                            sp.dma_start(bx[:, n, :], xg_dram[bass.ds(row, P), :]).then_inc(blk_loaded[n], 16)

                        def store(b, n):
                            sp.wait_ge(by_read, b + 1)
                            sp.dma_start(yg_dram[bass.ds(b * P, P), :], b_y[:, n, :]).then_inc(blk_stored[n], 16)

                        for b in range(2):
                            load(b, b)
                        for b in range(2, 4):
                            load(b, b)

                        def load_next(b, n):
                            sp.wait_ge(bx_full, b - 3)
                            load(b, n)

                        load_next(4, 0)
                        load_next(5, 1)
                        with sp.Fori(0, (NBLK - 8) // 4) as j:
                            for n in range(4):
                                load_next(4 * j + n + 6, (n + 2) % 4)
                                store(4 * j + n, n % 2)
                        for b in range(NBLK - 8, NBLK):
                            if b + 6 < NBLK:
                                load_next(b + 6, (b + 6) % 4)
                            store(b, b % 2)
                        for n in range(2):
                            sp.wait_ge(blk_stored[n], 16 * (NBLK // 2))

                    @block.scalar
                    def _(act):
                        e = nc.scalar
                        second_part_over(act)

                        def rows_high(b, u):
                            act.wait_ge(bx_full, b + 1)
                            e.activation(bxT_h[:, u, :, :].rearrange("p c n -> p (c n)"), psum[6 + u][:, 0:D], ACT.Copy).then_inc(bx_high, 1)

                        def gate(b, u):
                            act.wait_ge(bg_full, b + 1)
                            e.activation(b_silu[:, u, :], psum[u][:, 0:F], ACT.Silu).then_inc(bg_silu, 1)

                        def hidden_high(b, u):
                            act.wait_ge(bt_full, b + 1)
                            e.activation(bhT_h[:, u, 0:FULL, :].rearrange("p n k -> p (n k)"), psum[4][:, 0:FULL * P], ACT.Copy)
                            e.activation(bhT_h[0:REST, u, FULL, :], psum[4][0:REST, FULL * P:(FULL + 1) * P], ACT.Copy).then_inc(bt_high, 1)

                        def result(b, u, j):
                            act.wait_ge(by_full, b + 1)
                            act.wait_ge(blk_stored[u], 16 * j)
                            e.activation(b_y[:, u, :], psum[5][:, 0:D], ACT.Copy).then_inc(by_read, 1)

                        rows_high(0, 0)
                        act.wait_ge(down_in, 16 * FCE)
                        for n in range(FCE):
                            e.activation(wd_h[0:fe[n], n, :, :], wd_f[0:fe[n], n, :, :], ACT.Copy).then_inc(down_high, 1)

                        def step(b, u, j=None):
                            if not isinstance(b, int) or b < NBLK:
                                gate(b, u)
                            if not isinstance(b, int) or b + 1 < NBLK:
                                rows_high(b + 1, 1 - u)
                            if not isinstance(b, int) or 1 <= b <= NBLK:
                                hidden_high(b - 1, 1 - u)
                            if not isinstance(b, int) or b >= 2:
                                result(b - 2, u, b // 2 - 1 if isinstance(b, int) else j)

                        step(0, 0)
                        step(1, 1)
                        with act.Fori(0, NBLK // 2 - 2) as j:
                            for u in range(2):
                                step(2 * j + u + 2, u, j)
                        for b in range(NBLK - 2, NBLK + 2):
                            step(b, b % 2)

                    @block.vector
                    def _(dve):
                        e = nc.vector
                        second_part_over(dve)

                        def rows_low(b, u):
                            dve.wait_ge(bx_high, b + 1)
                            e.tensor_tensor(bxT_l[:, u, :, :].rearrange("p c n -> p (c n)"), psum[6 + u][:, 0:D],
                                            bxT_h[:, u, :, :].rearrange("p c n -> p (c n)").bitcast(f32), ALU.subtract).then_inc(bx_low, 1)

                        def hidden(b, u):
                            dve.wait_ge(bg_silu, b + 1)
                            e.tensor_tensor(b_h[:, u, :], b_silu[:, u, :], psum[2 + u][:, 0:F], ALU.mult).then_inc(bh_ready, 1)

                        def hidden_low(b, u):
                            dve.wait_ge(bt_high, b + 1)
                            e.tensor_tensor(bhT_l[:, u, 0:FULL, :].rearrange("p n k -> p (n k)"), psum[4][:, 0:FULL * P],
                                            bhT_h[:, u, 0:FULL, :].rearrange("p n k -> p (n k)").bitcast(f32), ALU.subtract)
                            e.tensor_tensor(bhT_l[0:REST, u, FULL, :], psum[4][0:REST, FULL * P:(FULL + 1) * P],
                                            bhT_h[0:REST, u, FULL, :].bitcast(f32), ALU.subtract).then_inc(bt_low, 1)

                        rows_low(0, 0)
                        for n in range(FCE):
                            dve.wait_ge(down_high, n + 1)
                            e.tensor_tensor(wd_l[0:fe[n], n, :, :], wd_f[0:fe[n], n, :, :], wd_h[0:fe[n], n, :, :].bitcast(f32),
                                            ALU.subtract).then_inc(down_low, 1)

                        def step(b, u):
                            if not isinstance(b, int) or b < NBLK:
                                hidden(b, u)
                            if not isinstance(b, int) or b + 1 < NBLK:
                                rows_low(b + 1, 1 - u)
                            if not isinstance(b, int) or 1 <= b <= NBLK:
                                hidden_low(b - 1, 1 - u)

                        step(0, 0)
                        step(1, 1)
                        with dve.Fori(0, NBLK // 2 - 2) as j:
                            for u in range(2):
                                step(2 * j + u + 2, u)
                        for b in range(NBLK - 2, NBLK + 1):
                            step(b, b % 2)

                    @block.tensor
                    def _(pe):
                        e = nc.tensor
                        second_part_over(pe)

                        def expert_of(b):
                            return pe.value_load(table[0:1, 1, bass.ds(b, 1)], min_val=0, max_val=E - 1)

                        def turn_rows(b, u, n, j):
                            pe.wait_ge(blk_loaded[n], 16 * (j + 1))
                            pe.wait_ge(bx_low, max(b - 1, 0) if isinstance(b, int) else b - 1)
                            for c in range(C):
                                op = e.matmul(psum[6 + u][:, c * P:(c + 1) * P], bx[:, n, c * P:(c + 1) * P], ident[:, :],
                                              start=True, stop=True, is_transpose=True)
                            op.then_inc(bx_full, 1)

                        def gate_up(b, u, x_):
                            pe.wait_ge(bx_low, b + 1)
                            pe.wait_ge(bh_ready, max(b - 1, 0) if isinstance(b, int) else b - 1)
                            for c in range(C):
                                for k in range(2):
                                    wh, wl = (w[:, bass.ds(x_ * C + c, 1), k, :].rearrange("p a f -> p (a f)") for w in (wgu_h, wgu_l))
                                    out_, xh, xl = psum[2 * k + u][:, 0:F], bxT_h[:, u, c, :], bxT_l[:, u, c, :]
                                    e.matmul(out_, xh, wh, start=(c == 0), stop=False)
                                    e.matmul(out_, xh, wl, start=False, stop=False)
                                    op = e.matmul(out_, xl, wh, start=False, stop=(c == C - 1))
                            op.then_inc(bg_full, 1)

                        def turn_hidden(b, u):
                            pe.wait_ge(bh_ready, b + 1)
                            pe.wait_ge(bt_low, b)
                            for n in range(FCE):
                                op = e.matmul(psum[4][0:fe[n], n * P:(n + 1) * P], b_h[:, u, n * P:n * P + fe[n]], ident[:, :],
                                              start=True, stop=True, is_transpose=True)
                            op.then_inc(bt_full, 1)

                        def down(b, u, x_):
                            pe.wait_ge(bt_low, b + 1)
                            pe.wait_ge(by_read, b)
                            for n in range(FCE):
                                wh, wl = (w[0:fe[n], n, bass.ds(x_, 1), :].rearrange("p a d -> p (a d)") for w in (wd_h, wd_l))
                                out_, hh, hl = psum[5][:, 0:D], bhT_h[0:fe[n], u, n, :], bhT_l[0:fe[n], u, n, :]
                                e.matmul(out_, hh, wh, start=(n == 0), stop=False)
                                e.matmul(out_, hh, wl, start=False, stop=False)
                                op = e.matmul(out_, hl, wh, start=False, stop=(n == FCE - 1))
                            op.then_inc(by_full, 1)

                        def step(b, u, m, j=None, chosen=None):
                            always = not isinstance(b, int)
                            if always:
                                if m not in chosen:
                                    chosen[m] = expert_of(b)
                                this = chosen[m]
                            else:
                                this = expert_of(b) if b < NBLK else None
                                earlier = expert_of(b - 2) if b >= 2 else None
                            if always or b < NBLK:
                                gate_up(b, u, this)
                            if always:
                                if m - 2 not in chosen:
                                    chosen[m - 2] = expert_of(b - 2)
                                elif m < 5:
                                    chosen[m + 1] = expert_of(b + 1)
                                earlier = chosen[m - 2]
                            if always or b + 1 < NBLK:
                                turn_rows(b + 1, 1 - u, (m + 1) % 4, (b + 1) // 4 if j is None else j + (m + 1) // 4)
                            if always or 1 <= b <= NBLK:
                                turn_hidden(b - 1, 1 - u)
                            if always or b >= 2:
                                down(b - 2, u, earlier)

                        turn_rows(0, 0, 0, 0)
                        step(0, 0, 0)
                        step(1, 1, 1)
                        pe.wait_ge(down_low, FCE)
                        with pe.Fori(0, NBLK // 4 - 1) as j:
                            chosen = {}
                            for m in range(2, 6):
                                step(4 * j + m, m % 2, m, j, chosen)
                        for b in range(NBLK - 2, NBLK + 2):
                            step(b, b % 2, b)

            R = 4
            assert SEQS % R == 0
            fin_loaded = [sem(f"fin_loaded{u}") for u in range(R)]
            gathered = [sem(f"gathered{u}") for u in range(R)]
            index_ready, exp_ready = sem("index_ready"), sem("exp_ready")
            shift_ready, x1_shifted = sem("shift_ready"), sem("x1_shifted")
            out_ready, out_stored, step_weight, step_last = (
                sem("out_ready"), [sem(f"out_stored{u}") for u in range(R)], sem("step_weight"), sem("step_last"))
            last = ExitStack()
            with last:
                def sb(name, shape, dt=f32):
                    return last.enter_context(nc.sbuf_tensor(name, shape, dt))

                f_x1 = sb("f_x1", [P, R, T, D])
                f_ys = sb("f_ys", [P, R, T, D])
                f_y = sb("f_y", [P, R, 2, T, D])
                f_out = sb("f_out", [P, R, T, D])
                index = sb("index", [P, R, T, 2], i32)
                index_all = sb("index_all", [P, TILES, 2], i32)
                moved = sb("moved", [P, TILES])
                weight = sb("weight", [P, 2, TILES])
                w_now = sb("w_now", [P, 2, 2 * T])
                probs = sb("probs", [P, TILES, E])
                picked = sb("picked", [P, TILES, E])
                z_sum = sb("z_sum", [P, 4, TILES])
                f_stats = sb("f_stats", [P, 2, T, 6])
                f_mv = sb("f_mv", [P, 2, T, 2])
                f_rstd = sb("f_rstd", [P, 3, 2, T])
                f_shift = sb("f_shift", [P, 2, T])

                def third_part_over(eng):
                    for n in range(2):
                        eng.wait_ge(blk_stored[n], 16 * (NBLK // 2))

                with nc.Block() as block:

                    @block.sync
                    def _(sp):
                        third_part_over(sp)

                        def load(j, u):
                            i = R * j + u
                            for src, dst in ((x1_dram, f_x1), (ys_dram, f_ys)):
                                sp.dma_start(dst[:, u, :, :], src[bass.ds(i, 1)].rearrange("a (t p) d -> p (a t) d", p=P)).then_inc(fin_loaded[u], 16)

                        def store(j, u):
                            i = R * j + u
                            sp.wait_ge(out_ready, i + 1)
                            sp.dma_start(out[bass.ds(i, 1)].rearrange("a (t p) d -> p (a t) d", p=P), f_out[:, u, :, :]).then_inc(out_stored[u], 16)

                        for u in range(R):
                            load(0, u)
                        with sp.Fori(0, SEQS // R - 1) as j:
                            for u in range(R):
                                store(j, u)
                                load(j + 1, u)
                        for u in range(R):
                            store(SEQS // R - 1, u)
                        for u in range(R):
                            sp.wait_ge(out_stored[u], 16 * (SEQS // R))

                    @block.gpsimd
                    def _(gp):
                        e = nc.gpsimd
                        third_part_over(gp)
                        with gp.Fori(0, SEQS // R) as j:
                            for u in range(R):
                                value = gp.to_reg(R * j + u + 1)
                                gp.wait_ge(blk_stored[0], 16)
                                gp.wait_ge(index_ready, value)
                                for t in range(T):
                                    for k in range(2):
                                        e.indirect_dma_start(out=f_y[:, u, k, t, :], out_offset=None, in_=yg_dram,
                                                             in_offset=bass.IndirectOffsetOnAxis(ap=index[:, u, t, k:k + 1], axis=0)
                                                             ).then_inc(gathered[u], 16)

                    @block.scalar
                    def _(act):
                        third_part_over(act)
                        e = nc.scalar
                        e.activation(probs[:, :, :], lg_all[:, :, :], ACT.Exp).then_inc(exp_ready, 1)
                        with act.Fori(0, SEQS // R) as j:
                            for u in range(R):
                                act.wait_ge(shift_ready, R // 2 * j + u // 2 + 1)
                                for t in range(T):
                                    op = e.activation(f_x1[:, u, t, :], f_x1[:, u, t, :], ACT.Identity, bias=f_shift[:, u % 2, t:t + 1])
                                op.then_inc(x1_shifted, 1)

                    @block.vector
                    def _(dve):
                        e = nc.vector
                        prepare, steps = Steps(step_weight, WEIGHT_STEPS), Steps(step_last, LAST_STEPS)

                        def wait_alone(s, value):
                            value = value if isinstance(value, int) else dve.to_reg(value)
                            dve.wait_ge(ys_stored, 16)
                            dve.wait_ge(s, value)

                        def link(steps, op, alone=False):
                            s, value = steps.next()
                            op.then_inc(s, 1)
                            (wait_alone if alone else dve.wait_ge)(s, value)

                        def more(j):
                            return not (isinstance(j, int) and j == SEQS // R - 1)

                        def indices(j, u):
                            e.tensor_copy(index[:, u, :, :], index_all[:, bass.ds(T * (R * j + u), T), :]).then_inc(index_ready, 1)

                        third_part_over(dve)
                        prepare.begin(0)
                        for k in range(2):
                            link(prepare, e.tensor_tensor(picked[:, :, :], oh_all[:, k, :, :],
                                                          shift[:, :].unsqueeze(1).to_broadcast([P, TILES, E]), ALU.mult))
                            link(prepare, e.tensor_reduce(moved[:, :], picked[:, :, :], AX.X, ALU.add))
                            link(prepare, e.tensor_tensor(index_all[:, :, k], pos_all[:, :, k], moved[:, :], ALU.add))
                        for u in range(R):
                            indices(0, u)
                        dve.wait_ge(exp_ready, 1)
                        z, p1, p2, s_ = (z_sum[:, k, :] for k in range(4))
                        link(prepare, e.tensor_reduce(z, probs[:, :, :], AX.X, ALU.add))
                        link(prepare, e.reciprocal(s_, z))
                        for k, p_ in ((0, p1), (1, p2)):
                            link(prepare, e.tensor_tensor(picked[:, :, :], probs[:, :, :], oh_all[:, k, :, :], ALU.mult))
                            link(prepare, e.tensor_reduce(p_, picked[:, :, :], AX.X, ALU.add))
                            link(prepare, e.tensor_tensor(p_, p_, s_, ALU.mult))
                        link(prepare, e.scalar_tensor_tensor(z, p1, TOP_EPS, p2, ALU.add, ALU.add))
                        link(prepare, e.reciprocal(s_, z))
                        for k, p_ in ((0, p1), (1, p2)):
                            link(prepare, e.scalar_tensor_tensor(weight[:, k, :], p_, TOP_SCALE, s_, ALU.mult, ALU.mult))
                        prepare.end()

                        def pair(j, first):
                            n = R // 2 * j + first // 2
                            steps.begin(n)
                            link(steps, e.tensor_copy(w_now[:, :, :], weight[:, :, bass.ds(2 * T * n, 2 * T)]))
                            for v_, u in ((0, first), (1, first + 1)):
                                dve.wait_ge(fin_loaded[u], 32 * (j + 1))
                                dve.wait_ge(gathered[u], 16 * 2 * T * (j + 1))
                                for k in range(2):
                                    for t in range(T):
                                        op = e.scalar_tensor_tensor(f_ys[:, u, t, :], f_y[:, u, k, t, :], w_now[:, k, v_ * T + t:v_ * T + t + 1],
                                                                    f_ys[:, u, t, :], ALU.mult, ALU.add)
                                    link(steps, op)
                                for t in range(T):
                                    op = e.bn_stats(f_stats[:, v_, t, :], f_ys[:, u, t, :])
                                if v_ == 0 and more(j):
                                    indices(j + 1, u)
                            link(steps, op, alone=True)
                            for u in range(2):
                                for t in range(T):
                                    op = e.bn_aggr(f_mv[:, u, t, :], f_stats[:, u, t, :])
                            link(steps, op)
                            if more(j):
                                indices(j + 1, first + 1)
                            y, v, w = (f_rstd[:, k, :, :] for k in range(3))
                            link(steps, e.tensor_scalar(v, f_mv[:, :, :, 1], EPS, None, ALU.add))
                            link(steps, e.tensor_scalar(w.bitcast(i32), v.bitcast(i32), 1, None, ALU.logical_shift_right))
                            link(steps, e.tensor_scalar(y.bitcast(i32), w.bitcast(i32), -1, RSQRT_SEED, ALU.mult, ALU.add))
                            for _ in range(3):
                                link(steps, e.tensor_tensor(w, y, y, ALU.mult))
                                link(steps, e.scalar_tensor_tensor(w, w, -0.5, v, ALU.mult, ALU.mult))
                                link(steps, e.scalar_tensor_tensor(y, w, 1.5, y, ALU.add, ALU.mult))
                            e.scalar_tensor_tensor(f_shift[:, :, :], f_mv[:, :, :, 0], -1.0, y, ALU.mult, ALU.mult).then_inc(shift_ready, 1)
                            for v_, u in ((0, first), (1, first + 1)):
                                dve.wait_ge(x1_shifted, R * j + u + 1)
                                dve.wait_ge(out_stored[u], 16 * j)
                                for t in range(T):
                                    op = e.scalar_tensor_tensor(f_out[:, u, t, :], f_ys[:, u, t, :], y[:, v_, t:t + 1], f_x1[:, u, t, :],
                                                                ALU.mult, ALU.add)
                                op.then_inc(out_ready, 1)
                            steps.end()

                        with dve.Fori(0, SEQS // R - 1) as j:
                            for first in range(0, R, 2):
                                pair(j, first)
                        for first in range(0, R, 2):
                            pair(SEQS // R - 1, first)


_INS = ["L0_attn_x", "L0_attn_qkv_w", "L0_attn_qkv_b", "L0_attn_rq_w", "L0_attn_rq_b", "L0_attn_rkv_w", "L0_attn_rkv_b",
        "L0_attn_rout_w", "L0_attn_rout_b", "L0_attn_out_w", "L0_attn_out_b", "L0_attn_gl_w", "L0_attn_gr_w",
        "L0_ffn_gate_w", "L0_ffn_w_gate", "L0_ffn_w_up", "L0_ffn_w_down", "L0_ffn_sw_gate", "L0_ffn_sw_up", "L0_ffn_sw_down"]
_OUTS = [((16, 512, 256), "float32")]


def kernel(**inputs):
    import numpy as _np
    import concourse.bacc as _bacc
    from concourse import mybir as _mybir
    from concourse.bass_utils import run_bass_kernel_spmd as _run

    nc = _bacc.Bacc("TRN2", target_bir_lowering=False, num_devices=1)
    arrays, args = {}, []
    for name in _INS:
        a = _np.ascontiguousarray(inputs[name])
        arrays[f"in_{name}_dram"] = a
        args.append(nc.dram_tensor(f"in_{name}_dram", a.shape, _mybir.dt.from_np(a.dtype), kind="ExternalInput").ap())
    for i, (shape, dtype) in enumerate(_OUTS):
        dt = _mybir.dt.from_np(_np.dtype(dtype))
        args.append(nc.dram_tensor(f"out_{i}_dram", shape, dt, kind="ExternalOutput").ap())
    sandwich_kernel(nc, *args)
    r = _run(nc, [arrays], core_ids=[0])
    return r.results[0]["out_0_dram"]
```
